# Optimizing a Trainium2 kernel written in Bass

```python
import numpy as np
import jax
import jax.numpy as jnp

def _softmax(x, axis=-1):
    return jax.nn.softmax(x, axis=axis)

def _gelu(x):
    return jax.nn.gelu(x, approximate=True)

def _silu(x):
    return jax.nn.silu(x)

def _sigmoid(x):
    return jax.nn.sigmoid(x)

def _layernorm(x, axis=-1, eps=1e-05):
    m = jnp.mean(x, axis=axis, keepdims=True)
    v = jnp.var(x, axis=axis, keepdims=True)
    return (x - m) / jnp.sqrt(v + eps)

def _scatter_add(tgt, idx, src, axis=0):
    return tgt.at[idx].add(src)

def _segment_sum(src, seg, n):
    return jax.ops.segment_sum(src, seg, n)
kernel_name = 'mk_audio_tower_d1_tok_audfeat2048_r4_d5baf7'

def setup_inputs(seed: int=0):
    np.random.seed(seed)
    _w = jnp.asarray

    def _rec_inputs():
        import jax
        import jax.numpy as jnp
        _rk = jax.random.key(seed)
        x = -5.77387e-05 + 0.999872 * jax.random.normal(jax.random.fold_in(_rk, 1), (8, 750, 320), jnp.float32)
        return x
    x = _rec_inputs()

    def _L0_tok_setup():
        import jax, jax.numpy as jnp
        import numpy as np
        B, S, ENC = (16, 375, 320)
        K = 2
        IN_DIM = ENC * K
        LLM = 512
        HID = 128
        E, TOPK = (8, 2)
        EPS = 1e-06

        def _ln(x, g, b):
            m = jnp.mean(x, -1, keepdims=True)
            v = jnp.mean((x - m) ** 2, -1, keepdims=True)
            return (x - m) * jax.lax.rsqrt(v + EPS) * g + b

        def _swiglu(x, w12, w3):
            h = x @ w12.T
            gate, val = jnp.split(h, 2, axis=-1)
            return jax.nn.silu(gate) * val @ w3.T
        key = jax.random.key(seed)
        ks = jax.random.split(key, 12)
        sc = 0.02
        return {'x': jax.random.normal(ks[0], (B, S, ENC), jnp.float32), 'ln_pre_g': 1.0 + sc * jax.random.normal(ks[1], (IN_DIM,), jnp.float32), 'ln_pre_b': sc * jax.random.normal(ks[2], (IN_DIM,), jnp.float32), 'router_w': sc * jax.random.normal(ks[3], (E, IN_DIM), jnp.float32), 'router_b': sc * jax.random.normal(ks[4], (E,), jnp.float32), 'shared_w12': sc * jax.random.normal(ks[5], (2 * HID, IN_DIM), jnp.float32), 'shared_w3': sc * jax.random.normal(ks[6], (LLM, HID), jnp.float32), 'experts_w12': sc * jax.random.normal(ks[7], (E, 2 * HID, IN_DIM), jnp.float32), 'experts_w3': sc * jax.random.normal(ks[8], (E, LLM, HID), jnp.float32), 'ln_post_g': 1.0 + sc * jax.random.normal(ks[9], (LLM,), jnp.float32), 'ln_post_b': sc * jax.random.normal(ks[10], (LLM,), jnp.float32)}
    _L0_tok_all = _L0_tok_setup()
    _L0_tok_in = {k: v for k, v in _L0_tok_all.items() if k in ('ln_pre_g', 'ln_pre_b', 'router_w', 'router_b', 'shared_w12', 'shared_w3', 'experts_w12', 'experts_w3', 'ln_post_g', 'ln_post_b')}
    del _L0_tok_all

    def _L0_attn_setup():
        import jax, jax.numpy as jnp
        import numpy as np
        H = 16
        KVH = 4
        D = 128
        HID = 512
        EPS = 1e-06
        GROUPS = H // KVH

        def elu_plus_one(x):
            return jax.nn.elu(x) + 1.0

        def _repeat_kv(x, b, s):
            x = x.reshape(b, s, KVH, 1, D)
            x = jnp.broadcast_to(x, (b, s, KVH, GROUPS, D))
            return x.reshape(b, s, H * D)

        def _split_heads(x, b, s, nh):
            return x.reshape(b, s, nh, D).transpose(0, 2, 1, 3)
        key = jax.random.key(seed)
        ks = jax.random.split(key, 8)
        s = 0.02
        return {'hidden_states': jax.random.normal(ks[0], (2, 1024, HID), jnp.float32), 'Wq': jax.random.normal(ks[1], (H * D, HID), jnp.float32) * s, 'bq': jnp.zeros((H * D,), jnp.float32), 'Wk': jax.random.normal(ks[2], (KVH * D, HID), jnp.float32) * s, 'bk': jnp.zeros((KVH * D,), jnp.float32), 'Wv': jax.random.normal(ks[3], (KVH * D, HID), jnp.float32) * s, 'bv': jnp.zeros((KVH * D,), jnp.float32), 'Wo': jax.random.normal(ks[4], (HID, H * D), jnp.float32) * s}
    _L0_attn_all = _L0_attn_setup()
    _L0_attn_in = {k: v for k, v in _L0_attn_all.items() if k in ('Wq', 'bq', 'Wk', 'bk', 'Wv', 'bv', 'Wo')}
    del _L0_attn_all

    def _L0_ffn_setup():
        import jax, jax.numpy as jnp
        import numpy as np
        B, L, D = (2, 256, 512)
        E, K = (8, 2)
        H, HS = (352, 704)
        key = jax.random.key(seed)
        ks = jax.random.split(key, 9)
        s = 0.02
        return {'x': jax.random.normal(ks[0], (B, L, D), dtype=jnp.float32), 'gate_w': jax.random.normal(ks[1], (E, D), dtype=jnp.float32) * s, 'w_gate': jax.random.normal(ks[2], (E, D, H), dtype=jnp.float32) * s, 'w_up': jax.random.normal(ks[3], (E, D, H), dtype=jnp.float32) * s, 'w_down': jax.random.normal(ks[4], (E, H, D), dtype=jnp.float32) * s, 'shgate_w': jax.random.normal(ks[5], (D,), dtype=jnp.float32) * s, 'shw_gate': jax.random.normal(ks[6], (D, HS), dtype=jnp.float32) * s, 'shw_up': jax.random.normal(ks[7], (D, HS), dtype=jnp.float32) * s, 'shw_down': jax.random.normal(ks[8], (HS, D), dtype=jnp.float32) * s}
    _L0_ffn_all = _L0_ffn_setup()
    _L0_ffn_in = {k: v for k, v in _L0_ffn_all.items() if k in ('gate_w', 'w_gate', 'w_up', 'w_down', 'shgate_w', 'shw_gate', 'shw_up', 'shw_down')}
    del _L0_ffn_all
    return {'x': x, 'L0_tok_ln_pre_g': _L0_tok_in['ln_pre_g'], 'L0_tok_ln_pre_b': _L0_tok_in['ln_pre_b'], 'L0_tok_router_w': _L0_tok_in['router_w'], 'L0_tok_router_b': _L0_tok_in['router_b'], 'L0_tok_shared_w12': _L0_tok_in['shared_w12'], 'L0_tok_shared_w3': _L0_tok_in['shared_w3'], 'L0_tok_experts_w12': _L0_tok_in['experts_w12'], 'L0_tok_experts_w3': _L0_tok_in['experts_w3'], 'L0_tok_ln_post_g': _L0_tok_in['ln_post_g'], 'L0_tok_ln_post_b': _L0_tok_in['ln_post_b'], 'L0_attn_Wq': _L0_attn_in['Wq'], 'L0_attn_bq': _L0_attn_in['bq'], 'L0_attn_Wk': _L0_attn_in['Wk'], 'L0_attn_bk': _L0_attn_in['bk'], 'L0_attn_Wv': _L0_attn_in['Wv'], 'L0_attn_bv': _L0_attn_in['bv'], 'L0_attn_Wo': _L0_attn_in['Wo'], 'L0_ffn_gate_w': _L0_ffn_in['gate_w'], 'L0_ffn_w_gate': _L0_ffn_in['w_gate'], 'L0_ffn_w_up': _L0_ffn_in['w_up'], 'L0_ffn_w_down': _L0_ffn_in['w_down'], 'L0_ffn_shgate_w': _L0_ffn_in['shgate_w'], 'L0_ffn_shw_gate': _L0_ffn_in['shw_gate'], 'L0_ffn_shw_up': _L0_ffn_in['shw_up'], 'L0_ffn_shw_down': _L0_ffn_in['shw_down']}

def reference(x, L0_tok_ln_pre_g, L0_tok_ln_pre_b, L0_tok_router_w, L0_tok_router_b, L0_tok_shared_w12, L0_tok_shared_w3, L0_tok_experts_w12, L0_tok_experts_w3, L0_tok_ln_post_g, L0_tok_ln_post_b, L0_attn_Wq, L0_attn_bq, L0_attn_Wk, L0_attn_bk, L0_attn_Wv, L0_attn_bv, L0_attn_Wo, L0_ffn_gate_w, L0_ffn_w_gate, L0_ffn_w_up, L0_ffn_w_down, L0_ffn_shgate_w, L0_ffn_shw_gate, L0_ffn_shw_up, L0_ffn_shw_down):
    import jax
    import jax.numpy as jnp

    def _L0_tok_ref(x, ln_pre_g, ln_pre_b, router_w, router_b, shared_w12, shared_w3, experts_w12, experts_w3, ln_post_g, ln_post_b):
        import jax, jax.numpy as jnp
        import numpy as np
        B, S, ENC = (16, 375, 320)
        K = 2
        IN_DIM = ENC * K
        LLM = 512
        HID = 128
        E, TOPK = (8, 2)
        EPS = 1e-06

        def _ln(x, g, b):
            m = jnp.mean(x, -1, keepdims=True)
            v = jnp.mean((x - m) ** 2, -1, keepdims=True)
            return (x - m) * jax.lax.rsqrt(v + EPS) * g + b

        def _swiglu(x, w12, w3):
            h = x @ w12.T
            gate, val = jnp.split(h, 2, axis=-1)
            return jax.nn.silu(gate) * val @ w3.T
        b, s, d = x.shape
        pad = -s % K
        if pad:
            x = jnp.pad(x, ((0, 0), (0, pad), (0, 0)))
        xk = x.reshape(b, -1, d * K)
        new_s = xk.shape[1]
        nx = _ln(xk.reshape(-1, d * K), ln_pre_g, ln_pre_b)
        shared = _swiglu(nx, shared_w12, shared_w3)
        logits = nx @ router_w.T + router_b
        probs = jax.nn.softmax(logits, -1)
        w, idx = jax.lax.top_k(probs, TOPK)
        w = w / (jnp.sum(w, -1, keepdims=True) + 1e-20)
        combine = jnp.sum(jax.nn.one_hot(idx, E, dtype=nx.dtype) * w[..., None], axis=1)
        hid = jnp.einsum('td,efd->tef', nx, experts_w12)
        gate, val = jnp.split(hid, 2, axis=-1)
        act = jax.nn.silu(gate) * val
        eo = jnp.einsum('teh,eoh->teo', act, experts_w3)
        routed = jnp.einsum('teo,te->to', eo, combine)
        out = _ln(shared + routed, ln_post_g, ln_post_b)
        return out.reshape(b, new_s, LLM)

    def _L0_attn_ref(hidden_states, Wq, bq, Wk, bk, Wv, bv, Wo):
        import jax, jax.numpy as jnp
        import numpy as np
        H = 16
        KVH = 4
        D = 128
        HID = 512
        EPS = 1e-06
        GROUPS = H // KVH

        def elu_plus_one(x):
            return jax.nn.elu(x) + 1.0

        def _repeat_kv(x, b, s):
            x = x.reshape(b, s, KVH, 1, D)
            x = jnp.broadcast_to(x, (b, s, KVH, GROUPS, D))
            return x.reshape(b, s, H * D)

        def _split_heads(x, b, s, nh):
            return x.reshape(b, s, nh, D).transpose(0, 2, 1, 3)
        b, s, _ = hidden_states.shape
        q = hidden_states @ Wq.T + bq
        k = hidden_states @ Wk.T + bk
        v = hidden_states @ Wv.T + bv
        k = _repeat_kv(k, b, s)
        v = _repeat_kv(v, b, s)
        q = _split_heads(q, b, s, H)
        k = _split_heads(k, b, s, H)
        v = _split_heads(v, b, s, H)
        sq = elu_plus_one(q)
        sk = elu_plus_one(k)
        kv = jnp.einsum('bhsd,bhse->bhde', sk, v)
        qkv = jnp.einsum('bhsd,bhde->bhse', sq, kv)
        k_sum = sk.sum(axis=2)
        norm = jnp.einsum('bhsd,bhd->bhs', sq, k_sum)
        attn = qkv / (norm[..., None] + EPS)
        attn = attn.transpose(0, 2, 1, 3).reshape(b, s, H * D)
        return attn @ Wo.T

    def _L0_ffn_ref(x, gate_w, w_gate, w_up, w_down, shgate_w, shw_gate, shw_up, shw_down):
        import jax, jax.numpy as jnp
        import numpy as np
        B, L, D = (2, 256, 512)
        E, K = (8, 2)
        H, HS = (352, 704)
        b, l, d = x.shape
        xf = x.reshape(-1, d)
        logits = jnp.einsum('td,ed->te', xf.astype(jnp.float32), gate_w)
        probs = jax.nn.softmax(logits.astype(jnp.float32), axis=-1)
        weights, indices = jax.lax.top_k(probs, K)
        weights = (weights / weights.sum(-1, keepdims=True)).astype(x.dtype)
        onehot = jax.nn.one_hot(indices, E, dtype=x.dtype)
        combine = jnp.einsum('tk,tke->te', weights, onehot)
        g = jnp.einsum('td,edh->teh', xf, w_gate)
        u = jnp.einsum('td,edh->teh', xf, w_up)
        h = jax.nn.silu(g) * u
        out = jnp.einsum('teh,ehd,te->td', h.astype(jnp.float32), w_down.astype(jnp.float32), combine.astype(jnp.float32))
        sgate = jax.nn.sigmoid(xf @ shgate_w)[:, None]
        sh = jax.nn.silu(xf @ shw_gate) * (xf @ shw_up) @ shw_down
        out = out + (sgate * sh).astype(jnp.float32)
        return out.astype(x.dtype).reshape(b, l, d)
    h = _L0_tok_ref(x, L0_tok_ln_pre_g, L0_tok_ln_pre_b, L0_tok_router_w, L0_tok_router_b, L0_tok_shared_w12, L0_tok_shared_w3, L0_tok_experts_w12, L0_tok_experts_w3, L0_tok_ln_post_g, L0_tok_ln_post_b)
    h = h + _L0_attn_ref(_layernorm(h, axis=-1), L0_attn_Wq, L0_attn_bq, L0_attn_Wk, L0_attn_bk, L0_attn_Wv, L0_attn_bv, L0_attn_Wo)
    h = h + _L0_ffn_ref(_layernorm(h, axis=-1), L0_ffn_gate_w, L0_ffn_w_gate, L0_ffn_w_up, L0_ffn_w_down, L0_ffn_shgate_w, L0_ffn_shw_gate, L0_ffn_shw_up, L0_ffn_shw_down)
    return h

_drawn_inputs = setup_inputs


def setup_inputs(seed=0):
    import zlib

    import numpy as np

    out = dict(_drawn_inputs(seed))
    spreads = {'L0_attn_bq': (0.0, 2.0), 'L0_attn_bk': (0.0, 2.0), 'L0_attn_bv': (0.0, 0.267)}
    factors = {'L0_tok_ln_post_g': 8.14,
     'L0_attn_Wq': 64.0,
     'L0_attn_Wk': 64.0,
     'L0_ffn_shgate_w': 55.752,
     'L0_tok_ln_post_b': 7.646,
     'L0_attn_Wv': 6.167,
     'L0_ffn_gate_w': 6.348,
     'L0_ffn_w_gate': 5.594,
     'L0_ffn_w_up': 5.466,
     'L0_ffn_w_down': 5.463,
     'L0_ffn_shw_gate': 4.355,
     'L0_ffn_shw_up': 4.27,
     'L0_ffn_shw_down': 4.27}
    for name, (base, spread) in spreads.items():
        noise = np.random.default_rng([zlib.crc32(name.encode()), seed]).standard_normal(out[name].shape)
        drawn = base * np.exp(spread * noise) if base else spread * noise
        out[name] = jnp.asarray(drawn.astype(out[name].dtype))
    for name, factor in factors.items():
        out[name] = (out[name] * factor).astype(out[name].dtype)
    return out
```

```python
from contextlib import ExitStack

import concourse.bass as bass
from concourse import mybir

ALU = mybir.AluOpType
ACT = mybir.ActivationFunctionType
AX = mybir.AxisListType
F32 = mybir.dt.float32
F32R = mybir.dt.float32r

T = 3000
TP = 125
NT = T // TP
D = 512
P = 128
ST = 4
SN = ST * TP
GROUPS = 2
GS = 3
GT = GS * ST
B = 8
BT = 3
E = 8
NH, NKV, HD = 16, 4, 128
BN = 376


class Link:

    def __init__(self, eng, sem):
        self.eng, self.sem, self.n, self.base = eng, sem, 0, 0

    def __call__(self, ins):
        self.n += 1
        ins.then_inc(self.sem, 1)
        self.eng.wait_ge(self.sem, self.base + self.n)

    def start(self, base):
        self.base, self.n = base, 0


def three(eng, out, w_hi, w_lo, x_hi, x_lo, first, last):
    eng.matmul(out, w_hi, x_hi, start=first, stop=False)
    eng.matmul(out, w_hi, x_lo, start=False, stop=False)
    return eng.matmul(out, w_lo, x_hi, start=False, stop=last)


def rstd_newton(link, dve, ve, rs, tmp):
    link(dve.reciprocal(rs, rs))
    link(dve.tensor_tensor(tmp, rs, rs, ALU.mult))
    link(dve.tensor_tensor(tmp, tmp, ve, ALU.mult))
    link(dve.tensor_scalar(tmp, tmp, -0.5, 1.5, ALU.mult, ALU.add))
    link(dve.tensor_tensor(rs, rs, tmp, ALU.mult))


def moe_phase(nc, x_src, w1, w2, router, router_b, ln_g, ln_b, post_g, post_b, ident_dram, dst, tag):
    tok = ln_g is not None
    NC, _, KW = w1.shape[0], w1.shape[1], w1.shape[2]
    K = x_src.shape[1]
    KT = K // P
    H = w2.shape[1]
    HS = [min(P, H - j) for j in range(0, H, P)]
    HT = len(HS)
    NR = router.shape[1]
    EPS_IN = 1e-6 if tok else 1e-5
    NPC = KT + HT
    NB = 2 if K > 512 else 1
    PAIRS = (NC - 2) // 2

    with ExitStack() as ctx:
        def sb(name, shape, dt=F32):
            return ctx.enter_context(nc.sbuf_tensor(f"{tag}_{name}", shape, dt))

        def sem(name):
            return nc.alloc_semaphore(f"{tag}_{name}")

        x_hi = sb("x_hi", [P, KT, GS * SN], F32R)
        x_lo = sb("x_lo", [P, KT, GS * SN], F32R)
        acc = sb("acc", [TP, GT, D])
        xn = sb("xn", [TP, 2, ST, K])
        w1_hi = sb("w1_hi", [P, 2, KT, 2 * H], F32R)
        w1_lo = sb("w1_lo", [P, 2, KT, 2 * H], F32R)
        w2_hi = sb("w2_hi", [P, 2, HT, D], F32R)
        w2_lo = sb("w2_lo", [P, 2, HT, D], F32R)
        w1_raw = sb("w1_raw", [P, KT, 2 * H])
        w2_raw = sb("w2_raw", [P, HT, D])
        sil = sb("sil", [P, 2, SN])
        hid = sb("hid", [P, 2, SN])
        h_hi = sb("h_hi", [P, 2, HT, SN], F32R)
        h_lo = sb("h_lo", [P, 2, HT, SN], F32R)
        ident = sb("ident", [P, P])
        r_raw = sb("r_raw", [P, KT, NR])
        r_hi = sb("r_hi", [P, KT, NR], F32R)
        r_lo = sb("r_lo", [P, KT, NR], F32R)
        rT = sil[0:NR, 0, :]
        st = sb("st", [TP, ST, NB, 6])
        mv = sb("mv", [TP, GT, 2])
        ve = sb("ve", [TP, GT])
        rs = sb("rs", [TP, GT])
        tmp = sb("tmp", [TP, GT])
        lg = sb("lg", [TP, GT, NR])
        pr = sb("pr", [TP, GT, E])
        key = sb("key", [TP, GT, E])
        one = sb("one", [TP, GT, E])
        red = sb("red", [TP, GT])
        top1 = sb("top1", [TP, GT])
        top2 = sb("top2", [TP, GT])
        comb = sb("comb", [TP, GT, NC])
        if tok:
            xf = sb("xf", [P, 2, SN])
            gb = sb("gb", [P, 2, KT])
            post = sb("post", [TP, 2, D])
            rb = sb("rb", [TP, E])
        iota = sb("iota", [TP, E])
        gu = ctx.enter_context(nc.psum_tensor(f"{tag}_gu", [P, 2, 2, 512], F32))
        dn = ctx.enter_context(nc.psum_tensor(f"{tag}_dn", [P, ST, 512], F32))

        const_in = sem("const_in")
        x_in = [sem(f"x_in{s}") for s in range(GS)]
        w_in = sem("w_in")
        stored = sem("stored")
        zero_done = sem("zero_done")
        iota_done = sem("iota_done")
        var_done = sem("var_done")
        sqrt_done = sem("sqrt_done")
        xn_done = sem("xn_done")
        tr_full = sem("tr_full")
        xf_done = sem("xf_done")
        xhi_done = sem("xhi_done")
        xlo_done = sem("xlo_done")
        rhi_done = sem("rhi_done")
        rlo_done = sem("rlo_done")
        rt_full = sem("rt_full")
        rt_done = sem("rt_done")
        lg_full = sem("lg_full")
        lg_done = sem("lg_done")
        mx_done = sem("mx_done")
        ex_done = sem("ex_done")
        whi_done = sem("whi_done")
        wlo_done = sem("wlo_done")
        gu_full = sem("gu_full")
        sil_done = sem("sil_done")
        h_done = sem("h_done")
        hhi_done = sem("hhi_done")
        hlo_done = sem("hlo_done")
        dn_full = sem("dn_full")
        acc_done = sem("acc_done")
        post_done = sem("post_done")
        psd = sem("psd")
        pve = sem("pve")
        chain = sem("chain")

        def chunks(eng, g, body):
            q0 = g * NC
            body(q0, 0, q0 % 2, True, False)
            with eng.Fori(0, PAIRS) as i:
                for j in (1, 2):
                    body(i * 2 + (q0 + j), i * 2 + j, (q0 + j) % 2, False, False)
            for c in range(2 * PAIRS + 1, NC):
                body(q0 + c, c, (q0 + c) % 2, False, g == GROUPS - 1 and c == NC - 1)

        def raw_pieces(par):
            out = [(w1_raw[:, k, :], w1_hi[:, par, k, :], w1_lo[:, par, k, :]) for k in range(KT)]
            out += [(w2_raw[0:n, j, :], w2_hi[0:n, par, j, :], w2_lo[0:n, par, j, :]) for j, n in enumerate(HS)]
            return out

        NW = 2 if H % P == 0 else 3

        block = ctx.enter_context(nc.Block())

        @block.sync
        def _(sp):
            def load(c):
                sp.dma_start(w1_raw[:], w1[c if isinstance(c, int) else bass.ds(c, 1)].rearrange(
                    "(k p) n -> p k n" if isinstance(c, int) else "o (k p) n -> p (o k) n", p=P)).then_inc(w_in, 16)
                w2c = w2[c] if isinstance(c, int) else w2[bass.ds(c, 1)].rearrange("o h n -> (o h) n")
                full = H // P
                sp.dma_start(w2_raw[:, 0:full, :], w2c[0:full * P, :].rearrange("(j p) n -> p j n", p=P)).then_inc(w_in, 16)
                if H % P:
                    sp.dma_start(w2_raw[0:H % P, full, :], w2c[full * P:H, :]).then_inc(w_in, 16)

            load(0)
            for g in range(GROUPS):
                def body(q, c, par, first, last):
                    if last:
                        return
                    sp.wait_ge(wlo_done, (q + 1) * NPC)
                    load(0 if isinstance(c, int) and c == NC - 1 else c + 1)
                chunks(sp, g, body)

        @block.gpsimd
        def _(pool):
            pool.dma_start(ident[:], ident_dram).then_inc(const_in, 16)
            pool.dma_start(r_raw[:], router.rearrange("(k p) n -> p k n", p=P)).then_inc(const_in, 16)
            if tok:
                pool.dma_start(gb[:, 0, :], ln_g).then_inc(const_in, 16)
                pool.dma_start(gb[:, 1, :], ln_b).then_inc(const_in, 16)
                pool.dma_start(post[:, 0, :], post_g.partition_broadcast(TP)).then_inc(const_in, 16)
                pool.dma_start(post[:, 1, :], post_b.partition_broadcast(TP)).then_inc(const_in, 16)
                pool.dma_start(rb[:], router_b.partition_broadcast(TP)).then_inc(const_in, 16)
            nc.gpsimd.iota(iota[:], pattern=[[1, E]], base=0, channel_multiplier=0,
                           allow_small_or_imprecise_dtypes=True).then_inc(iota_done, 1)
            for g in range(GROUPS):
                if tok:
                    if g:
                        pool.wait_ge(stored, 16 * g)
                    nc.gpsimd.memset(acc[:], 0.0).then_inc(zero_done, 1)
                for s in range(GS):
                    u = g * GS + s
                    rows = x_src[u * SN:(u + 1) * SN, :].rearrange("(t p) k -> p t k", p=TP)
                    if tok:
                        if u >= 2:
                            pool.wait_ge(tr_full, (u - 1) * KT)
                        pool.dma_start(xn[:, u % 2], rows).then_inc(x_in[s], 16)
                    else:
                        if g:
                            pool.wait_ge(stored, 16 * g)
                        pool.dma_start(acc[:, s * ST:(s + 1) * ST, :], rows).then_inc(x_in[s], 16)
                pool.wait_ge(post_done, g + 1)
                pool.dma_start(dst[g * GT * TP:(g + 1) * GT * TP, :].rearrange("(t p) d -> p t d", p=TP),
                               acc[:]).then_inc(stored, 16)
            pool.wait_ge(stored, 16 * GROUPS)

        NCONST = 16 * (7 if tok else 2)

        @block.tensor
        def _(pe):
            pe.wait_ge(const_in, NCONST)
            pe.wait_ge(rlo_done, 1)
            for g in range(GROUPS):
                if g:
                    pe.wait_ge(acc_done, g * NC * GS * ST + ST)
                for s in range(GS):
                    u = g * GS + s
                    pe.wait_ge(xn_done, (u + 1) * ST)
                    for k in range(KT):
                        n = u * KT + k
                        if n >= 2:
                            pe.wait_ge(xf_done if tok else xlo_done, n - 1)
                        for t in range(ST):
                            mm = pe.transpose(dn[:, n % 2, t * TP:(t + 1) * TP],
                                              xn[:, u % 2, t, k * P:(k + 1) * P], ident[0:TP, 0:TP])
                        mm.then_inc(tr_full, 1)
                    pe.wait_ge(xlo_done, (u + 1) * KT)
                    if u:
                        pe.wait_ge(rt_done, u)
                    for k in range(KT):
                        cols = slice(s * SN, (s + 1) * SN)
                        mm = three(pe, dn[0:NR, 2, 0:SN], r_hi[:, k, :], r_lo[:, k, :],
                                   x_hi[:, k, cols], x_lo[:, k, cols], k == 0, k == KT - 1)
                    mm.then_inc(rt_full, 1)
                    pe.wait_ge(rt_done, u + 1)
                    if u:
                        pe.wait_ge(lg_done, u)
                    for t in range(ST):
                        mm = pe.transpose(dn[0:TP, 3, t * NR:(t + 1) * NR], rT[:, t * TP:(t + 1) * TP],
                                          ident[0:NR, 0:NR])
                    mm.then_inc(lg_full, 1)
                pe.wait_ge(lg_done, (g + 1) * GS)

                def down(n, par, npar, s):
                    for t in range(ST):
                        pe.wait_ge(acc_done, n * ST + (t + 1))
                        for j, hs in enumerate(HS):
                            if t == 0:
                                pe.wait_ge(hlo_done, n * HT + (j + 3))
                            tk = slice(t * TP, (t + 1) * TP)
                            mm = three(pe, dn[0:TP, t, :], h_hi[0:hs, npar, j, tk], h_lo[0:hs, npar, j, tk],
                                         w2_hi[0:hs, par, j, :], w2_lo[0:hs, par, j, :], j == 0, j == HT - 1)
                        mm.then_inc(dn_full, 1)

                def body(q, c, par, first, last):
                    pe.wait_ge(wlo_done, (q + 1) * NPC)
                    for s in range(GS):
                        n, npar = q * GS + s, (par + s) % 2
                        cols = slice(s * SN, (s + 1) * SN)
                        for j, hs in enumerate(HS):
                            m, mpar = n * HT + j, (npar + j) % 2 if HT > 1 else npar
                            pe.wait_ge(h_done, m + 1)
                            for half in range(2):
                                for k in range(KT):
                                    wc = slice(half * H + j * P, half * H + j * P + hs)
                                    mm = three(pe, gu[0:hs, mpar, half, 0:SN], w1_hi[:, par, k, wc],
                                               w1_lo[:, par, k, wc], x_hi[:, k, cols], x_lo[:, k, cols],
                                               k == 0, k == KT - 1)
                            mm.then_inc(gu_full, 1)
                        if not (first and s == 0):
                            down(n - 1, par if s else 1 - par, 1 - npar, s)
                chunks(pe, g, body)
                qe = (g + 1) * NC - 1
                down(qe * GS + GS - 1, qe % 2, (qe + GS - 1) % 2, GS - 1)

        @block.scalar
        def _(act):
            act.wait_ge(const_in, NCONST)
            nc.scalar.activation(r_hi[:], r_raw[:], ACT.Copy).then_inc(rhi_done, 1)

            def split(q, par):
                act.wait_ge(w_in, (q + 1) * (16 * NW))
                for raw, hi, _ in raw_pieces(par):
                    nc.scalar.activation(hi, raw, ACT.Copy).then_inc(whi_done, 1)

            for g in range(GROUPS):
                for s in range(GS):
                    u = g * GS + s
                    act.wait_ge(var_done, u + 1)
                    nc.scalar.activation(rs[:, s * ST:(s + 1) * ST], ve[:, s * ST:(s + 1) * ST],
                                         ACT.Sqrt).then_inc(sqrt_done, 1)
                    for k in range(KT):
                        n = u * KT + k
                        cols = slice(s * SN, (s + 1) * SN)
                        act.wait_ge(tr_full, n + 1)
                        if tok:
                            if n >= 2:
                                act.wait_ge(xlo_done, n - 1)
                            nc.scalar.activation(xf[:, n % 2, :], dn[:, n % 2, 0:SN], ACT.Identity,
                                                 bias=gb[:, 1, k:k + 1], scale=gb[:, 0, k:k + 1]).then_inc(xf_done, 1)
                            act.wait_ge(xf_done, n + 1)
                            nc.scalar.activation(x_hi[:, k, cols], xf[:, n % 2, :], ACT.Copy).then_inc(xhi_done, 1)
                        else:
                            nc.scalar.activation(x_hi[:, k, cols], dn[:, n % 2, 0:SN], ACT.Copy).then_inc(xhi_done, 1)
                    act.wait_ge(rt_full, u + 1)
                    if u:
                        act.wait_ge(lg_full, u)
                    nc.scalar.activation(rT[:], dn[0:NR, 2, 0:SN], ACT.Copy).then_inc(rt_done, 1)
                if g == 0:
                    split(0, 0)
                act.wait_ge(mx_done, g + 1)
                nc.scalar.activation(pr[:], key[:], ACT.Exp).then_inc(ex_done, 1)
                if not tok:
                    act.wait_ge(lg_done, (g + 1) * GS)
                    nc.scalar.activation(comb[:, :, E:E + 1], lg[:, :, E:E + 1], ACT.Sigmoid).then_inc(ex_done, 1)

                def body(q, c, par, first, last):
                    for s in range(GS):
                        n, npar = q * GS + s, (par + s) % 2
                        for j, hs in enumerate(HS):
                            m, mpar = n * HT + j, (npar + j) % 2 if HT > 1 else npar
                            act.wait_ge(gu_full, m + 1)
                            act.wait_ge(h_done, m + 1)
                            nc.scalar.activation(sil[0:hs, mpar, :], gu[0:hs, mpar, 0, 0:SN],
                                                 ACT.Silu).then_inc(sil_done, 1)
                            act.wait_ge(h_done, m + 3)
                            if j == 0 and not (first and g == 0 and s < 2):
                                act.wait_ge(dn_full, (n - 1) * ST)
                            nc.scalar.activation(h_hi[0:hs, npar, j, :], hid[0:hs, mpar, :],
                                                 ACT.Copy).then_inc(hhi_done, 1)
                        if s == 0 and not last:
                            if not (first and g == 0):
                                act.wait_ge(dn_full, q * (GS * ST))
                            split(q + 1, 1 - par)
                chunks(act, g, body)
                if tok:
                    act.wait_ge(pve, g + 1)
                    nc.scalar.activation(rs[:], ve[:], ACT.Sqrt).then_inc(psd, 1)

        @block.vector
        def _(dve):
            link = Link(dve, chain)
            dve.sem_inc(h_done, 2)
            dve.sem_inc(hlo_done, 2)
            dve.sem_inc(acc_done, ST)
            if tok:
                link(nc.vector.memset(comb[:, :, E:NC], 1.0))
            dve.wait_ge(rhi_done, 1)
            nc.vector.tensor_tensor(r_lo[:], r_raw[:], r_hi[:].bitcast(F32), ALU.subtract).then_inc(rlo_done, 1)

            def split(q, par):
                for i, (raw, hi, lo) in enumerate(raw_pieces(par)):
                    dve.wait_ge(whi_done, q * NPC + (i + 1))
                    nc.vector.tensor_tensor(lo, raw, hi.bitcast(F32), ALU.subtract).then_inc(wlo_done, 1)

            def stats(src, t, slot, nb):
                for b in range(nb):
                    w = src.shape[-1] // nb
                    link(nc.vector.bn_stats(st[:, t, b, :], src[:, b * w:(b + 1) * w]))
                link(nc.vector.bn_aggr(mv[:, slot, :], st[:, t, 0:nb, :]))

            def bc(ap):
                return ap.unsqueeze(2).broadcast_to((TP, GT, E))

            for g in range(GROUPS):
                for s in range(GS):
                    u = g * GS + s
                    dve.wait_ge(x_in[s], 16 * (g + 1))
                    src = (lambda t: xn[:, u % 2, t, :]) if tok else (lambda t: acc[:, s * ST + t, :])
                    tl = slice(s * ST, (s + 1) * ST)
                    for t in range(ST):
                        stats(src(t), t, s * ST + t, NB)
                    nc.vector.tensor_scalar(ve[:, tl], mv[:, tl, 1], EPS_IN, None, ALU.add).then_inc(var_done, 1)
                    dve.wait_ge(sqrt_done, u + 1)
                    rstd_newton(link, nc.vector, ve[:, tl], rs[:, tl], tmp[:, tl])
                    if u >= 2:
                        dve.wait_ge(tr_full, (u - 1) * KT)
                    for t in range(ST):
                        i = s * ST + t
                        nc.vector.tensor_scalar(xn[:, u % 2, t, :], src(t), mv[:, i, 0:1], rs[:, i:i + 1],
                                                ALU.subtract, ALU.mult).then_inc(xn_done, 1)
                    for k in range(KT):
                        n = u * KT + k
                        cols = slice(s * SN, (s + 1) * SN)
                        dve.wait_ge(xhi_done, n + 1)
                        full = xf[:, n % 2, :] if tok else dn[:, n % 2, 0:SN]
                        nc.vector.tensor_tensor(x_lo[:, k, cols], full, x_hi[:, k, cols].bitcast(F32),
                                                ALU.subtract).then_inc(xlo_done, 1)
                    dve.wait_ge(lg_full, u + 1)
                    lp = dn[0:TP, 3, 0:ST * NR].rearrange("p (t e) -> p t e", e=NR)
                    if tok:
                        nc.vector.tensor_tensor(lg[:, tl, :], lp, rb[:].unsqueeze(1).broadcast_to((TP, ST, E)),
                                                ALU.add).then_inc(lg_done, 1)
                    else:
                        nc.vector.tensor_copy(lg[:, tl, :], lp).then_inc(lg_done, 1)

                if g == 0:
                    split(0, 0)
                dve.wait_ge(lg_done, (g + 1) * GS)
                link(nc.vector.tensor_reduce(red[:], lg[:, :, 0:E], AX.X, ALU.max))
                nc.vector.tensor_tensor(key[:], lg[:, :, 0:E], bc(red[:]), ALU.subtract).then_inc(mx_done, 1)
                dve.wait_ge(ex_done, (g + 1) * (1 if tok else 2))
                dve.wait_ge(iota_done, 1)
                link(nc.vector.tensor_reduce(red[:], pr[:], AX.X, ALU.add))
                link(nc.vector.reciprocal(red[:], red[:]))
                link(nc.vector.tensor_tensor(pr[:], pr[:], bc(red[:]), ALU.mult))
                link(nc.vector.memset(comb[:, :, 0:E], 0.0))
                ib = iota[:].unsqueeze(1).broadcast_to((TP, GT, E))
                for top in (top1, top2):
                    link(nc.vector.tensor_reduce(top[:], pr[:], AX.X, ALU.max))
                    link(nc.vector.tensor_tensor(key[:], pr[:], bc(top[:]), ALU.is_lt))
                    link(nc.vector.tensor_scalar(key[:], key[:], float(E), None, ALU.mult))
                    link(nc.vector.tensor_tensor(key[:], key[:], ib, ALU.add))
                    link(nc.vector.tensor_reduce(red[:], key[:], AX.X, ALU.min))
                    link(nc.vector.tensor_tensor(one[:], ib, bc(red[:]), ALU.is_equal))
                    link(nc.vector.tensor_tensor(key[:], one[:], bc(top[:]), ALU.mult))
                    link(nc.vector.tensor_tensor(comb[:, :, 0:E], comb[:, :, 0:E], key[:], ALU.add))
                    link(nc.vector.tensor_scalar(one[:], one[:], -2.0, None, ALU.mult))
                    link(nc.vector.tensor_tensor(pr[:], pr[:], one[:], ALU.add))
                link(nc.vector.tensor_tensor(red[:], top1[:], top2[:], ALU.add))
                if tok:
                    link(nc.vector.tensor_scalar(red[:], red[:], 1e-20, None, ALU.add))
                link(nc.vector.reciprocal(red[:], red[:]))
                link(nc.vector.tensor_tensor(comb[:, :, 0:E], comb[:, :, 0:E], bc(red[:]), ALU.mult))
                if not tok:
                    link(nc.vector.tensor_copy(comb[:, :, E + 1:E + 2], comb[:, :, E:E + 1]))
                if tok:
                    dve.wait_ge(zero_done, g + 1)

                def add(n, c, s):
                    for t in range(ST):
                        i = s * ST + t
                        dve.wait_ge(dn_full, n * ST + (t + 1))
                        w = comb[:, i, c:c + 1] if isinstance(c, int) else comb[:, i, bass.ds(c, 1)]
                        if not (isinstance(n, int) and n < GS):
                            dve.wait_ge(acc_done, (n - GS) * ST + (t + 1 + ST))
                        nc.vector.scalar_tensor_tensor(out=acc[:, i, :], in0=dn[0:TP, t, :], scalar=w,
                                                       in1=acc[:, i, :], op0=ALU.mult,
                                                       op1=ALU.add).then_inc(acc_done, 1)

                def body(q, c, par, first, last):
                    for s in range(GS):
                        n, npar = q * GS + s, (par + s) % 2
                        for j, hs in enumerate(HS):
                            m, mpar = n * HT + j, (npar + j) % 2 if HT > 1 else npar
                            dve.wait_ge(sil_done, m + 1)
                            dve.wait_ge(hlo_done, m + 1)
                            nc.vector.tensor_tensor(hid[0:hs, mpar, :], sil[0:hs, mpar, :],
                                                    gu[0:hs, mpar, 1, 0:SN], ALU.mult).then_inc(h_done, 1)
                            dve.wait_ge(hhi_done, m + 1)
                            nc.vector.tensor_tensor(h_lo[0:hs, npar, j, :], hid[0:hs, mpar, :],
                                                    h_hi[0:hs, npar, j, :].bitcast(F32),
                                                    ALU.subtract).then_inc(hlo_done, 1)
                        if s == 0 and not last:
                            split(q + 1, 1 - par)
                        if not (first and s == 0):
                            add(n - 1, c if s else c - 1, (s - 1) % GS)
                chunks(dve, g, body)
                qe = (g + 1) * NC - 1
                add(qe * GS + GS - 1, NC - 1, GS - 1)

                if tok:
                    dve.wait_ge(acc_done, (g + 1) * NC * GS * ST + ST)
                    for i in range(GT):
                        stats(acc[:, i, :], i % ST, i, 1)
                    nc.vector.tensor_scalar(ve[:], mv[:, :, 1], 1e-6, None, ALU.add).then_inc(pve, 1)
                    dve.wait_ge(psd, g + 1)
                    rstd_newton(link, nc.vector, ve[:], rs[:], tmp[:])
                    for i in range(GT):
                        link(nc.vector.tensor_scalar(acc[:, i, :], acc[:, i, :], mv[:, i, 0:1], rs[:, i:i + 1],
                                                     ALU.subtract, ALU.mult))
                        link(nc.vector.tensor_tensor(acc[:, i, :], acc[:, i, :], post[:, 0, :], ALU.mult))
                        link(nc.vector.tensor_tensor(acc[:, i, :], acc[:, i, :], post[:, 1, :], ALU.add))
                    dve.sem_inc(post_done, 1)
                else:
                    dve.wait_ge(acc_done, (g + 1) * NC * GS * ST + ST)
                    dve.sem_inc(post_done, 1)



def kv_phase(nc, h_src, wk, wv, bk, bv, ident_dram, xT_hi_d, xT_lo_d, kv_hi_d, kv_lo_d):
    KT = D // P
    VW = HD + 2
    with ExitStack() as ctx:
        def sb(name, shape, dt=F32):
            return ctx.enter_context(nc.sbuf_tensor(f"kv_{name}", shape, dt))

        def sem(name):
            return nc.alloc_semaphore(f"kv_{name}")

        ident = sb("ident", [P, P])
        w_raw = sb("w_raw", [P, 2, KT, D])
        w_hi = sb("w_hi", [P, 2, KT, D], F32R)
        w_lo = sb("w_lo", [P, 2, KT, D], F32R)
        bias = sb("bias", [TP, 2, D])
        h_in = sb("h_in", [TP, 2, BT, D])
        xn = sb("xn", [TP, 2, BT, D])
        x_hi = sb("x_hi", [P, 2, KT, BN], F32R)
        x_lo = sb("x_lo", [P, 2, KT, BN], F32R)
        kf = sb("kf", [TP, 2, D])
        ex = sb("ex", [TP, 2, D])
        vf = sb("vf", [TP, 2, D])
        k_hi = sb("k_hi", [TP, 2, BT, D], F32R)
        k_lo = sb("k_lo", [TP, 2, BT, D], F32R)
        v_hi = sb("v_hi", [TP, 2, BT, NKV, VW], F32R)
        v_lo = sb("v_lo", [TP, 2, BT, NKV, VW], F32R)
        kv_hi = sb("kv_hi", [P, 2, NKV, VW], F32R)
        kv_lo = sb("kv_lo", [P, 2, NKV, VW], F32R)
        st = sb("st", [TP, BT, 6])
        fence = sb("fence", [1, 2])
        mv = sb("mv", [TP, BT, 2])
        ve = sb("ve", [TP, BT])
        rs = sb("rs", [TP, BT])
        tmp = sb("tmp", [TP, BT])
        tp = ctx.enter_context(nc.psum_tensor("kv_tp", [P, 2, 512], F32))
        kp = ctx.enter_context(nc.psum_tensor("kv_kp", [P, 2, 2, 512], F32))
        kvp = ctx.enter_context(nc.psum_tensor("kv_kvp", [P, 2, 512], F32))

        const_in = sem("const_in")
        h_loaded = [sem("h_in0"), sem("h_in1")]
        x_out = [sem("x_out0"), sem("x_out1")]
        kv_out = [sem("kv_out0"), sem("kv_out1")]
        pads = sem("pads")
        whi_done = sem("whi_done")
        wlo_done = sem("wlo_done")
        var_done = sem("var_done")
        sqrt_done = sem("sqrt_done")
        xn_done = sem("xn_done")
        tr_full = sem("tr_full")
        xhi_done = sem("xhi_done")
        xlo_done = sem("xlo_done")
        k_full = sem("k_full")
        v_full = sem("v_full")
        kb_done = sem("kb_done")
        mn_done = sem("mn_done")
        ex_done = sem("ex_done")
        sk_done = sem("sk_done")
        vb_done = sem("vb_done")
        khi_done = sem("khi_done")
        vhi_done = sem("vhi_done")
        klo_done = sem("klo_done")
        vlo_done = sem("vlo_done")
        kv_full = sem("kv_full")
        kvhi_done = sem("kvhi_done")
        kvlo_done = sem("kvlo_done")
        bn_done = sem("bn_done")
        aggr_done = sem("aggr_done")
        chain = sem("chain")

        def sequences(eng, body):
            for b in range(2):
                body(b, b, True)
            with eng.Fori(2, B - 1, 2) as i:
                for par in range(2):
                    body(i + par, par, False)

        def at(d, b):
            return d[b] if isinstance(b, int) else d[bass.ds(b, 1)].squeeze(0)

        block = ctx.enter_context(nc.Block())

        def rows(b):
            r = h_src[b * (BT * TP):(b + 1) * (BT * TP), :] if isinstance(b, int) \
                else h_src[bass.ds(b * (BT * TP), BT * TP), :]
            return r.rearrange("(t p) d -> p t d", p=TP)

        @block.sync
        def _(sp):
            sp.dma_start(h_in[:, 0], rows(0)).then_inc(h_loaded[0], 16)
            sp.dma_start(ident[:], ident_dram).then_inc(const_in, 16)
            sp.dma_start(w_raw[:, 0], wk.rearrange("(k p) n -> p k n", p=P)).then_inc(const_in, 16)
            sp.dma_start(w_raw[:, 1], wv.rearrange("(k p) n -> p k n", p=P)).then_inc(const_in, 16)
            sp.dma_start(bias[:, 0, :], bk.partition_broadcast(TP)).then_inc(const_in, 16)
            sp.dma_start(bias[:, 1, :], bv.partition_broadcast(TP)).then_inc(const_in, 16)
            sp.dma_start(h_in[:, 1], rows(1)).then_inc(h_loaded[1], 16)
            with sp.Fori(2, B - 1, 2) as i:
                for par in range(2):
                    sp.wait_ge(xn_done, (i + (par - 1)) * BT)
                    sp.dma_start(h_in[:, par], rows(i + par)).then_inc(h_loaded[par], 16)

        @block.gpsimd
        def _(pool):
            nc.gpsimd.memset(x_hi[:, :, :, BT * TP:BN].bitcast(F32), 0.0).then_inc(pads, 1)
            nc.gpsimd.memset(x_lo[:, :, :, BT * TP:BN].bitcast(F32), 0.0).then_inc(pads, 1)
            nc.gpsimd.memset(v_hi[:, :, :, :, HD:VW].bitcast(F32), 1.0).then_inc(pads, 1)
            nc.gpsimd.memset(v_lo[:, :, :, :, HD:VW].bitcast(F32), 0.0).then_inc(pads, 1)
            pool.wait_ge(pads, 4)

            def body(b, par, first):
                pool.wait_ge(xlo_done, (b + 1) * KT)
                pool.dma_start(at(xT_hi_d, b), x_hi[:, par].bitcast(F32)).then_inc(x_out[par], 16)
                pool.dma_start(at(xT_lo_d, b), x_lo[:, par].bitcast(F32)).then_inc(x_out[par], 16)
                pool.wait_ge(kvlo_done, (b + 1) * 2)
                pool.dma_start(at(kv_hi_d, b), kv_hi[:, par].bitcast(F32)).then_inc(kv_out[par], 16)
                pool.dma_start(at(kv_lo_d, b), kv_lo[:, par].bitcast(F32)).then_inc(kv_out[par], 16)
            sequences(pool, body)
            for par in range(2):
                pool.wait_ge(x_out[par], 16 * B)
                pool.wait_ge(kv_out[par], 16 * B)

        @block.tensor
        def _(pe):
            pe.wait_ge(const_in, 80)
            pe.wait_ge(pads, 4)
            pe.wait_ge(wlo_done, 2)

            def project(b, par, first):
                for k in range(KT):
                    pe.wait_ge(xn_done, (b + 1) * BT)
                    if not (first and b == 0 and k < 2):
                        pe.wait_ge(xlo_done, b * KT + (k - 1))
                    for i in range(BT):
                        mm = pe.transpose(tp[:, k % 2, i * TP:(i + 1) * TP], xn[:, par, i, k * P:(k + 1) * P],
                                          ident[0:TP, 0:TP])
                    mm.then_inc(tr_full, 1)
                pe.wait_ge(xlo_done, (b + 1) * KT)
                for i in range(BT):
                    n = b * BT + i
                    bank = (par + i) % 2
                    for j, free, full in ((0, kb_done, k_full), (1, vb_done, v_full)):
                        if not (first and b * BT + i < 2):
                            pe.wait_ge(free, n - 1)
                        for k in range(KT):
                            tk = slice(i * TP, (i + 1) * TP)
                            mm = three(pe, kp[0:TP, bank, j, :], x_hi[:, par, k, tk], x_lo[:, par, k, tk],
                                       w_hi[:, j, k, :], w_lo[:, j, k, :], k == 0, k == KT - 1)
                        mm.then_inc(full, 1)

            def sums(b, par, first):
                pe.wait_ge(klo_done, (b + 1) * BT)
                pe.wait_ge(vlo_done, (b + 1) * BT)
                for g in range(NKV):
                    if g % 2 == 0 and not (first and b == 0):
                        pe.wait_ge(kvlo_done, b * 2 + (g // 2 - 1))
                    for i in range(BT):
                        hd = slice(g * HD, (g + 1) * HD)
                        mm = three(pe, kvp[:, g // 2, (g % 2) * VW:(g % 2 + 1) * VW], k_hi[:, par, i, hd],
                                   k_lo[:, par, i, hd], v_hi[:, par, i, g, :], v_lo[:, par, i, g, :],
                                   i == 0, i == BT - 1)
                    if g % 2:
                        mm.then_inc(kv_full, 1)

            project(0, 0, True)
            project(1, 1, True)
            sums(0, 0, True)
            with pe.Fori(2, B - 1, 2) as i:
                for par in range(2):
                    project(i + par, par, False)
                    sums(i + (par - 1), 1 - par, False)
            sums(B - 1, (B - 1) % 2, False)

        @block.scalar
        def _(act):
            act.wait_ge(const_in, 80)
            act.wait_ge(pads, 4)
            for j in range(2):
                nc.scalar.activation(w_hi[:, j], w_raw[:, j], ACT.Copy).then_inc(whi_done, 1)

            def project(b, par, first):
                act.wait_ge(var_done, b + 1)
                nc.scalar.activation(rs[:], ve[:], ACT.Sqrt).then_inc(sqrt_done, 1)
                if not first:
                    act.wait_ge(x_out[par], (b - par) * 16)
                    act.wait_ge(v_full, (b - 1) * BT)
                for k in range(KT):
                    act.wait_ge(tr_full, b * KT + (k + 1))
                    nc.scalar.activation(x_hi[:, par, k, 0:BT * TP], tp[:, k % 2, 0:BT * TP],
                                         ACT.Copy).then_inc(xhi_done, 1)
                if not first:
                    act.wait_ge(kv_full, (b - 1) * 2)
                for i in range(BT):
                    n, z = b * BT + i, (par + i) % 2
                    act.wait_ge(mn_done, n + 1)
                    nc.scalar.activation(ex[:, z, :], ex[:, z, :], ACT.Exp).then_inc(ex_done, 1)
                    act.wait_ge(sk_done, n + 1)
                    nc.scalar.activation(k_hi[:, par, i, :], kf[:, z, :], ACT.Copy).then_inc(khi_done, 1)
                    act.wait_ge(vb_done, n + 1)
                    nc.scalar.activation(v_hi[:, par, i, :, 0:HD], vf[:, z, :].rearrange("p (g d) -> p g d", d=HD),
                                         ACT.Copy).then_inc(vhi_done, 1)

            def sums(b, par, first):
                if not first:
                    act.wait_ge(kv_out[par], (b - par) * 16)
                for c in range(2):
                    act.wait_ge(kv_full, b * 2 + (c + 1))
                    nc.scalar.activation(kv_hi[:, par, 2 * c:2 * c + 2, :],
                                         kvp[:, c, 0:2 * VW].rearrange("p (g d) -> p g d", d=VW),
                                         ACT.Copy).then_inc(kvhi_done, 1)

            project(0, 0, True)
            project(1, 1, True)
            sums(0, 0, True)
            project(2, 0, False)
            sums(1, 1, True)
            project(3, 1, False)
            sums(2, 0, False)
            with act.Fori(4, B - 1, 2) as i:
                for par in range(2):
                    project(i + par, par, False)
                    sums(i + (par - 1), 1 - par, False)
            sums(B - 1, (B - 1) % 2, False)

        @block.vector
        def _(dve):
            link = Link(dve, chain)
            for j in range(2):
                dve.wait_ge(whi_done, j + 1)
                nc.vector.tensor_tensor(w_lo[:, j], w_raw[:, j], w_hi[:, j].bitcast(F32),
                                        ALU.subtract).then_inc(wlo_done, 1)
            PER = 5

            def project(b, par, first):
                link.start(b * PER)
                dve.wait_ge(h_loaded[par], (b - par) * 8 + 16)
                for i in range(BT):
                    nc.vector.bn_stats(st[:, i, :], h_in[:, par, i, :]).then_inc(bn_done, 1)
                for i in range(BT):
                    if i == 0:
                        dve.wait_ge(bn_done, (b + 1) * BT)
                        nc.vector.memset(fence[:, par:par + 1], 0.0)
                    nc.vector.bn_aggr(mv[:, i, :], st[:, i, :]).then_inc(aggr_done, 1)
                dve.wait_ge(aggr_done, (b + 1) * BT)
                nc.vector.tensor_scalar(ve[:], mv[:, :, 1], 1e-5, None, ALU.add).then_inc(var_done, 1)
                dve.wait_ge(sqrt_done, b + 1)
                rstd_newton(link, nc.vector, ve[:], rs[:], tmp[:])
                if not first:
                    dve.wait_ge(tr_full, (b - 1) * KT)
                for i in range(BT):
                    nc.vector.tensor_scalar(xn[:, par, i, :], h_in[:, par, i, :], mv[:, i, 0:1], rs[:, i:i + 1],
                                            ALU.subtract, ALU.mult).then_inc(xn_done, 1)
                for k in range(KT):
                    dve.wait_ge(xhi_done, b * KT + (k + 1))
                    nc.vector.tensor_tensor(x_lo[:, par, k, 0:BT * TP], tp[:, k % 2, 0:BT * TP],
                                            x_hi[:, par, k, 0:BT * TP].bitcast(F32),
                                            ALU.subtract).then_inc(xlo_done, 1)
                for i in range(BT):
                    n, z = b * BT + i, (par + i) % 2
                    early = first and b * BT + i < 2
                    dve.wait_ge(k_full, n + 1)
                    if not early:
                        dve.wait_ge(klo_done, n - 1)
                    nc.vector.tensor_tensor(kf[:, z, :], kp[0:TP, z, 0, :], bias[:, 0, :], ALU.add).then_inc(kb_done, 1)
                    dve.wait_ge(kb_done, n + 1)
                    nc.vector.tensor_scalar(ex[:, z, :], kf[:, z, :], 0.0, None, ALU.min).then_inc(mn_done, 1)
                    dve.wait_ge(v_full, n + 1)
                    if not early:
                        dve.wait_ge(vlo_done, n - 1)
                    nc.vector.tensor_tensor(vf[:, z, :], kp[0:TP, z, 1, :], bias[:, 1, :], ALU.add).then_inc(vb_done, 1)
                    dve.wait_ge(ex_done, n + 1)
                    nc.vector.scalar_tensor_tensor(out=kf[:, z, :], in0=kf[:, z, :], scalar=0.0, in1=ex[:, z, :],
                                                   op0=ALU.max, op1=ALU.add).then_inc(sk_done, 1)
                    dve.wait_ge(khi_done, n + 1)
                    nc.vector.tensor_tensor(k_lo[:, par, i, :], kf[:, z, :], k_hi[:, par, i, :].bitcast(F32),
                                            ALU.subtract).then_inc(klo_done, 1)
                    dve.wait_ge(vhi_done, n + 1)
                    nc.vector.tensor_tensor(v_lo[:, par, i, :, 0:HD], vf[:, z, :].rearrange("p (g d) -> p g d", d=HD),
                                            v_hi[:, par, i, :, 0:HD].bitcast(F32),
                                            ALU.subtract).then_inc(vlo_done, 1)
                assert link.n == PER

            def sums(b, par, first):
                for c in range(2):
                    dve.wait_ge(kvhi_done, b * 2 + (c + 1))
                    nc.vector.tensor_tensor(kv_lo[:, par, 2 * c:2 * c + 2, :],
                                            kvp[:, c, 0:2 * VW].rearrange("p (g d) -> p g d", d=VW),
                                            kv_hi[:, par, 2 * c:2 * c + 2, :].bitcast(F32),
                                            ALU.subtract).then_inc(kvlo_done, 1)

            project(0, 0, True)
            project(1, 1, True)
            sums(0, 0, True)
            with dve.Fori(2, B - 1, 2) as i:
                for par in range(2):
                    project(i + par, par, False)
                    sums(i + (par - 1), 1 - par, False)
            sums(B - 1, (B - 1) % 2, False)


def query_phase(nc, h_src, wq, wo, bq, ident_dram, xT_hi_d, xT_lo_d, kv_hi_d, kv_lo_d, dst):
    KT = D // P
    VW = HD + 2
    PIECE = 1024
    NPQ = KT * NH * HD // PIECE
    with ExitStack() as ctx:
        def sb(name, shape, dt=F32):
            return ctx.enter_context(nc.sbuf_tensor(f"q_{name}", shape, dt))

        def sem(name):
            return nc.alloc_semaphore(f"q_{name}")

        ident = sb("ident", [P, P])
        raw = sb("raw", [P, 2, PIECE])
        wq_hi = sb("wq_hi", [P, KT, NH * HD], F32R)
        wq_lo = sb("wq_lo", [P, KT, NH * HD], F32R)
        wo_hi = sb("wo_hi", [P, NH, D], F32R)
        wo_lo = sb("wo_lo", [P, NH, D], F32R)
        bias = sb("bias", [P, NH])
        x_hi = sb("x_hi", [P, 2, KT, BN], F32R)
        x_lo = sb("x_lo", [P, 2, KT, BN], F32R)
        kv_hi = sb("kv_hi", [P, 2, NKV, VW], F32R)
        kv_lo = sb("kv_lo", [P, 2, NKV, VW], F32R)
        res = sb("res", [TP, 2, BT, D])
        rel = sb("rel", [P, 2, BN])
        ex = sb("ex", [P, 2, BN])
        q_hi = sb("q_hi", [P, 2, BN], F32R)
        q_lo = sb("q_lo", [P, 2, BN], F32R)
        rn = sb("rn", [TP, BT, 1])
        at = sb("at", [TP, 2, BT, HD])
        a_hi = sb("a_hi", [P, 2, BN], F32R)
        a_lo = sb("a_lo", [P, 2, BN], F32R)
        qp = ctx.enter_context(nc.psum_tensor("q_qp", [P, 2, 512], F32))
        op = ctx.enter_context(nc.psum_tensor("q_op", [P, 512], F32))
        tp = ctx.enter_context(nc.psum_tensor("q_tp", [P, 512], F32))
        wp = ctx.enter_context(nc.psum_tensor("q_wp", [P, BT, 512], F32))

        const_in = sem("const_in")
        w_in = [sem("w_in0"), sem("w_in1")]
        b_in = [sem("b_in0"), sem("b_in1")]
        stored = [sem("stored0"), sem("stored1")]
        whi_done = sem("whi_done")
        wlo_done = sem("wlo_done")
        q_full = sem("q_full")
        rel_done = sem("rel_done")
        mn_done = sem("mn_done")
        ex_done = sem("ex_done")
        sq_done = sem("sq_done")
        qhi_done = sem("qhi_done")
        qlo_done = sem("qlo_done")
        o_full = sem("o_full")
        at_done = sem("at_done")
        tr_full = sem("tr_full")
        ahi_done = sem("ahi_done")
        alo_done = sem("alo_done")
        wo_full = sem("wo_full")
        res_done = sem("res_done")
        chain = sem("chain")

        STEPS = 2 * NH
        SKEW = 3

        def steps(eng, body):
            for l in range(STEPS):
                body(0, l, True)
            with eng.Fori(STEPS, B * NH, STEPS) as n0:
                for l in range(STEPS):
                    body(n0, l, False)
            for l in range(SKEW):
                body(B * NH, l, None)

        def head(l):
            l = l % STEPS
            return l // NH, l % NH, l % 2

        def at_seq(d, b):
            return d[b] if isinstance(b, int) else d[bass.ds(b, 1)].squeeze(0)

        def rows(d, b):
            r = d[b * (BT * TP):(b + 1) * (BT * TP), :] if isinstance(b, int) \
                else d[bass.ds(b * (BT * TP), BT * TP), :]
            return r.rearrange("(t p) d -> p t d", p=TP)

        block = ctx.enter_context(nc.Block())

        wo_v = wo.rearrange("(h p) n -> p h n", p=P)

        def piece(i):
            if i < NPQ:
                k, c = divmod(i, NH * HD // PIECE)
                return (wq[k * P:(k + 1) * P, c * PIECE:(c + 1) * PIECE], wq_hi[:, k, c * PIECE:(c + 1) * PIECE], wq_lo[:, k, c * PIECE:(c + 1) * PIECE])
            h = (i - NPQ) * (PIECE // D)
            hs = slice(h, h + PIECE // D)
            return (wo_v[:, hs, :], wo_hi[:, hs, :], wo_lo[:, hs, :])

        def raw_of(i):
            return raw[:, i % 2, :] if i < NPQ else raw[:, i % 2, :].rearrange("p (h n) -> p h n", n=D)

        @block.sync
        def _(sp):
            def load(b, par):
                for d, s in ((xT_hi_d, x_hi), (xT_lo_d, x_lo), (kv_hi_d, kv_hi), (kv_lo_d, kv_lo)):
                    sp.dma_start(s[:, par].bitcast(F32), at_seq(d, b)).then_inc(b_in[par], 16)
                sp.dma_start(res[:, par], rows(h_src, b)).then_inc(b_in[par], 16)

            sp.dma_start(ident[:], ident_dram).then_inc(const_in, 16)
            sp.dma_start(bias[:], bq).then_inc(const_in, 16)
            for i in range(2 * NPQ):
                if i == 4:
                    load(0, 0)
                if i >= 2:
                    sp.wait_ge(wlo_done, i - 1)
                sp.dma_start(raw_of(i), piece(i)[0]).then_inc(w_in[i % 2], 16)
            load(1, 1)
            with sp.Fori(2, B - 1, 2) as b:
                for par in range(2):
                    sp.wait_ge(stored[par], b * 8)
                    load(b + par, par)

        @block.gpsimd
        def _(pool):
            with pool.Fori(0, B - 1, 2) as b:
                for par in range(2):
                    pool.wait_ge(res_done, (b + (par + 1)) * BT)
                    pool.dma_start(rows(dst, b + par), res[:, par]).then_inc(stored[par], 16)
            for par in range(2):
                pool.wait_ge(stored[par], 8 * B)

        @block.tensor
        def _(pe):
            pe.wait_ge(const_in, 32)
            pe.wait_ge(wlo_done, 2 * NPQ)

            def body(n0, l, new):
                if new is not None:
                    s, h, z = head(l)
                    if h == 0:
                        pe.wait_ge(b_in[s], n0 * (5 * 16) // (2 * NH) + 80 if isinstance(n0, int) else
                                   (n0 // (2 * NH)) * 80 + 80)
                    if not (new and l < 2):
                        pe.wait_ge(mn_done, n0 + (l - 1))
                        pe.wait_ge(rel_done, n0 + (l - 1))
                    for k in range(KT):
                        hd = slice(h * HD, (h + 1) * HD)
                        mm = three(pe, qp[:, z, 0:BN], wq_hi[:, k, hd], wq_lo[:, k, hd], x_hi[:, s, k, :],
                                   x_lo[:, s, k, :], k == 0, k == KT - 1)
                    mm.then_inc(q_full, 1)
                if not (new and l < 1) and not (new is None and l >= 1):
                    s, h, z = head(l - 1)
                    pe.wait_ge(qlo_done, n0 + l)
                    if not (new and l < 2):
                        pe.wait_ge(at_done, n0 + (l - 1))
                    for i in range(BT):
                        tk = slice(i * TP, (i + 1) * TP)
                        mm = three(pe, op[0:TP, i * VW:(i + 1) * VW], q_hi[:, z, tk], q_lo[:, z, tk],
                                   kv_hi[:, s, h // (NH // NKV), :], kv_lo[:, s, h // (NH // NKV), :], True, True)
                    mm.then_inc(o_full, 1)
                if not (new and l < 2) and not (new is None and l >= 2):
                    s, h, z = head(l - 2)
                    pe.wait_ge(at_done, n0 + (l - 1))
                    if not (new and l < 3):
                        pe.wait_ge(alo_done, n0 + (l - 2))
                    for i in range(BT):
                        mm = pe.transpose(tp[:, i * TP:(i + 1) * TP], at[:, z, i, :], ident[0:TP, 0:TP])
                    mm.then_inc(tr_full, 1)
                if not (new and l < 3):
                    s, h, z = head(l - 3)
                    pe.wait_ge(alo_done, n0 + (l - 2))
                    if h == 0 and not (new and l < NH):
                        pe.wait_ge(res_done, 3 * ((l - 3) // NH) if isinstance(n0, int) and n0 == 0 else
                                   (n0 // NH) * BT + BT * ((l - 3) // NH))
                    for i in range(BT):
                        tk = slice(i * TP, (i + 1) * TP)
                        mm = three(pe, wp[0:TP, i, :], a_hi[:, z, tk], a_lo[:, z, tk], wo_hi[:, h, :],
                                   wo_lo[:, h, :], h == 0, h == NH - 1)
                    mm.then_inc(wo_full, 1)
            steps(pe, body)

        @block.scalar
        def _(act):
            act.wait_ge(const_in, 32)
            for i in range(2 * NPQ):
                act.wait_ge(w_in[i % 2], 16 * (i // 2 + 1))
                nc.scalar.activation(piece(i)[1], raw_of(i), ACT.Copy).then_inc(whi_done, 1)

            def body(n0, l, new):
                if new is not None:
                    s, h, z = head(l)
                    act.wait_ge(q_full, n0 + (l + 1))
                    if not (new and l < 2):
                        act.wait_ge(qlo_done, n0 + (l - 1))
                    nc.scalar.activation(rel[:, z, :], qp[:, z, 0:BN], ACT.Relu, bias=bias[:, h:h + 1]).then_inc(rel_done, 1)
                    act.wait_ge(mn_done, n0 + (l + 1))
                    nc.scalar.activation(ex[:, z, :], ex[:, z, :], ACT.Exp).then_inc(ex_done, 1)
                    act.wait_ge(sq_done, n0 + (l + 1))
                    if not (new and l < 2):
                        act.wait_ge(o_full, n0 + (l - 1))
                    nc.scalar.activation(q_hi[:, z, :], rel[:, z, :], ACT.Copy).then_inc(qhi_done, 1)
                if not (new and l < 2) and not (new is None and l >= 2):
                    s, h, z = head(l - 2)
                    act.wait_ge(tr_full, n0 + (l - 1))
                    if not (new and l < 4):
                        act.wait_ge(wo_full, n0 + (l - 3))
                    nc.scalar.activation(a_hi[:, z, 0:BT * TP], tp[:, 0:BT * TP], ACT.Copy).then_inc(ahi_done, 1)
            steps(act, body)

        @block.vector
        def _(dve):
            for i in range(2 * NPQ):
                dve.wait_ge(whi_done, i + 1)
                _, hi, lo = piece(i)
                nc.vector.tensor_tensor(lo, raw_of(i), hi.bitcast(F32), ALU.subtract).then_inc(wlo_done, 1)
            dve.wait_ge(const_in, 32)
            link = Link(dve, chain)

            def body(n0, l, new):
                if new is not None:
                    s, h, z = head(l)
                    dve.wait_ge(rel_done, n0 + (l + 1))
                    if not (new and l < 2):
                        dve.wait_ge(sq_done, n0 + (l - 1))
                    nc.vector.tensor_scalar(ex[:, z, :], qp[:, z, 0:BN], bias[:, h:h + 1], 0.0, ALU.add,
                                            ALU.min).then_inc(mn_done, 1)
                    dve.wait_ge(ex_done, n0 + (l + 1))
                    nc.vector.tensor_tensor(rel[:, z, :], rel[:, z, :], ex[:, z, :], ALU.add).then_inc(sq_done, 1)
                    dve.wait_ge(qhi_done, n0 + (l + 1))
                    nc.vector.tensor_tensor(q_lo[:, z, :], rel[:, z, :], q_hi[:, z, :].bitcast(F32),
                                            ALU.subtract).then_inc(qlo_done, 1)
                if not (new and l < 1) and not (new is None and l >= 1):
                    s, h, z = head(l - 1)
                    dve.wait_ge(o_full, n0 + l)
                    if not (new and l < 3):
                        dve.wait_ge(tr_full, n0 + (l - 2))
                    link.start((n0 + (l - 1)) * 2)
                    o3 = op[0:TP, 0:BT * VW].rearrange("p (t v) -> p t v", v=VW)
                    link(nc.vector.tensor_scalar(rn[:], o3[:, :, HD:HD + 1], 1e-6, None, ALU.add))
                    link(nc.vector.reciprocal(rn[:], rn[:]))
                    nc.vector.tensor_tensor(at[:, z], o3[:, :, 0:HD], rn[:].broadcast_to((TP, BT, HD)),
                                            ALU.mult).then_inc(at_done, 1)
                if not (new and l < 2) and not (new is None and l >= 2):
                    s, h, z = head(l - 2)
                    dve.wait_ge(ahi_done, n0 + (l - 1))
                    nc.vector.tensor_tensor(a_lo[:, z, 0:BT * TP], tp[:, 0:BT * TP],
                                            a_hi[:, z, 0:BT * TP].bitcast(F32), ALU.subtract).then_inc(alo_done, 1)
                if not (new and l < 3):
                    s, h, z = head(l - 3)
                    if h == NH - 1:
                        dve.wait_ge(wo_full, n0 + (l - 2))
                        for i in range(BT):
                            nc.vector.tensor_tensor(res[:, s, i, :], wp[0:TP, i, :], res[:, s, i, :],
                                                    ALU.add).then_inc(res_done, 1)
            steps(dve, body)


def build(nc, x, ln_pre_g, ln_pre_b, tok_router, tok_router_b, tok_w1, tok_w2, ln_post_g, ln_post_b, wq, bq, wk,
          bk, wv, bv, wo, ffn_router, ffn_w1, ffn_w2, ident, out):
    def scratch(name, shape, dt):
        return nc.dram_tensor(name, shape, dt, kind="Internal").ap()

    h1 = scratch("h1", (T, D), F32)
    h2 = scratch("h2", (T, D), F32)
    xT_hi = scratch("xT_hi", (B, P, D // P, BN), F32)
    xT_lo = scratch("xT_lo", (B, P, D // P, BN), F32)
    kv_hi = scratch("kv_hi", (B, P, NKV, HD + 2), F32)
    kv_lo = scratch("kv_lo", (B, P, NKV, HD + 2), F32)
    moe_phase(nc, x, tok_w1, tok_w2, tok_router, tok_router_b, ln_pre_g, ln_pre_b, ln_post_g, ln_post_b, ident, h1, "tok")
    kv_phase(nc, h1, wk, wv, bk, bv, ident, xT_hi, xT_lo, kv_hi, kv_lo)
    query_phase(nc, h1, wq, wo, bq, ident, xT_hi, xT_lo, kv_hi, kv_lo, h2)
    moe_phase(nc, h2, ffn_w1, ffn_w2, ffn_router, None, None, None, None, None, ident, out, "ffn")


def kernel(**inputs):
    import numpy as np
    from concourse import bacc
    from concourse.bass_utils import run_bass_kernel_spmd

    a = {k: np.asarray(v) for k, v in inputs.items()}
    L = "L0_"
    shw_g, shw_u, shw_d = a[L + "ffn_shw_gate"], a[L + "ffn_shw_up"], a[L + "ffn_shw_down"]
    H = a[L + "ffn_w_gate"].shape[2]
    halves = [slice(i * H, (i + 1) * H) for i in range(shw_g.shape[1] // H)]
    w_gate = np.concatenate([a[L + "ffn_w_gate"]] + [shw_g[None, :, s] for s in halves])
    w_up = np.concatenate([a[L + "ffn_w_up"]] + [shw_u[None, :, s] for s in halves])
    arrays = {
        "x": a["x"].reshape(T, -1),
        "ln_pre_g": a[L + "tok_ln_pre_g"].reshape(-1, P).T,
        "ln_pre_b": a[L + "tok_ln_pre_b"].reshape(-1, P).T,
        "tok_router": a[L + "tok_router_w"].T,
        "tok_router_b": a[L + "tok_router_b"],
        "tok_w1": np.concatenate([a[L + "tok_experts_w12"], a[L + "tok_shared_w12"][None]]).transpose(0, 2, 1),
        "tok_w2": np.concatenate([a[L + "tok_experts_w3"], a[L + "tok_shared_w3"][None]]).transpose(0, 2, 1),
        "ln_post_g": a[L + "tok_ln_post_g"],
        "ln_post_b": a[L + "tok_ln_post_b"],
        "wq": a[L + "attn_Wq"].T,
        "bq": a[L + "attn_bq"].reshape(NH, HD).T,
        "wk": a[L + "attn_Wk"].T,
        "bk": a[L + "attn_bk"],
        "wv": a[L + "attn_Wv"].T,
        "bv": a[L + "attn_bv"],
        "wo": a[L + "attn_Wo"].T,
        "ffn_router": np.concatenate([a[L + "ffn_gate_w"], a[L + "ffn_shgate_w"][None]]).T,
        "ffn_w1": np.concatenate([w_gate, w_up], axis=2),
        "ffn_w2": np.concatenate([a[L + "ffn_w_down"]] + [shw_d[None, s] for s in halves]),
        "ident": np.eye(P, dtype=np.float32),
    }
    arrays = {k: np.ascontiguousarray(v) for k, v in arrays.items()}
    nc = bacc.Bacc("TRN2", target_bir_lowering=False, num_devices=1)
    args = [nc.dram_tensor(k, v.shape, mybir.dt.from_np(v.dtype), kind="ExternalInput").ap() for k, v in arrays.items()]
    out = nc.dram_tensor("out", (T, D), F32, kind="ExternalOutput").ap()
    build(nc, *args, out)
    r = run_bass_kernel_spmd(nc, [arrays], core_ids=[0])
    return r.results[0]["out"].reshape(B, T // B, D)
```

```python
from contextlib import ExitStack

import concourse.bass as bass
from concourse import mybir

ALU = mybir.AluOpType
ACT = mybir.ActivationFunctionType
AX = mybir.AxisListType
F32 = mybir.dt.float32
F32R = mybir.dt.float32r
I32 = mybir.dt.int32

T = 3000
TP = 125
NT = T // TP
D = 512
P = 128
ST = 4
SN = ST * TP
GROUPS = 2
GS = 3
GT = GS * ST
B = 8
BT = 3
E = 8
NH, NKV, HD = 16, 4, 128
UNIT = 256
NU = (2 * T + E * (UNIT - 1)) // UNIT
BN = 376


class Link:

    def __init__(self, eng, sem):
        self.eng, self.sem, self.n, self.base = eng, sem, 0, 0

    def __call__(self, ins):
        self.n += 1
        ins.then_inc(self.sem, 1)
        self.eng.wait_ge(self.sem, self.base + self.n)

    def start(self, base):
        self.base, self.n = base, 0


class Semaphores:

    def __init__(self, nc):
        self.nc, self.all = nc, []

    def __enter__(self):
        return self

    def new(self, name):
        self.all.append(self.nc.alloc_semaphore(name))
        return self.all[-1]

    def __exit__(self, *error):
        if error[0] is None:
            self.nc.clear_and_free_semaphores(self.all)
            self.nc.all_engine_barrier()


def three(eng, out, w_hi, w_lo, x_hi, x_lo, first, last):
    eng.matmul(out, w_hi, x_hi, start=first, stop=False)
    eng.matmul(out, w_hi, x_lo, start=False, stop=False)
    return eng.matmul(out, w_lo, x_hi, start=False, stop=last)


def rstd_newton(link, dve, ve, rs, tmp):
    link(dve.reciprocal(rs, rs))
    link(dve.tensor_tensor(tmp, rs, rs, ALU.mult))
    link(dve.tensor_tensor(tmp, tmp, ve, ALU.mult))
    link(dve.tensor_scalar(tmp, tmp, -0.5, 1.5, ALU.mult, ALU.add))
    link(dve.tensor_tensor(rs, rs, tmp, ALU.mult))


def moe_phase(nc, x_src, w1, w2, router, router_b, ln_g, ln_b, post_g, post_b, ident_dram, dst, tag,
              routes=None, xn_d=None):
    tok = ln_g is not None
    NC, _, KW = w1.shape[0], w1.shape[1], w1.shape[2]
    K = x_src.shape[1]
    KT = K // P
    H = w2.shape[1]
    HS = [min(P, H - j) for j in range(0, H, P)]
    HT = len(HS)
    NR = router.shape[1]
    EPS_IN = 1e-6 if tok else 1e-5
    NPC = KT + HT
    NB = 2 if K > 512 else 1
    PAIRS = (NC - 2) // 2

    with Semaphores(nc) as sems, ExitStack() as ctx:
        def sb(name, shape, dt=F32):
            return ctx.enter_context(nc.sbuf_tensor(f"{tag}_{name}", shape, dt))

        def sem(name):
            return sems.new(f"{tag}_{name}")

        x_hi = sb("x_hi", [P, KT, GS * SN], F32R)
        x_lo = sb("x_lo", [P, KT, GS * SN], F32R)
        acc = sb("acc", [TP, GT, D])
        xn = sb("xn", [TP, 2, ST, K])
        w1_hi = sb("w1_hi", [P, 2, KT, 2 * H], F32R)
        w1_lo = sb("w1_lo", [P, 2, KT, 2 * H], F32R)
        w2_hi = sb("w2_hi", [P, 2, HT, D], F32R)
        w2_lo = sb("w2_lo", [P, 2, HT, D], F32R)
        w1_raw = sb("w1_raw", [P, KT, 2 * H])
        w2_raw = sb("w2_raw", [P, HT, D])
        sil = sb("sil", [P, 2, SN])
        hid = sb("hid", [P, 2, SN])
        h_hi = sb("h_hi", [P, 2, HT, SN], F32R)
        h_lo = sb("h_lo", [P, 2, HT, SN], F32R)
        ident = sb("ident", [P, P])
        r_raw = sb("r_raw", [P, KT, NR])
        r_hi = sb("r_hi", [P, KT, NR], F32R)
        r_lo = sb("r_lo", [P, KT, NR], F32R)
        rT = sil[0:NR, 0, :]
        st = sb("st", [TP, ST, NB, 6])
        mv = sb("mv", [TP, GT, 2])
        ve = sb("ve", [TP, GT])
        rs = sb("rs", [TP, GT])
        tmp = sb("tmp", [TP, GT])
        lg = sb("lg", [TP, GT, NR])
        pr = sb("pr", [TP, GT, E])
        key = sb("key", [TP, GT, E])
        red = sb("red", [TP, GT])
        top1 = sb("top1", [TP, GT])
        top2 = sb("top2", [TP, GT])
        comb = sb("comb", [TP, GT, NC])
        if tok:
            xf = sb("xf", [P, 2, SN])
            gb = sb("gb", [P, 2, KT])
            post = sb("post", [TP, 2, D])
            rb = sb("rb", [TP, E])
            one = sb("one", [TP, GT, E])
        iota = sb("iota", [TP, E])
        gu = ctx.enter_context(nc.psum_tensor(f"{tag}_gu", [P, 2, 2, 512], F32))
        dn = ctx.enter_context(nc.psum_tensor(f"{tag}_dn", [P, ST, 512], F32))

        const_in = sem("const_in")
        x_in = [sem(f"x_in{s}") for s in range(GS)]
        w_in = sem("w_in")
        stored = sem("stored")
        xn_out = [sem("xn_out0"), sem("xn_out1")]
        zero_done = sem("zero_done")
        iota_done = sem("iota_done")
        var_done = sem("var_done")
        sqrt_done = sem("sqrt_done")
        xn_done = sem("xn_done")
        tr_full = sem("tr_full")
        xf_done = sem("xf_done")
        xhi_done = sem("xhi_done")
        xlo_done = sem("xlo_done")
        rhi_done = sem("rhi_done")
        rlo_done = sem("rlo_done")
        rt_full = sem("rt_full")
        rt_done = sem("rt_done")
        lg_full = sem("lg_full")
        lg_done = sem("lg_done")
        mx_done = sem("mx_done")
        ex_done = sem("ex_done")
        whi_done = sem("whi_done")
        wlo_done = sem("wlo_done")
        gu_full = sem("gu_full")
        sil_done = sem("sil_done")
        h_done = sem("h_done")
        hhi_done = sem("hhi_done")
        hlo_done = sem("hlo_done")
        dn_full = sem("dn_full")
        acc_done = sem("acc_done")
        post_done = sem("post_done")
        psd = sem("psd")
        pve = sem("pve")
        chain = sem("chain")

        def chunks(eng, g, body):
            q0 = g * NC
            body(q0, 0, q0 % 2, True, False)
            if PAIRS:
                with eng.Fori(0, PAIRS) as i:
                    for j in (1, 2):
                        body(i * 2 + (q0 + j), i * 2 + j, (q0 + j) % 2, False, False)
            for c in range(2 * PAIRS + 1, NC):
                body(q0 + c, c, (q0 + c) % 2, False, g == GROUPS - 1 and c == NC - 1)

        def raw_pieces(par):
            out = [(w1_raw[:, k, :], w1_hi[:, par, k, :], w1_lo[:, par, k, :]) for k in range(KT)]
            out += [(w2_raw[0:n, j, :], w2_hi[0:n, par, j, :], w2_lo[0:n, par, j, :]) for j, n in enumerate(HS)]
            return out

        NW = 2 if H % P == 0 else 3

        block = ctx.enter_context(nc.Block())

        @block.sync
        def _(sp):
            def load(c):
                sp.dma_start(w1_raw[:], w1[c if isinstance(c, int) else bass.ds(c, 1)].rearrange(
                    "(k p) n -> p k n" if isinstance(c, int) else "o (k p) n -> p (o k) n", p=P)).then_inc(w_in, 16)
                w2c = w2[c] if isinstance(c, int) else w2[bass.ds(c, 1)].rearrange("o h n -> (o h) n")
                full = H // P
                sp.dma_start(w2_raw[:, 0:full, :], w2c[0:full * P, :].rearrange("(j p) n -> p j n", p=P)).then_inc(w_in, 16)
                if H % P:
                    sp.dma_start(w2_raw[0:H % P, full, :], w2c[full * P:H, :]).then_inc(w_in, 16)

            load(0)
            for g in range(GROUPS):
                def body(q, c, par, first, last):
                    if last:
                        return
                    sp.wait_ge(wlo_done, (q + 1) * NPC)
                    load(0 if isinstance(c, int) and c == NC - 1 else c + 1)
                chunks(sp, g, body)

        @block.gpsimd
        def _(pool):
            pool.dma_start(ident[:], ident_dram).then_inc(const_in, 16)
            pool.dma_start(r_raw[:], router.rearrange("(k p) n -> p k n", p=P)).then_inc(const_in, 16)
            if tok:
                pool.dma_start(gb[:, 0, :], ln_g).then_inc(const_in, 16)
                pool.dma_start(gb[:, 1, :], ln_b).then_inc(const_in, 16)
                pool.dma_start(post[:, 0, :], post_g.partition_broadcast(TP)).then_inc(const_in, 16)
                pool.dma_start(post[:, 1, :], post_b.partition_broadcast(TP)).then_inc(const_in, 16)
                pool.dma_start(rb[:], router_b.partition_broadcast(TP)).then_inc(const_in, 16)
            nc.gpsimd.iota(iota[:], pattern=[[1, E]], base=0, channel_multiplier=0,
                           allow_small_or_imprecise_dtypes=True).then_inc(iota_done, 1)
            for g in range(GROUPS):
                if tok:
                    if g:
                        pool.wait_ge(stored, 16 * g)
                    nc.gpsimd.memset(acc[:], 0.0).then_inc(zero_done, 1)
                for s in range(GS):
                    u = g * GS + s
                    rows = x_src[u * SN:(u + 1) * SN, :].rearrange("(t p) k -> p t k", p=TP)
                    if tok:
                        if u >= 2:
                            pool.wait_ge(tr_full, (u - 1) * KT)
                        pool.dma_start(xn[:, u % 2], rows).then_inc(x_in[s], 16)
                    else:
                        if g:
                            pool.wait_ge(stored, 16 * g)
                        pool.dma_start(acc[:, s * ST:(s + 1) * ST, :], rows).then_inc(x_in[s], 16)
                if not tok:
                    for s in range(GS):
                        u = g * GS + s
                        pool.wait_ge(xn_done, (u + 1) * ST)
                        pool.dma_start(xn_d[u * SN:(u + 1) * SN, :].rearrange("(t p) k -> p t k", p=TP),
                                       xn[:, u % 2]).then_inc(xn_out[u % 2], 16)
                pool.wait_ge(post_done, g + 1)
                pool.dma_start(dst[g * GT * TP:(g + 1) * GT * TP, :].rearrange("(t p) d -> p t d", p=TP),
                               acc[:]).then_inc(stored, 16)
            pool.wait_ge(stored, 16 * GROUPS)
            if not tok:
                for par in range(2):
                    pool.wait_ge(xn_out[par], 16 * (GROUPS * GS // 2))

        NCONST = 16 * (7 if tok else 2)

        @block.tensor
        def _(pe):
            pe.wait_ge(const_in, NCONST)
            pe.wait_ge(rlo_done, 1)
            for g in range(GROUPS):
                if g:
                    pe.wait_ge(acc_done, g * NC * GS * ST + ST)
                for s in range(GS):
                    u = g * GS + s
                    pe.wait_ge(xn_done, (u + 1) * ST)
                    for k in range(KT):
                        n = u * KT + k
                        if n >= 2:
                            pe.wait_ge(xf_done if tok else xlo_done, n - 1)
                        for t in range(ST):
                            mm = pe.transpose(dn[:, n % 2, t * TP:(t + 1) * TP],
                                              xn[:, u % 2, t, k * P:(k + 1) * P], ident[0:TP, 0:TP])
                        mm.then_inc(tr_full, 1)
                    pe.wait_ge(xlo_done, (u + 1) * KT)
                    if u:
                        pe.wait_ge(rt_done, u)
                    for k in range(KT):
                        cols = slice(s * SN, (s + 1) * SN)
                        mm = three(pe, dn[0:NR, 2, 0:SN], r_hi[:, k, :], r_lo[:, k, :],
                                   x_hi[:, k, cols], x_lo[:, k, cols], k == 0, k == KT - 1)
                    mm.then_inc(rt_full, 1)
                    pe.wait_ge(rt_done, u + 1)
                    if u:
                        pe.wait_ge(lg_done, u)
                    for t in range(ST):
                        mm = pe.transpose(dn[0:TP, 3, t * NR:(t + 1) * NR], rT[:, t * TP:(t + 1) * TP],
                                          ident[0:NR, 0:NR])
                    mm.then_inc(lg_full, 1)
                pe.wait_ge(lg_done, (g + 1) * GS)

                def down(n, par, npar, s):
                    for t in range(ST):
                        pe.wait_ge(acc_done, n * ST + (t + 1))
                        for j, hs in enumerate(HS):
                            if t == 0:
                                pe.wait_ge(hlo_done, n * HT + (j + 3))
                            tk = slice(t * TP, (t + 1) * TP)
                            mm = three(pe, dn[0:TP, t, :], h_hi[0:hs, npar, j, tk], h_lo[0:hs, npar, j, tk],
                                         w2_hi[0:hs, par, j, :], w2_lo[0:hs, par, j, :], j == 0, j == HT - 1)
                        mm.then_inc(dn_full, 1)

                def body(q, c, par, first, last):
                    pe.wait_ge(wlo_done, (q + 1) * NPC)
                    for s in range(GS):
                        n, npar = q * GS + s, (par + s) % 2
                        cols = slice(s * SN, (s + 1) * SN)
                        for j, hs in enumerate(HS):
                            m, mpar = n * HT + j, (npar + j) % 2 if HT > 1 else npar
                            pe.wait_ge(h_done, m + 1)
                            for half in range(2):
                                for k in range(KT):
                                    wc = slice(half * H + j * P, half * H + j * P + hs)
                                    mm = three(pe, gu[0:hs, mpar, half, 0:SN], w1_hi[:, par, k, wc],
                                               w1_lo[:, par, k, wc], x_hi[:, k, cols], x_lo[:, k, cols],
                                               k == 0, k == KT - 1)
                            mm.then_inc(gu_full, 1)
                        if not (first and s == 0):
                            down(n - 1, par if s else 1 - par, 1 - npar, s)
                chunks(pe, g, body)
                qe = (g + 1) * NC - 1
                down(qe * GS + GS - 1, qe % 2, (qe + GS - 1) % 2, GS - 1)

        @block.scalar
        def _(act):
            act.wait_ge(const_in, NCONST)
            nc.scalar.activation(r_hi[:], r_raw[:], ACT.Copy).then_inc(rhi_done, 1)

            def split(q, par):
                act.wait_ge(w_in, (q + 1) * (16 * NW))
                for raw, hi, _ in raw_pieces(par):
                    nc.scalar.activation(hi, raw, ACT.Copy).then_inc(whi_done, 1)

            for g in range(GROUPS):
                for s in range(GS):
                    u = g * GS + s
                    act.wait_ge(var_done, u + 1)
                    nc.scalar.activation(rs[:, s * ST:(s + 1) * ST], ve[:, s * ST:(s + 1) * ST],
                                         ACT.Sqrt).then_inc(sqrt_done, 1)
                    for k in range(KT):
                        n = u * KT + k
                        cols = slice(s * SN, (s + 1) * SN)
                        act.wait_ge(tr_full, n + 1)
                        if tok:
                            if n >= 2:
                                act.wait_ge(xlo_done, n - 1)
                            nc.scalar.activation(xf[:, n % 2, :], dn[:, n % 2, 0:SN], ACT.Identity,
                                                 bias=gb[:, 1, k:k + 1], scale=gb[:, 0, k:k + 1]).then_inc(xf_done, 1)
                            act.wait_ge(xf_done, n + 1)
                            nc.scalar.activation(x_hi[:, k, cols], xf[:, n % 2, :], ACT.Copy).then_inc(xhi_done, 1)
                        else:
                            nc.scalar.activation(x_hi[:, k, cols], dn[:, n % 2, 0:SN], ACT.Copy).then_inc(xhi_done, 1)
                    act.wait_ge(rt_full, u + 1)
                    if u:
                        act.wait_ge(lg_full, u)
                    nc.scalar.activation(rT[:], dn[0:NR, 2, 0:SN], ACT.Copy).then_inc(rt_done, 1)
                if g == 0:
                    split(0, 0)
                act.wait_ge(mx_done, g + 1)
                nc.scalar.activation(pr[:], key[:], ACT.Exp).then_inc(ex_done, 1)
                if not tok:
                    act.wait_ge(lg_done, (g + 1) * GS)
                    nc.scalar.activation(comb[:, :, 0:1], lg[:, :, E:E + 1], ACT.Sigmoid).then_inc(ex_done, 1)

                def body(q, c, par, first, last):
                    for s in range(GS):
                        n, npar = q * GS + s, (par + s) % 2
                        for j, hs in enumerate(HS):
                            m, mpar = n * HT + j, (npar + j) % 2 if HT > 1 else npar
                            act.wait_ge(gu_full, m + 1)
                            act.wait_ge(h_done, m + 1)
                            nc.scalar.activation(sil[0:hs, mpar, :], gu[0:hs, mpar, 0, 0:SN],
                                                 ACT.Silu).then_inc(sil_done, 1)
                            act.wait_ge(h_done, m + 3)
                            if j == 0 and not (first and g == 0 and s < 2):
                                act.wait_ge(dn_full, (n - 1) * ST)
                            nc.scalar.activation(h_hi[0:hs, npar, j, :], hid[0:hs, mpar, :],
                                                 ACT.Copy).then_inc(hhi_done, 1)
                        if s == 0 and not last:
                            if not (first and g == 0):
                                act.wait_ge(dn_full, q * (GS * ST))
                            split(q + 1, 1 - par)
                chunks(act, g, body)
                if tok:
                    act.wait_ge(pve, g + 1)
                    nc.scalar.activation(rs[:], ve[:], ACT.Sqrt).then_inc(psd, 1)

        @block.vector
        def _(dve):
            link = Link(dve, chain)
            dve.sem_inc(h_done, 2)
            dve.sem_inc(hlo_done, 2)
            dve.sem_inc(acc_done, ST)
            if tok:
                link(nc.vector.memset(comb[:, :, E:NC], 1.0))
            dve.wait_ge(rhi_done, 1)
            nc.vector.tensor_tensor(r_lo[:], r_raw[:], r_hi[:].bitcast(F32), ALU.subtract).then_inc(rlo_done, 1)

            def split(q, par):
                for i, (raw, hi, lo) in enumerate(raw_pieces(par)):
                    dve.wait_ge(whi_done, q * NPC + (i + 1))
                    nc.vector.tensor_tensor(lo, raw, hi.bitcast(F32), ALU.subtract).then_inc(wlo_done, 1)

            def stats(src, t, slot, nb):
                for b in range(nb):
                    w = src.shape[-1] // nb
                    link(nc.vector.bn_stats(st[:, t, b, :], src[:, b * w:(b + 1) * w]))
                link(nc.vector.bn_aggr(mv[:, slot, :], st[:, t, 0:nb, :]))

            def bc(ap):
                return ap.unsqueeze(2).broadcast_to((TP, GT, E))

            for g in range(GROUPS):
                for s in range(GS):
                    u = g * GS + s
                    dve.wait_ge(x_in[s], 16 * (g + 1))
                    src = (lambda t: xn[:, u % 2, t, :]) if tok else (lambda t: acc[:, s * ST + t, :])
                    tl = slice(s * ST, (s + 1) * ST)
                    for t in range(ST):
                        stats(src(t), t, s * ST + t, NB)
                    nc.vector.tensor_scalar(ve[:, tl], mv[:, tl, 1], EPS_IN, None, ALU.add).then_inc(var_done, 1)
                    dve.wait_ge(sqrt_done, u + 1)
                    rstd_newton(link, nc.vector, ve[:, tl], rs[:, tl], tmp[:, tl])
                    if u >= 2:
                        dve.wait_ge(tr_full, (u - 1) * KT)
                        if not tok:
                            dve.wait_ge(xn_out[u % 2], 16 * (u // 2))
                    for t in range(ST):
                        i = s * ST + t
                        nc.vector.tensor_scalar(xn[:, u % 2, t, :], src(t), mv[:, i, 0:1], rs[:, i:i + 1],
                                                ALU.subtract, ALU.mult).then_inc(xn_done, 1)
                    for k in range(KT):
                        n = u * KT + k
                        cols = slice(s * SN, (s + 1) * SN)
                        dve.wait_ge(xhi_done, n + 1)
                        full = xf[:, n % 2, :] if tok else dn[:, n % 2, 0:SN]
                        nc.vector.tensor_tensor(x_lo[:, k, cols], full, x_hi[:, k, cols].bitcast(F32),
                                                ALU.subtract).then_inc(xlo_done, 1)
                    dve.wait_ge(lg_full, u + 1)
                    lp = dn[0:TP, 3, 0:ST * NR].rearrange("p (t e) -> p t e", e=NR)
                    if tok:
                        nc.vector.tensor_tensor(lg[:, tl, :], lp, rb[:].unsqueeze(1).broadcast_to((TP, ST, E)),
                                                ALU.add).then_inc(lg_done, 1)
                    else:
                        nc.vector.tensor_copy(lg[:, tl, :], lp).then_inc(lg_done, 1)

                if g == 0:
                    split(0, 0)
                dve.wait_ge(lg_done, (g + 1) * GS)
                link(nc.vector.tensor_reduce(red[:], lg[:, :, 0:E], AX.X, ALU.max))
                nc.vector.tensor_tensor(key[:], lg[:, :, 0:E], bc(red[:]), ALU.subtract).then_inc(mx_done, 1)
                dve.wait_ge(ex_done, (g + 1) * (1 if tok else 2))
                dve.wait_ge(iota_done, 1)
                link(nc.vector.tensor_reduce(red[:], pr[:], AX.X, ALU.add))
                link(nc.vector.reciprocal(red[:], red[:]))
                link(nc.vector.tensor_tensor(pr[:], pr[:], bc(red[:]), ALU.mult))
                if tok:
                    link(nc.vector.memset(comb[:, :, 0:E], 0.0))
                ib = iota[:].unsqueeze(1).broadcast_to((TP, GT, E))
                for r, top in enumerate((top1, top2)):
                    hot = one[:] if tok else routes["hot"][:, r, g * GT:(g + 1) * GT, :]
                    link(nc.vector.tensor_reduce(top[:], pr[:], AX.X, ALU.max))
                    link(nc.vector.tensor_tensor(key[:], pr[:], bc(top[:]), ALU.is_lt))
                    link(nc.vector.tensor_scalar(key[:], key[:], float(E), None, ALU.mult))
                    link(nc.vector.tensor_tensor(key[:], key[:], ib, ALU.add))
                    link(nc.vector.tensor_reduce(red[:], key[:], AX.X, ALU.min))
                    link(nc.vector.tensor_tensor(hot, ib, bc(red[:]), ALU.is_equal))
                    if tok:
                        link(nc.vector.tensor_tensor(key[:], hot, bc(top[:]), ALU.mult))
                        link(nc.vector.tensor_tensor(comb[:, :, 0:E], comb[:, :, 0:E], key[:], ALU.add))
                    link(nc.vector.tensor_scalar(key[:], hot, -2.0, None, ALU.mult))
                    link(nc.vector.tensor_tensor(pr[:], pr[:], key[:], ALU.add))
                link(nc.vector.tensor_tensor(red[:], top1[:], top2[:], ALU.add))
                if tok:
                    link(nc.vector.tensor_scalar(red[:], red[:], 1e-20, None, ALU.add))
                link(nc.vector.reciprocal(red[:], red[:]))
                if tok:
                    link(nc.vector.tensor_tensor(comb[:, :, 0:E], comb[:, :, 0:E], bc(red[:]), ALU.mult))
                else:
                    for r, top in enumerate((top1, top2)):
                        link(nc.vector.tensor_tensor(routes["weight"][:, r, g * GT:(g + 1) * GT], top[:], red[:],
                                                     ALU.mult))
                    for c in range(1, NC):
                        link(nc.vector.tensor_copy(comb[:, :, c:c + 1], comb[:, :, 0:1]))
                if tok:
                    dve.wait_ge(zero_done, g + 1)

                def add(n, c, s):
                    for t in range(ST):
                        i = s * ST + t
                        dve.wait_ge(dn_full, n * ST + (t + 1))
                        w = comb[:, i, c:c + 1] if isinstance(c, int) else comb[:, i, bass.ds(c, 1)]
                        if not (isinstance(n, int) and n < GS):
                            dve.wait_ge(acc_done, (n - GS) * ST + (t + 1 + ST))
                        nc.vector.scalar_tensor_tensor(out=acc[:, i, :], in0=dn[0:TP, t, :], scalar=w,
                                                       in1=acc[:, i, :], op0=ALU.mult,
                                                       op1=ALU.add).then_inc(acc_done, 1)

                def body(q, c, par, first, last):
                    for s in range(GS):
                        n, npar = q * GS + s, (par + s) % 2
                        for j, hs in enumerate(HS):
                            m, mpar = n * HT + j, (npar + j) % 2 if HT > 1 else npar
                            dve.wait_ge(sil_done, m + 1)
                            dve.wait_ge(hlo_done, m + 1)
                            nc.vector.tensor_tensor(hid[0:hs, mpar, :], sil[0:hs, mpar, :],
                                                    gu[0:hs, mpar, 1, 0:SN], ALU.mult).then_inc(h_done, 1)
                            dve.wait_ge(hhi_done, m + 1)
                            nc.vector.tensor_tensor(h_lo[0:hs, npar, j, :], hid[0:hs, mpar, :],
                                                    h_hi[0:hs, npar, j, :].bitcast(F32),
                                                    ALU.subtract).then_inc(hlo_done, 1)
                        if s == 0 and not last:
                            split(q + 1, 1 - par)
                        if not (first and s == 0):
                            add(n - 1, c if s else c - 1, (s - 1) % GS)
                chunks(dve, g, body)
                qe = (g + 1) * NC - 1
                add(qe * GS + GS - 1, NC - 1, GS - 1)

                if tok:
                    dve.wait_ge(acc_done, (g + 1) * NC * GS * ST + ST)
                    for i in range(GT):
                        stats(acc[:, i, :], i % ST, i, 1)
                    nc.vector.tensor_scalar(ve[:], mv[:, :, 1], 1e-6, None, ALU.add).then_inc(pve, 1)
                    dve.wait_ge(psd, g + 1)
                    rstd_newton(link, nc.vector, ve[:], rs[:], tmp[:])
                    for i in range(GT):
                        link(nc.vector.tensor_scalar(acc[:, i, :], acc[:, i, :], mv[:, i, 0:1], rs[:, i:i + 1],
                                                     ALU.subtract, ALU.mult))
                        link(nc.vector.tensor_tensor(acc[:, i, :], acc[:, i, :], post[:, 0, :], ALU.mult))
                        link(nc.vector.tensor_tensor(acc[:, i, :], acc[:, i, :], post[:, 1, :], ALU.add))
                    dve.sem_inc(post_done, 1)
                else:
                    dve.wait_ge(acc_done, (g + 1) * NC * GS * ST + ST)
                    dve.sem_inc(post_done, 1)



def kv_phase(nc, h_src, wk, wv, bk, bv, ident_dram, xT_hi_d, xT_lo_d, kv_hi_d, kv_lo_d):
    KT = D // P
    VW = HD + 2
    with Semaphores(nc) as sems, ExitStack() as ctx:
        def sb(name, shape, dt=F32):
            return ctx.enter_context(nc.sbuf_tensor(f"kv_{name}", shape, dt))

        def sem(name):
            return sems.new(f"kv_{name}")

        ident = sb("ident", [P, P])
        w_raw = sb("w_raw", [P, 2, KT, D])
        w_hi = sb("w_hi", [P, 2, KT, D], F32R)
        w_lo = sb("w_lo", [P, 2, KT, D], F32R)
        bias = sb("bias", [TP, 2, D])
        h_in = sb("h_in", [TP, 2, BT, D])
        xn = sb("xn", [TP, 2, BT, D])
        x_hi = sb("x_hi", [P, 2, KT, BN], F32R)
        x_lo = sb("x_lo", [P, 2, KT, BN], F32R)
        kf = sb("kf", [TP, 2, D])
        ex = sb("ex", [TP, 2, D])
        vf = sb("vf", [TP, 2, D])
        k_hi = sb("k_hi", [TP, 2, BT, D], F32R)
        k_lo = sb("k_lo", [TP, 2, BT, D], F32R)
        v_hi = sb("v_hi", [TP, 2, BT, NKV, VW], F32R)
        v_lo = sb("v_lo", [TP, 2, BT, NKV, VW], F32R)
        kv_hi = sb("kv_hi", [P, 2, NKV, VW], F32R)
        kv_lo = sb("kv_lo", [P, 2, NKV, VW], F32R)
        st = sb("st", [TP, BT, 6])
        fence = sb("fence", [1, 2])
        mv = sb("mv", [TP, BT, 2])
        ve = sb("ve", [TP, BT])
        rs = sb("rs", [TP, BT])
        tmp = sb("tmp", [TP, BT])
        tp = ctx.enter_context(nc.psum_tensor("kv_tp", [P, 2, 512], F32))
        kp = ctx.enter_context(nc.psum_tensor("kv_kp", [P, 2, 2, 512], F32))
        kvp = ctx.enter_context(nc.psum_tensor("kv_kvp", [P, 2, 512], F32))

        const_in = sem("const_in")
        h_loaded = [sem("h_in0"), sem("h_in1")]
        x_out = [sem("x_out0"), sem("x_out1")]
        kv_out = [sem("kv_out0"), sem("kv_out1")]
        pads = sem("pads")
        whi_done = sem("whi_done")
        wlo_done = sem("wlo_done")
        var_done = sem("var_done")
        sqrt_done = sem("sqrt_done")
        xn_done = sem("xn_done")
        tr_full = sem("tr_full")
        xhi_done = sem("xhi_done")
        xlo_done = sem("xlo_done")
        k_full = sem("k_full")
        v_full = sem("v_full")
        kb_done = sem("kb_done")
        mn_done = sem("mn_done")
        ex_done = sem("ex_done")
        sk_done = sem("sk_done")
        vb_done = sem("vb_done")
        khi_done = sem("khi_done")
        vhi_done = sem("vhi_done")
        klo_done = sem("klo_done")
        vlo_done = sem("vlo_done")
        kv_full = sem("kv_full")
        kvhi_done = sem("kvhi_done")
        kvlo_done = sem("kvlo_done")
        bn_done = sem("bn_done")
        aggr_done = sem("aggr_done")
        chain = sem("chain")

        def sequences(eng, body):
            for b in range(2):
                body(b, b, True)
            with eng.Fori(2, B - 1, 2) as i:
                for par in range(2):
                    body(i + par, par, False)

        def at(d, b):
            return d[b] if isinstance(b, int) else d[bass.ds(b, 1)].squeeze(0)

        block = ctx.enter_context(nc.Block())

        def rows(b):
            r = h_src[b * (BT * TP):(b + 1) * (BT * TP), :] if isinstance(b, int) \
                else h_src[bass.ds(b * (BT * TP), BT * TP), :]
            return r.rearrange("(t p) d -> p t d", p=TP)

        @block.sync
        def _(sp):
            sp.dma_start(h_in[:, 0], rows(0)).then_inc(h_loaded[0], 16)
            sp.dma_start(ident[:], ident_dram).then_inc(const_in, 16)
            sp.dma_start(w_raw[:, 0], wk.rearrange("(k p) n -> p k n", p=P)).then_inc(const_in, 16)
            sp.dma_start(w_raw[:, 1], wv.rearrange("(k p) n -> p k n", p=P)).then_inc(const_in, 16)
            sp.dma_start(bias[:, 0, :], bk.partition_broadcast(TP)).then_inc(const_in, 16)
            sp.dma_start(bias[:, 1, :], bv.partition_broadcast(TP)).then_inc(const_in, 16)
            sp.dma_start(h_in[:, 1], rows(1)).then_inc(h_loaded[1], 16)
            with sp.Fori(2, B - 1, 2) as i:
                for par in range(2):
                    sp.wait_ge(xn_done, (i + (par - 1)) * BT)
                    sp.dma_start(h_in[:, par], rows(i + par)).then_inc(h_loaded[par], 16)

        @block.gpsimd
        def _(pool):
            nc.gpsimd.memset(x_hi[:, :, :, BT * TP:BN].bitcast(F32), 0.0).then_inc(pads, 1)
            nc.gpsimd.memset(x_lo[:, :, :, BT * TP:BN].bitcast(F32), 0.0).then_inc(pads, 1)
            nc.gpsimd.memset(v_hi[:, :, :, :, HD:VW].bitcast(F32), 1.0).then_inc(pads, 1)
            nc.gpsimd.memset(v_lo[:, :, :, :, HD:VW].bitcast(F32), 0.0).then_inc(pads, 1)
            pool.wait_ge(pads, 4)

            def body(b, par, first):
                pool.wait_ge(xlo_done, (b + 1) * KT)
                pool.dma_start(at(xT_hi_d, b), x_hi[:, par].bitcast(F32)).then_inc(x_out[par], 16)
                pool.dma_start(at(xT_lo_d, b), x_lo[:, par].bitcast(F32)).then_inc(x_out[par], 16)
                pool.wait_ge(kvlo_done, (b + 1) * 2)
                pool.dma_start(at(kv_hi_d, b), kv_hi[:, par].bitcast(F32)).then_inc(kv_out[par], 16)
                pool.dma_start(at(kv_lo_d, b), kv_lo[:, par].bitcast(F32)).then_inc(kv_out[par], 16)
            sequences(pool, body)
            for par in range(2):
                pool.wait_ge(x_out[par], 16 * B)
                pool.wait_ge(kv_out[par], 16 * B)

        @block.tensor
        def _(pe):
            pe.wait_ge(const_in, 80)
            pe.wait_ge(pads, 4)
            pe.wait_ge(wlo_done, 2)

            def project(b, par, first):
                for k in range(KT):
                    pe.wait_ge(xn_done, (b + 1) * BT)
                    if not (first and b == 0 and k < 2):
                        pe.wait_ge(xlo_done, b * KT + (k - 1))
                    for i in range(BT):
                        mm = pe.transpose(tp[:, k % 2, i * TP:(i + 1) * TP], xn[:, par, i, k * P:(k + 1) * P],
                                          ident[0:TP, 0:TP])
                    mm.then_inc(tr_full, 1)
                pe.wait_ge(xlo_done, (b + 1) * KT)
                for i in range(BT):
                    n = b * BT + i
                    bank = (par + i) % 2
                    for j, free, full in ((0, kb_done, k_full), (1, vb_done, v_full)):
                        if not (first and b * BT + i < 2):
                            pe.wait_ge(free, n - 1)
                        for k in range(KT):
                            tk = slice(i * TP, (i + 1) * TP)
                            mm = three(pe, kp[0:TP, bank, j, :], x_hi[:, par, k, tk], x_lo[:, par, k, tk],
                                       w_hi[:, j, k, :], w_lo[:, j, k, :], k == 0, k == KT - 1)
                        mm.then_inc(full, 1)

            def sums(b, par, first):
                pe.wait_ge(klo_done, (b + 1) * BT)
                pe.wait_ge(vlo_done, (b + 1) * BT)
                for g in range(NKV):
                    if g % 2 == 0 and not (first and b == 0):
                        pe.wait_ge(kvlo_done, b * 2 + (g // 2 - 1))
                    for i in range(BT):
                        hd = slice(g * HD, (g + 1) * HD)
                        mm = three(pe, kvp[:, g // 2, (g % 2) * VW:(g % 2 + 1) * VW], k_hi[:, par, i, hd],
                                   k_lo[:, par, i, hd], v_hi[:, par, i, g, :], v_lo[:, par, i, g, :],
                                   i == 0, i == BT - 1)
                    if g % 2:
                        mm.then_inc(kv_full, 1)

            project(0, 0, True)
            project(1, 1, True)
            sums(0, 0, True)
            with pe.Fori(2, B - 1, 2) as i:
                for par in range(2):
                    project(i + par, par, False)
                    sums(i + (par - 1), 1 - par, False)
            sums(B - 1, (B - 1) % 2, False)

        @block.scalar
        def _(act):
            act.wait_ge(const_in, 80)
            act.wait_ge(pads, 4)
            for j in range(2):
                nc.scalar.activation(w_hi[:, j], w_raw[:, j], ACT.Copy).then_inc(whi_done, 1)

            def project(b, par, first):
                act.wait_ge(var_done, b + 1)
                nc.scalar.activation(rs[:], ve[:], ACT.Sqrt).then_inc(sqrt_done, 1)
                if not first:
                    act.wait_ge(x_out[par], (b - par) * 16)
                    act.wait_ge(v_full, (b - 1) * BT)
                for k in range(KT):
                    act.wait_ge(tr_full, b * KT + (k + 1))
                    nc.scalar.activation(x_hi[:, par, k, 0:BT * TP], tp[:, k % 2, 0:BT * TP],
                                         ACT.Copy).then_inc(xhi_done, 1)
                if not first:
                    act.wait_ge(kv_full, (b - 1) * 2)
                for i in range(BT):
                    n, z = b * BT + i, (par + i) % 2
                    act.wait_ge(mn_done, n + 1)
                    nc.scalar.activation(ex[:, z, :], ex[:, z, :], ACT.Exp).then_inc(ex_done, 1)
                    act.wait_ge(sk_done, n + 1)
                    nc.scalar.activation(k_hi[:, par, i, :], kf[:, z, :], ACT.Copy).then_inc(khi_done, 1)
                    act.wait_ge(vb_done, n + 1)
                    nc.scalar.activation(v_hi[:, par, i, :, 0:HD], vf[:, z, :].rearrange("p (g d) -> p g d", d=HD),
                                         ACT.Copy).then_inc(vhi_done, 1)

            def sums(b, par, first):
                if not first:
                    act.wait_ge(kv_out[par], (b - par) * 16)
                for c in range(2):
                    act.wait_ge(kv_full, b * 2 + (c + 1))
                    nc.scalar.activation(kv_hi[:, par, 2 * c:2 * c + 2, :],
                                         kvp[:, c, 0:2 * VW].rearrange("p (g d) -> p g d", d=VW),
                                         ACT.Copy).then_inc(kvhi_done, 1)

            project(0, 0, True)
            project(1, 1, True)
            sums(0, 0, True)
            project(2, 0, False)
            sums(1, 1, True)
            project(3, 1, False)
            sums(2, 0, False)
            with act.Fori(4, B - 1, 2) as i:
                for par in range(2):
                    project(i + par, par, False)
                    sums(i + (par - 1), 1 - par, False)
            sums(B - 1, (B - 1) % 2, False)

        @block.vector
        def _(dve):
            link = Link(dve, chain)
            for j in range(2):
                dve.wait_ge(whi_done, j + 1)
                nc.vector.tensor_tensor(w_lo[:, j], w_raw[:, j], w_hi[:, j].bitcast(F32),
                                        ALU.subtract).then_inc(wlo_done, 1)
            PER = 5

            def project(b, par, first):
                link.start(b * PER)
                dve.wait_ge(h_loaded[par], (b - par) * 8 + 16)
                for i in range(BT):
                    nc.vector.bn_stats(st[:, i, :], h_in[:, par, i, :]).then_inc(bn_done, 1)
                for i in range(BT):
                    if i == 0:
                        dve.wait_ge(bn_done, (b + 1) * BT)
                        nc.vector.memset(fence[:, par:par + 1], 0.0)
                    nc.vector.bn_aggr(mv[:, i, :], st[:, i, :]).then_inc(aggr_done, 1)
                dve.wait_ge(aggr_done, (b + 1) * BT)
                nc.vector.tensor_scalar(ve[:], mv[:, :, 1], 1e-5, None, ALU.add).then_inc(var_done, 1)
                dve.wait_ge(sqrt_done, b + 1)
                rstd_newton(link, nc.vector, ve[:], rs[:], tmp[:])
                if not first:
                    dve.wait_ge(tr_full, (b - 1) * KT)
                for i in range(BT):
                    nc.vector.tensor_scalar(xn[:, par, i, :], h_in[:, par, i, :], mv[:, i, 0:1], rs[:, i:i + 1],
                                            ALU.subtract, ALU.mult).then_inc(xn_done, 1)
                for k in range(KT):
                    dve.wait_ge(xhi_done, b * KT + (k + 1))
                    nc.vector.tensor_tensor(x_lo[:, par, k, 0:BT * TP], tp[:, k % 2, 0:BT * TP],
                                            x_hi[:, par, k, 0:BT * TP].bitcast(F32),
                                            ALU.subtract).then_inc(xlo_done, 1)
                for i in range(BT):
                    n, z = b * BT + i, (par + i) % 2
                    early = first and b * BT + i < 2
                    dve.wait_ge(k_full, n + 1)
                    if not early:
                        dve.wait_ge(klo_done, n - 1)
                    nc.vector.tensor_tensor(kf[:, z, :], kp[0:TP, z, 0, :], bias[:, 0, :], ALU.add).then_inc(kb_done, 1)
                    dve.wait_ge(kb_done, n + 1)
                    nc.vector.tensor_scalar(ex[:, z, :], kf[:, z, :], 0.0, None, ALU.min).then_inc(mn_done, 1)
                    dve.wait_ge(v_full, n + 1)
                    if not early:
                        dve.wait_ge(vlo_done, n - 1)
                    nc.vector.tensor_tensor(vf[:, z, :], kp[0:TP, z, 1, :], bias[:, 1, :], ALU.add).then_inc(vb_done, 1)
                    dve.wait_ge(ex_done, n + 1)
                    nc.vector.scalar_tensor_tensor(out=kf[:, z, :], in0=kf[:, z, :], scalar=0.0, in1=ex[:, z, :],
                                                   op0=ALU.max, op1=ALU.add).then_inc(sk_done, 1)
                    dve.wait_ge(khi_done, n + 1)
                    nc.vector.tensor_tensor(k_lo[:, par, i, :], kf[:, z, :], k_hi[:, par, i, :].bitcast(F32),
                                            ALU.subtract).then_inc(klo_done, 1)
                    dve.wait_ge(vhi_done, n + 1)
                    nc.vector.tensor_tensor(v_lo[:, par, i, :, 0:HD], vf[:, z, :].rearrange("p (g d) -> p g d", d=HD),
                                            v_hi[:, par, i, :, 0:HD].bitcast(F32),
                                            ALU.subtract).then_inc(vlo_done, 1)
                assert link.n == PER

            def sums(b, par, first):
                for c in range(2):
                    dve.wait_ge(kvhi_done, b * 2 + (c + 1))
                    nc.vector.tensor_tensor(kv_lo[:, par, 2 * c:2 * c + 2, :],
                                            kvp[:, c, 0:2 * VW].rearrange("p (g d) -> p g d", d=VW),
                                            kv_hi[:, par, 2 * c:2 * c + 2, :].bitcast(F32),
                                            ALU.subtract).then_inc(kvlo_done, 1)

            project(0, 0, True)
            project(1, 1, True)
            sums(0, 0, True)
            with dve.Fori(2, B - 1, 2) as i:
                for par in range(2):
                    project(i + par, par, False)
                    sums(i + (par - 1), 1 - par, False)
            sums(B - 1, (B - 1) % 2, False)


def query_phase(nc, h_src, wq, wo, bq, ident_dram, xT_hi_d, xT_lo_d, kv_hi_d, kv_lo_d, dst):
    KT = D // P
    VW = HD + 2
    PIECE = 1024
    NPQ = KT * NH * HD // PIECE
    with Semaphores(nc) as sems, ExitStack() as ctx:
        def sb(name, shape, dt=F32):
            return ctx.enter_context(nc.sbuf_tensor(f"q_{name}", shape, dt))

        def sem(name):
            return sems.new(f"q_{name}")

        ident = sb("ident", [P, P])
        raw = sb("raw", [P, 2, PIECE])
        wq_hi = sb("wq_hi", [P, KT, NH * HD], F32R)
        wq_lo = sb("wq_lo", [P, KT, NH * HD], F32R)
        wo_hi = sb("wo_hi", [P, NH, D], F32R)
        wo_lo = sb("wo_lo", [P, NH, D], F32R)
        bias = sb("bias", [P, NH])
        x_hi = sb("x_hi", [P, 2, KT, BN], F32R)
        x_lo = sb("x_lo", [P, 2, KT, BN], F32R)
        kv_hi = sb("kv_hi", [P, 2, NKV, VW], F32R)
        kv_lo = sb("kv_lo", [P, 2, NKV, VW], F32R)
        res = sb("res", [TP, 2, BT, D])
        rel = sb("rel", [P, 2, BN])
        ex = sb("ex", [P, 2, BN])
        q_hi = sb("q_hi", [P, 2, BN], F32R)
        q_lo = sb("q_lo", [P, 2, BN], F32R)
        rn = sb("rn", [TP, BT, 1])
        at = sb("at", [TP, 2, BT, HD])
        a_hi = sb("a_hi", [P, 2, BN], F32R)
        a_lo = sb("a_lo", [P, 2, BN], F32R)
        qp = ctx.enter_context(nc.psum_tensor("q_qp", [P, 2, 512], F32))
        op = ctx.enter_context(nc.psum_tensor("q_op", [P, 512], F32))
        tp = ctx.enter_context(nc.psum_tensor("q_tp", [P, 512], F32))
        wp = ctx.enter_context(nc.psum_tensor("q_wp", [P, BT, 512], F32))

        const_in = sem("const_in")
        w_in = [sem("w_in0"), sem("w_in1")]
        b_in = [sem("b_in0"), sem("b_in1")]
        stored = [sem("stored0"), sem("stored1")]
        whi_done = sem("whi_done")
        wlo_done = sem("wlo_done")
        q_full = sem("q_full")
        rel_done = sem("rel_done")
        mn_done = sem("mn_done")
        ex_done = sem("ex_done")
        sq_done = sem("sq_done")
        qhi_done = sem("qhi_done")
        qlo_done = sem("qlo_done")
        o_full = sem("o_full")
        at_done = sem("at_done")
        tr_full = sem("tr_full")
        ahi_done = sem("ahi_done")
        alo_done = sem("alo_done")
        wo_full = sem("wo_full")
        res_done = sem("res_done")
        chain = sem("chain")

        STEPS = 2 * NH
        SKEW = 3

        def steps(eng, body):
            for l in range(STEPS):
                body(0, l, True)
            with eng.Fori(STEPS, B * NH, STEPS) as n0:
                for l in range(STEPS):
                    body(n0, l, False)
            for l in range(SKEW):
                body(B * NH, l, None)

        def head(l):
            l = l % STEPS
            return l // NH, l % NH, l % 2

        def at_seq(d, b):
            return d[b] if isinstance(b, int) else d[bass.ds(b, 1)].squeeze(0)

        def rows(d, b):
            r = d[b * (BT * TP):(b + 1) * (BT * TP), :] if isinstance(b, int) \
                else d[bass.ds(b * (BT * TP), BT * TP), :]
            return r.rearrange("(t p) d -> p t d", p=TP)

        block = ctx.enter_context(nc.Block())

        wo_v = wo.rearrange("(h p) n -> p h n", p=P)

        def piece(i):
            if i < NPQ:
                k, c = divmod(i, NH * HD // PIECE)
                return (wq[k * P:(k + 1) * P, c * PIECE:(c + 1) * PIECE], wq_hi[:, k, c * PIECE:(c + 1) * PIECE], wq_lo[:, k, c * PIECE:(c + 1) * PIECE])
            h = (i - NPQ) * (PIECE // D)
            hs = slice(h, h + PIECE // D)
            return (wo_v[:, hs, :], wo_hi[:, hs, :], wo_lo[:, hs, :])

        def raw_of(i):
            return raw[:, i % 2, :] if i < NPQ else raw[:, i % 2, :].rearrange("p (h n) -> p h n", n=D)

        @block.sync
        def _(sp):
            def load(b, par):
                for d, s in ((xT_hi_d, x_hi), (xT_lo_d, x_lo), (kv_hi_d, kv_hi), (kv_lo_d, kv_lo)):
                    sp.dma_start(s[:, par].bitcast(F32), at_seq(d, b)).then_inc(b_in[par], 16)
                sp.dma_start(res[:, par], rows(h_src, b)).then_inc(b_in[par], 16)

            sp.dma_start(ident[:], ident_dram).then_inc(const_in, 16)
            sp.dma_start(bias[:], bq).then_inc(const_in, 16)
            for i in range(2 * NPQ):
                if i == 4:
                    load(0, 0)
                if i >= 2:
                    sp.wait_ge(wlo_done, i - 1)
                sp.dma_start(raw_of(i), piece(i)[0]).then_inc(w_in[i % 2], 16)
            load(1, 1)
            with sp.Fori(2, B - 1, 2) as b:
                for par in range(2):
                    sp.wait_ge(stored[par], b * 8)
                    load(b + par, par)

        @block.gpsimd
        def _(pool):
            with pool.Fori(0, B - 1, 2) as b:
                for par in range(2):
                    pool.wait_ge(res_done, (b + (par + 1)) * BT)
                    pool.dma_start(rows(dst, b + par), res[:, par]).then_inc(stored[par], 16)
            for par in range(2):
                pool.wait_ge(stored[par], 8 * B)

        @block.tensor
        def _(pe):
            pe.wait_ge(const_in, 32)
            pe.wait_ge(wlo_done, 2 * NPQ)

            def body(n0, l, new):
                if new is not None:
                    s, h, z = head(l)
                    if h == 0:
                        pe.wait_ge(b_in[s], n0 * (5 * 16) // (2 * NH) + 80 if isinstance(n0, int) else
                                   (n0 // (2 * NH)) * 80 + 80)
                    if not (new and l < 2):
                        pe.wait_ge(mn_done, n0 + (l - 1))
                        pe.wait_ge(rel_done, n0 + (l - 1))
                    for k in range(KT):
                        hd = slice(h * HD, (h + 1) * HD)
                        mm = three(pe, qp[:, z, 0:BN], wq_hi[:, k, hd], wq_lo[:, k, hd], x_hi[:, s, k, :],
                                   x_lo[:, s, k, :], k == 0, k == KT - 1)
                    mm.then_inc(q_full, 1)
                if not (new and l < 1) and not (new is None and l >= 1):
                    s, h, z = head(l - 1)
                    pe.wait_ge(qlo_done, n0 + l)
                    if not (new and l < 2):
                        pe.wait_ge(at_done, n0 + (l - 1))
                    for i in range(BT):
                        tk = slice(i * TP, (i + 1) * TP)
                        mm = three(pe, op[0:TP, i * VW:(i + 1) * VW], q_hi[:, z, tk], q_lo[:, z, tk],
                                   kv_hi[:, s, h // (NH // NKV), :], kv_lo[:, s, h // (NH // NKV), :], True, True)
                    mm.then_inc(o_full, 1)
                if not (new and l < 2) and not (new is None and l >= 2):
                    s, h, z = head(l - 2)
                    pe.wait_ge(at_done, n0 + (l - 1))
                    if not (new and l < 3):
                        pe.wait_ge(alo_done, n0 + (l - 2))
                    for i in range(BT):
                        mm = pe.transpose(tp[:, i * TP:(i + 1) * TP], at[:, z, i, :], ident[0:TP, 0:TP])
                    mm.then_inc(tr_full, 1)
                if not (new and l < 3):
                    s, h, z = head(l - 3)
                    pe.wait_ge(alo_done, n0 + (l - 2))
                    if h == 0 and not (new and l < NH):
                        pe.wait_ge(res_done, 3 * ((l - 3) // NH) if isinstance(n0, int) and n0 == 0 else
                                   (n0 // NH) * BT + BT * ((l - 3) // NH))
                    for i in range(BT):
                        tk = slice(i * TP, (i + 1) * TP)
                        mm = three(pe, wp[0:TP, i, :], a_hi[:, z, tk], a_lo[:, z, tk], wo_hi[:, h, :],
                                   wo_lo[:, h, :], h == 0, h == NH - 1)
                    mm.then_inc(wo_full, 1)
            steps(pe, body)

        @block.scalar
        def _(act):
            act.wait_ge(const_in, 32)
            for i in range(2 * NPQ):
                act.wait_ge(w_in[i % 2], 16 * (i // 2 + 1))
                nc.scalar.activation(piece(i)[1], raw_of(i), ACT.Copy).then_inc(whi_done, 1)

            def body(n0, l, new):
                if new is not None:
                    s, h, z = head(l)
                    act.wait_ge(q_full, n0 + (l + 1))
                    if not (new and l < 2):
                        act.wait_ge(qlo_done, n0 + (l - 1))
                    nc.scalar.activation(rel[:, z, :], qp[:, z, 0:BN], ACT.Relu, bias=bias[:, h:h + 1]).then_inc(rel_done, 1)
                    act.wait_ge(mn_done, n0 + (l + 1))
                    nc.scalar.activation(ex[:, z, :], ex[:, z, :], ACT.Exp).then_inc(ex_done, 1)
                    act.wait_ge(sq_done, n0 + (l + 1))
                    if not (new and l < 2):
                        act.wait_ge(o_full, n0 + (l - 1))
                    nc.scalar.activation(q_hi[:, z, :], rel[:, z, :], ACT.Copy).then_inc(qhi_done, 1)
                if not (new and l < 2) and not (new is None and l >= 2):
                    s, h, z = head(l - 2)
                    act.wait_ge(tr_full, n0 + (l - 1))
                    if not (new and l < 4):
                        act.wait_ge(wo_full, n0 + (l - 3))
                    nc.scalar.activation(a_hi[:, z, 0:BT * TP], tp[:, 0:BT * TP], ACT.Copy).then_inc(ahi_done, 1)
            steps(act, body)

        @block.vector
        def _(dve):
            for i in range(2 * NPQ):
                dve.wait_ge(whi_done, i + 1)
                _, hi, lo = piece(i)
                nc.vector.tensor_tensor(lo, raw_of(i), hi.bitcast(F32), ALU.subtract).then_inc(wlo_done, 1)
            dve.wait_ge(const_in, 32)
            link = Link(dve, chain)

            def body(n0, l, new):
                if new is not None:
                    s, h, z = head(l)
                    dve.wait_ge(rel_done, n0 + (l + 1))
                    if not (new and l < 2):
                        dve.wait_ge(sq_done, n0 + (l - 1))
                    nc.vector.tensor_scalar(ex[:, z, :], qp[:, z, 0:BN], bias[:, h:h + 1], 0.0, ALU.add,
                                            ALU.min).then_inc(mn_done, 1)
                    dve.wait_ge(ex_done, n0 + (l + 1))
                    nc.vector.tensor_tensor(rel[:, z, :], rel[:, z, :], ex[:, z, :], ALU.add).then_inc(sq_done, 1)
                    dve.wait_ge(qhi_done, n0 + (l + 1))
                    nc.vector.tensor_tensor(q_lo[:, z, :], rel[:, z, :], q_hi[:, z, :].bitcast(F32),
                                            ALU.subtract).then_inc(qlo_done, 1)
                if not (new and l < 1) and not (new is None and l >= 1):
                    s, h, z = head(l - 1)
                    dve.wait_ge(o_full, n0 + l)
                    if not (new and l < 3):
                        dve.wait_ge(tr_full, n0 + (l - 2))
                    link.start((n0 + (l - 1)) * 2)
                    o3 = op[0:TP, 0:BT * VW].rearrange("p (t v) -> p t v", v=VW)
                    link(nc.vector.tensor_scalar(rn[:], o3[:, :, HD:HD + 1], 1e-6, None, ALU.add))
                    link(nc.vector.reciprocal(rn[:], rn[:]))
                    nc.vector.tensor_tensor(at[:, z], o3[:, :, 0:HD], rn[:].broadcast_to((TP, BT, HD)),
                                            ALU.mult).then_inc(at_done, 1)
                if not (new and l < 2) and not (new is None and l >= 2):
                    s, h, z = head(l - 2)
                    dve.wait_ge(ahi_done, n0 + (l - 1))
                    nc.vector.tensor_tensor(a_lo[:, z, 0:BT * TP], tp[:, 0:BT * TP],
                                            a_hi[:, z, 0:BT * TP].bitcast(F32), ALU.subtract).then_inc(alo_done, 1)
                if not (new and l < 3):
                    s, h, z = head(l - 3)
                    if h == NH - 1:
                        dve.wait_ge(wo_full, n0 + (l - 2))
                        for i in range(BT):
                            nc.vector.tensor_tensor(res[:, s, i, :], wp[0:TP, i, :], res[:, s, i, :],
                                                    ALU.add).then_inc(res_done, 1)
            steps(dve, body)


def expert_phase(nc, xn_d, w1, w2, routes, ident_dram, upper_dram, ids_d, y_d):
    KT = D // P
    H = w2.shape[1]
    HS = [min(P, H - j) for j in range(0, H, P)]
    HT = len(HS)
    UH = UNIT // P
    MAXC = -(-T // UNIT)
    with Semaphores(nc) as sems, ExitStack() as ctx:
        def sb(name, shape, dt=F32):
            return ctx.enter_context(nc.sbuf_tensor(f"ex_{name}", shape, dt))

        def sem(name):
            return sems.new(f"ex_{name}")

        ident = sb("ident", [P, P])
        upper = sb("upper", [TP, TP])
        ones = sb("ones", [TP, TP])
        both = sb("both", [TP, NT, E])
        tot = sb("tot", [TP, NT, E])
        cum = sb("cum", [TP, 2, NT, E])
        slotmap = sb("slotmap", [TP, NT, E])
        thr = sb("thr", [TP, MAXC])
        over = sb("over", [TP, E, MAXC])
        units = sb("units", [TP, E])
        uinc = sb("uinc", [TP, 2, E])
        uiota = sb("uiota", [TP, NU])
        uge = sb("uge", [TP, NU, E])
        uexp = sb("uexp", [TP, NU])
        uexp_i = sb("uexp_i", [TP, NU], I32)
        slot_f = sb("slot_f", [TP, NT])
        tok_id = sb("tok_id", [TP, NT], I32)
        zero_i = sb("zero_i", [P, NU * UH], I32)
        fence = sb("fence", [1, 2])
        ids = sb("ids", [P, 2, UH], I32)
        xg = sb("xg", [P, 2, UH, D])
        x_hi = sb("x_hi", [P, 2, KT, UNIT], F32R)
        x_lo = sb("x_lo", [P, 2, KT, UNIT], F32R)
        w1_raw = sb("w1_raw", [P, 2, KT, 2 * H])
        w2_raw = sb("w2_raw", [P, 2, HT, D])
        w1_hi = sb("w1_hi", [P, 2, KT, 2 * H], F32R)
        w1_lo = sb("w1_lo", [P, 2, KT, 2 * H], F32R)
        w2_hi = sb("w2_hi", [P, 2, HT, D], F32R)
        w2_lo = sb("w2_lo", [P, 2, HT, D], F32R)
        sil = sb("sil", [P, 2, UNIT])
        hid = sb("hid", [P, 2, UNIT])
        h_hi = sb("h_hi", [P, 2, HT, UNIT], F32R)
        h_lo = sb("h_lo", [P, 2, HT, UNIT], F32R)
        y = sb("y", [P, 2, UH, D])
        gu = ctx.enter_context(nc.psum_tensor("ex_gu", [P, 2, 2, UNIT], F32))
        tp = ctx.enter_context(nc.psum_tensor("ex_tp", [P, 2, 2, UNIT], F32))
        dn = ctx.enter_context(nc.psum_tensor("ex_dn", [P, 2, UH, D], F32))

        const_in = sem("const_in")
        tables = sem("tables")
        sums_full = sem("sums_full")
        table_done = sem("table_done")
        slots_done = sem("slots_done")
        ids_zero = sem("ids_zero")
        ids_out = sem("ids_out")
        fenced = sem("fenced")
        ids_in = [sem("ids_in0"), sem("ids_in1")]
        x_in = [sem("x_in0"), sem("x_in1")]
        w_in = [sem("w_in0"), sem("w_in1")]
        y_out = [sem("y_out0"), sem("y_out1")]
        tr_full = sem("tr_full")
        xhi_done = sem("xhi_done")
        xlo_done = sem("xlo_done")
        w1hi_done = sem("w1hi_done")
        w1lo_done = sem("w1lo_done")
        w2hi_done = sem("w2hi_done")
        w2lo_done = sem("w2lo_done")
        gu_full = sem("gu_full")
        sil_done = sem("sil_done")
        h_done = sem("h_done")
        hhi_done = sem("hhi_done")
        hlo_done = sem("hlo_done")
        dn_full = sem("dn_full")
        y_done = sem("y_done")
        chain = sem("chain")

        def loop(eng, body):
            body(0, 0, True)
            body(1, 1, True)
            with eng.Fori(2, NU - 1 if NU % 2 else NU, 2) as i:
                for par in range(2):
                    body(i + par, par, False)
            if NU % 2:
                body(NU - 1, 0, False)

        block = ctx.enter_context(nc.Block())

        def half_rows(d, u):
            r = d[u * UNIT:(u + 1) * UNIT, :] if isinstance(u, int) else d[bass.ds(u * UNIT, UNIT), :]
            return r.rearrange("(p h) d -> p h d", p=P)

        @block.sync
        def _(sp):
            sp.dma_start(ident[:], ident_dram).then_inc(const_in, 16)
            sp.dma_start(upper[:], upper_dram[0:TP, 0:TP]).then_inc(const_in, 16)
            sp.wait_ge(tables, 5)
            sp.dma_start(ids_d.rearrange("(p a) o -> p (a o)", p=P), zero_i[:]).then_inc(ids_zero, 16)
            sp.wait_ge(table_done, 1)

            def load(u, par):
                at = uexp_i[0:1, u:u + 1] if isinstance(u, int) else uexp_i[0:1, bass.ds(u, 1)]
                e = sp.value_load(at, min_val=0, max_val=E - 1)
                sp.dma_start(w1_raw[:, par], w1[bass.ds(e, 1)].rearrange("o (k p) n -> p (o k) n", p=P))\
                  .then_inc(w_in[par], 16)
                w2e = w2[bass.ds(e, 1)].rearrange("o h n -> (o h) n")
                full = H // P
                sp.dma_start(w2_raw[:, par, 0:full, :], w2e[0:full * P, :].rearrange("(j p) n -> p j n", p=P))\
                  .then_inc(w_in[par], 16)
                sp.dma_start(w2_raw[0:H % P, par, full, :], w2e[full * P:H, :]).then_inc(w_in[par], 16)

            load(0, 0)
            load(1, 1)

            def body(u, par, first):
                sp.wait_ge(w2lo_done, (u + 1) * HT)
                load(u + 2, par)
            body(0, 0, True)
            with sp.Fori(1, NU - 3, 2) as i:
                for j in range(2):
                    body(i + j, (1 + j) % 2, False)
            for u in range(NU - 2 - (NU - 3) % 2, NU - 2):
                body(u, u % 2, False)

        @block.gpsimd
        def _(pool):
            nc.gpsimd.memset(ones[:], 1.0).then_inc(tables, 1)
            nc.gpsimd.iota(thr[:], pattern=[[UNIT, MAXC]], base=0, channel_multiplier=0,
                           allow_small_or_imprecise_dtypes=True).then_inc(tables, 1)
            nc.gpsimd.iota(uiota[:], pattern=[[1, NU]], base=0, channel_multiplier=0,
                           allow_small_or_imprecise_dtypes=True).then_inc(tables, 1)
            nc.gpsimd.iota(tok_id[:], pattern=[[TP, NT]], base=0, channel_multiplier=1).then_inc(tables, 1)
            nc.gpsimd.memset(zero_i[:], 0).then_inc(tables, 1)
            nc.gpsimd.memset(fence[:], 0.0).then_inc(tables, 1)
            pool.wait_ge(tables, 6)
            pool.wait_ge(slots_done, 2)
            pool.wait_ge(ids_zero, 16)
            for r in range(2):
                for i in range(NT):
                    pool.indirect_dma_start(ids_d, bass.IndirectOffsetOnAxis(ap=routes["slot"][:, r, i:i + 1], axis=0),
                                            tok_id[:, i:i + 1], None).then_inc(ids_out, 16)
            pool.wait_ge(ids_out, 16 * 2 * NT)

            def body(u, par, first):
                if not first:
                    pool.wait_ge(x_in[par], (u - par) * (16 * UH // 2))
                pool.dma_start(ids[:, par, :], half_rows(ids_d, u).rearrange("p h o -> p (h o)")).then_inc(ids_in[par], 16)
                if not first:
                    pool.wait_ge(tr_full, (u - 1) * 2)
                pool.wait_ge(ids_in[par], (u - par) * 8 + 16)
                if not (first and u == 0):
                    pool.wait_ge(fenced, u)
                nc.gpsimd.tensor_tensor(fence[:, 0:1], fence[:, 1:2], fence[:, 1:2], ALU.add).then_inc(fenced, 1)
                for h in range(UH):
                    pool.indirect_dma_start(xg[:, par, h, :], None, xn_d,
                                            bass.IndirectOffsetOnAxis(ap=ids[:, par, h:h + 1], axis=0))\
                        .then_inc(x_in[par], 16)
            loop(pool, body)

        @block.tensor
        def _(pe):
            pe.wait_ge(const_in, 32)
            pe.wait_ge(tables, 6)
            pe.wait_ge(chain, 1)
            flat = both[:].rearrange("p t e -> p (t e)")
            pe.matmul(dn[0:TP, 0, 0, 0:NT * E], upper[:], flat, start=True, stop=True)
            pe.matmul(dn[0:TP, 0, 1, 0:NT * E], ones[:], flat, start=True, stop=True).then_inc(sums_full, 1)
            pe.wait_ge(slots_done, 2)

            def transposes(u, par, first):
                pe.wait_ge(x_in[par], (u - par) * (16 * UH // 2) + 16 * UH)
                for kk in range(KT // 2):
                    if not (first and u == 0):
                        pe.wait_ge(xlo_done, (u - 1) * (KT // 2) + (kk + 1))
                    for k in range(2):
                        for h in range(UH):
                            kc = (2 * kk + k) * P
                            mm = pe.transpose(tp[:, kk, k, h * P:(h + 1) * P], xg[:, par, h, kc:kc + P], ident[:])
                    mm.then_inc(tr_full, 1)

            def gate_up(u, par, first):
                pe.wait_ge(w1lo_done, (u + 1) * KT)
                pe.wait_ge(xlo_done, (u + 1) * (KT // 2))
                for j, hs in enumerate(HS):
                    m, mpar = u * HT + j, (par + j) % 2
                    pe.wait_ge(h_done, m + 1)
                    for half in range(2):
                        for k in range(KT):
                            wc = slice(half * H + j * P, half * H + j * P + hs)
                            mm = three(pe, gu[0:hs, mpar, half, :], w1_hi[:, par, k, wc], w1_lo[:, par, k, wc],
                                       x_hi[:, par, k, :], x_lo[:, par, k, :], k == 0, k == KT - 1)
                    mm.then_inc(gu_full, 1)

            def down(u, par, first):
                pe.wait_ge(w2lo_done, (u + 1) * HT)
                pe.wait_ge(hlo_done, (u + 1) * HT + 2)
                if not first:
                    pe.wait_ge(y_done, (u - 1) * UH)
                for t in range(UH):
                    for j, hs in enumerate(HS):
                        tk = slice(t * P, (t + 1) * P)
                        mm = three(pe, dn[:, par, t, :], h_hi[0:hs, par, j, tk], h_lo[0:hs, par, j, tk],
                                   w2_hi[0:hs, par, j, :], w2_lo[0:hs, par, j, :], j == 0, j == HT - 1)
                    mm.then_inc(dn_full, 1)

            transposes(0, 0, True)
            gate_up(0, 0, True)
            transposes(1, 1, True)
            gate_up(1, 1, True)
            transposes(2, 0, False)
            down(0, 0, True)
            gate_up(2, 0, False)
            transposes(3, 1, False)
            down(1, 1, True)
            with pe.Fori(3, NU - 2, 2) as i:
                for j in range(2):
                    par = (1 + j) % 2
                    gate_up(i + j, par, False)
                    transposes(i + (j + 1), 1 - par, False)
                    down(i + (j - 1), 1 - par, False)
            for u in range(NU - 1 - (NU - 4) % 2, NU):
                gate_up(u, u % 2, False)
                if u + 1 < NU:
                    transposes(u + 1, (u + 1) % 2, False)
                down(u - 1, (u - 1) % 2, False)
            down(NU - 1, (NU - 1) % 2, False)

        def split_x(eng, u, par, first, act):
            if act and not first:
                eng.wait_ge(gu_full, (u - 1) * HT)
            for kk in range(KT // 2):
                src, hi, lo = tp[:, kk], x_hi[:, par, 2 * kk:2 * kk + 2, :], x_lo[:, par, 2 * kk:2 * kk + 2, :]
                if act:
                    eng.wait_ge(tr_full, u * (KT // 2) + (kk + 1))
                    nc.scalar.activation(hi, src, ACT.Copy).then_inc(xhi_done, 1)
                else:
                    eng.wait_ge(xhi_done, u * (KT // 2) + (kk + 1))
                    nc.vector.tensor_tensor(lo, src, hi.bitcast(F32), ALU.subtract).then_inc(xlo_done, 1)

        def split_w1(eng, u, par, first, act, pieces):
            if act and 0 in pieces:
                eng.wait_ge(w_in[par], (u - par) * 24 + 48)
                if not first:
                    eng.wait_ge(gu_full, (u - 1) * HT)
            for k in pieces:
                raw, hi, lo = w1_raw[:, par, k, :], w1_hi[:, par, k, :], w1_lo[:, par, k, :]
                if act:
                    nc.scalar.activation(hi, raw, ACT.Copy).then_inc(w1hi_done, 1)
                else:
                    eng.wait_ge(w1hi_done, u * KT + (k + 1))
                    nc.vector.tensor_tensor(lo, raw, hi.bitcast(F32), ALU.subtract).then_inc(w1lo_done, 1)

        def split_w2(eng, u, par, first, act):
            if act:
                eng.wait_ge(w_in[par], (u - par) * 24 + 48)
                if not first:
                    eng.wait_ge(dn_full, (u - 1) * UH)
            for j, hs in enumerate(HS):
                raw, hi, lo = w2_raw[0:hs, par, j, :], w2_hi[0:hs, par, j, :], w2_lo[0:hs, par, j, :]
                if act:
                    nc.scalar.activation(hi, raw, ACT.Copy).then_inc(w2hi_done, 1)
                else:
                    eng.wait_ge(w2hi_done, u * HT + (j + 1))
                    nc.vector.tensor_tensor(lo, raw, hi.bitcast(F32), ALU.subtract).then_inc(w2lo_done, 1)

        def hidden(eng, u, par, first, act, between):
            for j, hs in enumerate(HS):
                m, mpar = u * HT + j, (par + j) % 2
                if act:
                    eng.wait_ge(gu_full, m + 1)
                    eng.wait_ge(h_done, m + 1)
                    nc.scalar.activation(sil[0:hs, mpar, :], gu[0:hs, mpar, 0, :], ACT.Silu).then_inc(sil_done, 1)
                    between(2 * j)
                    eng.wait_ge(h_done, m + 3)
                    if j == 0 and not first:
                        eng.wait_ge(dn_full, (u - 1) * UH)
                    nc.scalar.activation(h_hi[0:hs, par, j, :], hid[0:hs, mpar, :], ACT.Copy).then_inc(hhi_done, 1)
                    between(2 * j + 1)
                else:
                    eng.wait_ge(sil_done, m + 1)
                    eng.wait_ge(hlo_done, m + 1)
                    nc.vector.tensor_tensor(hid[0:hs, mpar, :], sil[0:hs, mpar, :], gu[0:hs, mpar, 1, :],
                                            ALU.mult).then_inc(h_done, 1)
                    between(2 * j)
                    eng.wait_ge(hhi_done, m + 1)
                    nc.vector.tensor_tensor(h_lo[0:hs, par, j, :], hid[0:hs, mpar, :],
                                            h_hi[0:hs, par, j, :].bitcast(F32), ALU.subtract).then_inc(hlo_done, 1)
                    between(2 * j + 1)

        def store(eng, u, par, first, act):
            if act:
                for t in range(UH):
                    eng.wait_ge(dn_full, u * UH + (t + 1))
                    if t == 0 and not first:
                        eng.wait_ge(y_out[par], (u - par) * 8)
                    nc.scalar.activation(y[:, par, t, :], dn[:, par, t, :], ACT.Copy).then_inc(y_done, 1)
                eng.wait_ge(y_done, (u + 1) * UH)
                eng.dma_start(half_rows(y_d, u), y[:, par]).then_inc(y_out[par], 16)

        def schedule(eng, act):
            split_w1(eng, 0, 0, True, act, range(KT))
            split_w2(eng, 0, 0, True, act)
            split_x(eng, 0, 0, True, act)

            def body(u, par, first, firsts, last=False):
                def between(i):
                    if not last and i < KT:
                        split_w1(eng, u + 1, 1 - par, first, act, [i])
                hidden(eng, u, par, firsts, act, between)
                if not last:
                    split_x(eng, u + 1, 1 - par, first, act)
                    split_w2(eng, u + 1, 1 - par, first, act)

            body(0, 0, True, True)
            body(1, 1, False, True)
            store(eng, 0, 0, True, act)
            body(2, 0, False, False)
            store(eng, 1, 1, True, act)
            with eng.Fori(3, NU - 2, 2) as i:
                for j in range(2):
                    par = (1 + j) % 2
                    body(i + j, par, False, False)
                    store(eng, i + (j - 1), 1 - par, False, act)
            for u in range(NU - 1 - (NU - 4) % 2, NU):
                body(u, u % 2, False, False, u == NU - 1)
                store(eng, u - 1, (u - 1) % 2, False, act)
            store(eng, NU - 1, (NU - 1) % 2, False, act)

        @block.scalar
        def _(act):
            schedule(act, True)
            for par in range(2):
                act.wait_ge(y_out[par], 16 * ((NU + 1 - par) // 2))

        @block.vector
        def _(dve):
            v = nc.vector
            link = Link(dve, chain)
            hot = routes["hot"]
            link(v.tensor_tensor(both[:], hot[:, 0], hot[:, 1], ALU.add))
            dve.wait_ge(tables, 6)
            dve.wait_ge(sums_full, 1)
            rank = dn[0:TP, 0, 0, 0:NT * E].rearrange("p (t e) -> p t e", e=E)
            link(v.tensor_copy(tot[:], dn[0:TP, 0, 1, 0:NT * E].rearrange("p (t e) -> p t e", e=E)))
            src, step, z = tot[:], 1, 0
            while step < NT:
                link(v.tensor_copy(cum[:, z, 0:step, :], src[:, 0:step, :]))
                link(v.tensor_tensor(cum[:, z, step:NT, :], src[:, step:NT, :], src[:, 0:NT - step, :], ALU.add))
                src, step, z = cum[:, z], step * 2, 1 - z
            link(v.tensor_tensor(over[:], src[:, NT - 1, :].unsqueeze(2).broadcast_to((TP, E, MAXC)),
                                 thr[:].unsqueeze(1).broadcast_to((TP, E, MAXC)), ALU.is_gt))
            link(v.tensor_reduce(units[:], over[:], AX.X, ALU.add))
            usrc, step, uz = units[:], 1, 0
            while step < E:
                link(v.tensor_copy(uinc[:, uz, 0:step], usrc[:, 0:step]))
                link(v.tensor_tensor(uinc[:, uz, step:E], usrc[:, step:E], usrc[:, 0:E - step], ALU.add))
                usrc, step, uz = uinc[:, uz], step * 2, 1 - uz
            link(v.tensor_tensor(uge[:], usrc.unsqueeze(1).broadcast_to((TP, NU, E)),
                                 uiota[:].unsqueeze(2).broadcast_to((TP, NU, E)), ALU.is_le))
            link(v.tensor_reduce(uexp[:], uge[:], AX.X, ALU.add))
            link(v.tensor_scalar(uexp[:], uexp[:], float(E - 1), None, ALU.min))
            v.tensor_copy(uexp_i[:], uexp[:]).then_inc(table_done, 1)
            link(v.tensor_tensor(units[:], usrc, units[:], ALU.subtract))
            link(v.tensor_scalar(units[:], units[:], float(UNIT), None, ALU.mult))
            link(v.tensor_tensor(slotmap[:], src, tot[:], ALU.subtract))
            link(v.tensor_tensor(slotmap[:], slotmap[:], rank, ALU.add))
            link(v.tensor_tensor(slotmap[:], slotmap[:], units[:].unsqueeze(1).broadcast_to((TP, NT, E)), ALU.add))
            for r in range(2):
                link(v.tensor_tensor(both[:], hot[:, r], slotmap[:], ALU.mult))
                link(v.tensor_reduce(slot_f[:], both[:], AX.X, ALU.add))
                v.tensor_copy(routes["slot"][:, r, :], slot_f[:]).then_inc(slots_done, 1)
                dve.wait_ge(slots_done, r + 1)
            dve.sem_inc(h_done, 2)
            dve.sem_inc(hlo_done, 2)
            schedule(dve, False)


def combine_phase(nc, base_d, y_d, routes, dst):
    R = 4
    with Semaphores(nc) as sems, ExitStack() as ctx:
        base = ctx.enter_context(nc.sbuf_tensor("cb_base", [TP, R, D], F32))
        ys = ctx.enter_context(nc.sbuf_tensor("cb_y", [TP, R, 2, D], F32))
        base_in = [sems.new(f"cb_base_in{i}") for i in range(R)]
        y_in = [sems.new(f"cb_y_in{i}") for i in range(R)]
        stored = [sems.new(f"cb_stored{i}") for i in range(R)]
        added = sems.new("cb_added")
        block = ctx.enter_context(nc.Block())

        @block.sync
        def _(sp):
            for i in range(NT):
                if i >= R:
                    sp.wait_ge(stored[i % R], 16 * (i // R))
                sp.dma_start(base[:, i % R, :], base_d[i * TP:(i + 1) * TP, :]).then_inc(base_in[i % R], 16)

        @block.gpsimd
        def _(pool):
            for i in range(NT):
                if i >= R:
                    pool.wait_ge(added, 2 * (i - R + 1))
                for r in range(2):
                    pool.indirect_dma_start(ys[:, i % R, r, :], None, y_d,
                                            bass.IndirectOffsetOnAxis(ap=routes["slot"][:, r, i:i + 1], axis=0))\
                        .then_inc(y_in[i % R], 16)

        @block.vector
        def _(dve):
            for i in range(NT):
                dve.wait_ge(base_in[i % R], 16 * (i // R + 1))
                dve.wait_ge(y_in[i % R], 32 * (i // R + 1))
                for r in range(2):
                    nc.vector.scalar_tensor_tensor(out=base[:, i % R, :], in0=ys[:, i % R, r, :],
                                                   scalar=routes["weight"][:, r, i:i + 1], in1=base[:, i % R, :],
                                                   op0=ALU.mult, op1=ALU.add).then_inc(added, 1)
                    if r == 0:
                        dve.wait_ge(added, 2 * i + 1)

        @block.scalar
        def _(act):
            for i in range(NT):
                act.wait_ge(added, 2 * (i + 1))
                act.dma_start(dst[i * TP:(i + 1) * TP, :], base[:, i % R, :]).then_inc(stored[i % R], 16)
            for r in range(R):
                act.wait_ge(stored[r], 16 * (NT // R))


def build(nc, x, ln_pre_g, ln_pre_b, tok_router, tok_router_b, tok_w1, tok_w2, ln_post_g, ln_post_b, wq, bq, wk,
          bk, wv, bv, wo, ffn_router, ffn_w1, ffn_w2,
          ffn_sh1, ffn_sh2, ident, upper, out):
    def scratch(name, shape, dt):
        return nc.dram_tensor(name, shape, dt, kind="Internal").ap()

    h1 = scratch("h1", (T, D), F32)
    h2 = scratch("h2", (T, D), F32)
    xT_hi = scratch("xT_hi", (B, P, D // P, BN), F32)
    xT_lo = scratch("xT_lo", (B, P, D // P, BN), F32)
    kv_hi = scratch("kv_hi", (B, P, NKV, HD + 2), F32)
    kv_lo = scratch("kv_lo", (B, P, NKV, HD + 2), F32)
    moe_phase(nc, x, tok_w1, tok_w2, tok_router, tok_router_b, ln_pre_g, ln_pre_b, ln_post_g, ln_post_b, ident, h1, "tok")
    kv_phase(nc, h1, wk, wv, bk, bv, ident, xT_hi, xT_lo, kv_hi, kv_lo)
    query_phase(nc, h1, wq, wo, bq, ident, xT_hi, xT_lo, kv_hi, kv_lo, h2)
    base = scratch("base", (T, D), F32)
    xn = scratch("xn", (T, D), F32)
    ids = scratch("ids", (NU * UNIT, 1), I32)
    y = scratch("y", (NU * UNIT, D), F32)
    with ExitStack() as ctx:
        routes = {
            "hot": ctx.enter_context(nc.sbuf_tensor("rt_hot", [TP, 2, NT, E], F32)),
            "weight": ctx.enter_context(nc.sbuf_tensor("rt_weight", [TP, 2, NT], F32)),
            "slot": ctx.enter_context(nc.sbuf_tensor("rt_slot", [TP, 2, NT], I32)),
        }
        moe_phase(nc, h2, ffn_sh1, ffn_sh2, ffn_router, None, None, None, None, None, ident, base, "ffn", routes, xn)
        expert_phase(nc, xn, ffn_w1, ffn_w2, routes, ident, upper, ids, y)
        combine_phase(nc, base, y, routes, out)


def kernel(**inputs):
    import numpy as np
    from concourse import bacc
    from concourse.bass_utils import run_bass_kernel_spmd

    a = {k: np.asarray(v) for k, v in inputs.items()}
    L = "L0_"
    shw_g, shw_u, shw_d = a[L + "ffn_shw_gate"], a[L + "ffn_shw_up"], a[L + "ffn_shw_down"]
    H = a[L + "ffn_w_gate"].shape[2]
    halves = [slice(i * H, (i + 1) * H) for i in range(shw_g.shape[1] // H)]
    sh1 = np.stack([np.concatenate([shw_g[:, s], shw_u[:, s]], axis=1) for s in halves])
    sh2 = np.stack([shw_d[s] for s in halves])
    arrays = {
        "x": a["x"].reshape(T, -1),
        "ln_pre_g": a[L + "tok_ln_pre_g"].reshape(-1, P).T,
        "ln_pre_b": a[L + "tok_ln_pre_b"].reshape(-1, P).T,
        "tok_router": a[L + "tok_router_w"].T,
        "tok_router_b": a[L + "tok_router_b"],
        "tok_w1": np.concatenate([a[L + "tok_experts_w12"], a[L + "tok_shared_w12"][None]]).transpose(0, 2, 1),
        "tok_w2": np.concatenate([a[L + "tok_experts_w3"], a[L + "tok_shared_w3"][None]]).transpose(0, 2, 1),
        "ln_post_g": a[L + "tok_ln_post_g"],
        "ln_post_b": a[L + "tok_ln_post_b"],
        "wq": a[L + "attn_Wq"].T,
        "bq": a[L + "attn_bq"].reshape(NH, HD).T,
        "wk": a[L + "attn_Wk"].T,
        "bk": a[L + "attn_bk"],
        "wv": a[L + "attn_Wv"].T,
        "bv": a[L + "attn_bv"],
        "wo": a[L + "attn_Wo"].T,
        "ffn_router": np.concatenate([a[L + "ffn_gate_w"], a[L + "ffn_shgate_w"][None]]).T,
        "ffn_w1": np.concatenate([a[L + "ffn_w_gate"], a[L + "ffn_w_up"]], axis=2),
        "ffn_w2": a[L + "ffn_w_down"],
        "ffn_sh1": sh1,
        "ffn_sh2": sh2,
        "ident": np.eye(P, dtype=np.float32),
        "upper": np.triu(np.ones((P, P), np.float32), 1),
    }
    arrays = {k: np.ascontiguousarray(v) for k, v in arrays.items()}
    nc = bacc.Bacc("TRN2", target_bir_lowering=False, num_devices=1)
    args = [nc.dram_tensor(k, v.shape, mybir.dt.from_np(v.dtype), kind="ExternalInput").ap() for k, v in arrays.items()]
    out = nc.dram_tensor("out", (T, D), F32, kind="ExternalOutput").ap()
    build(nc, *args, out)
    r = run_bass_kernel_spmd(nc, [arrays], core_ids=[0])
    return r.results[0]["out"].reshape(B, T // B, D)
```

```python
from contextlib import ExitStack

import concourse.bass as bass
from concourse import mybir

ALU = mybir.AluOpType
ACT = mybir.ActivationFunctionType
AX = mybir.AxisListType
F32 = mybir.dt.float32
F32R = mybir.dt.float32r
I32 = mybir.dt.int32

T = 3000
TP = 125
NT = T // TP
D = 512
P = 128
ST = 4
SN = ST * TP
GROUPS = 2
GS = 3
GT = GS * ST
B = 8
BT = 3
E = 8
NH, NKV, HD = 16, 4, 128
UNIT = 256
NU = (2 * T + E * (UNIT - 1)) // UNIT
BN = 376


class Link:

    def __init__(self, eng, sem):
        self.eng, self.sem, self.n, self.base = eng, sem, 0, 0

    def __call__(self, ins):
        self.n += 1
        ins.then_inc(self.sem, 1)
        self.eng.wait_ge(self.sem, self.base + self.n)

    def start(self, base):
        self.base, self.n = base, 0


class Semaphores:

    def __init__(self, nc):
        self.nc, self.all = nc, []

    def __enter__(self):
        return self

    def new(self, name):
        self.all.append(self.nc.alloc_semaphore(name))
        return self.all[-1]

    def __exit__(self, *error):
        if error[0] is None:
            self.nc.clear_and_free_semaphores(self.all)
            self.nc.all_engine_barrier()


def three(eng, out, w_hi, w_lo, x_hi, x_lo, first, last):
    eng.matmul(out, w_hi, x_hi, start=first, stop=False)
    eng.matmul(out, w_hi, x_lo, start=False, stop=False)
    return eng.matmul(out, w_lo, x_hi, start=False, stop=last)


NEWTON = 5


def rstd_newton(link, dve, ve, rs, tmp):
    link(dve.reciprocal(rs, rs))
    link(dve.tensor_tensor(tmp, rs, rs, ALU.mult))
    link(dve.tensor_tensor(tmp, tmp, ve, ALU.mult))
    link(dve.tensor_scalar(tmp, tmp, -0.5, 1.5, ALU.mult, ALU.add))
    link(dve.tensor_tensor(rs, rs, tmp, ALU.mult))


def moe_phase(nc, x_src, w1_cols, w2_rows, hidden_sizes, router, router_b, ln_g, ln_b, post_g, post_b, ident_dram,
              dst, tag, routes=None, xn_d=None):
    tok = ln_g is not None
    HS = hidden_sizes
    NC = len(HS)
    K = x_src.shape[1]
    KT = K // P
    NR = router.shape[1]
    EPS_IN = 1e-6 if tok else 1e-5
    NB = 2 if K > 512 else 1
    NW = NC if tok else 1
    N = BT * TP

    ROUTER, LOGITS, SOFTMAX, EXP, TOP_A, TOP_B = KT, KT + 1, KT + 1, KT + 2, KT + 3, KT + 4
    STATS, ROOT, NORM = range(NC - 5, NC - 2), NC - 2, NC - 1
    POST_STATS, POST_ROOT, POST = 1, 2, range(3, 3 + BT)

    with Semaphores(nc) as sems, ExitStack() as ctx:
        def sb(name, shape, dt=F32):
            return ctx.enter_context(nc.sbuf_tensor(f"{tag}_{name}", shape, dt))

        def sem(name):
            return sems.new(f"{tag}_{name}")

        w1_hi = sb("w1_hi", [P, NC, KT, 2, P], F32R)
        w1_lo = sb("w1_lo", [P, NC, KT, 2, P], F32R)
        w2_hi = sb("w2_hi", [P, NC, D], F32R)
        w2_lo = sb("w2_lo", [P, NC, D], F32R)
        RING = 2 if tok else 4
        raw = sb("raw", [P, RING, KT * P])
        x_hi = sb("x_hi", [P, 2, KT, BN], F32R)
        x_lo = sb("x_lo", [P, 2, KT, BN], F32R)
        xn = sb("xn", [TP, 2, BT, K])
        acc = sb("acc", [TP, 2, BT, D])
        sil = sb("sil", [P, 2, BN])
        hid = sb("hid", [P, 2, BN])
        h_hi = sb("h_hi", [P, 2, BN], F32R)
        h_lo = sb("h_lo", [P, 2, BN], F32R)
        ident = sb("ident", [P, P])
        r_raw = sb("r_raw", [P, KT, NR])
        r_hi = sb("r_hi", [P, KT, NR], F32R)
        r_lo = sb("r_lo", [P, KT, NR], F32R)
        st = sb("st", [TP, BT, NB, 6])
        mv = sb("mv", [TP, BT, 2])
        ve = sb("ve", [TP, BT])
        rs = sb("rs", [TP, BT])
        tmp = sb("tmp", [TP, BT])
        fence = sb("fence", [1, 4])
        lg = sb("lg", [TP, BT, NR])
        pr = sb("pr", [TP, BT, E])
        key = sb("key", [TP, BT, E])
        one = sb("one", [TP, BT, E])
        red = sb("red", [TP, BT])
        tops = [sb("top1", [TP, BT]), sb("top2", [TP, BT])]
        comb = sb("comb", [TP, 2, BT, NW])
        iota = sb("iota", [TP, E])
        xf = sb("xf", [P if tok else NR, N])
        rT = xf[0:NR, :]
        if tok:
            gb = sb("gb", [P, 2, KT])
            post = sb("post", [TP, 2, D])
            rb = sb("rb", [TP, E])
            post_st = sb("post_st", [TP, BT, 6])
            post_mv = sb("post_mv", [TP, BT, 2])
            post_ve = sb("post_ve", [TP, BT])
            post_rs = sb("post_rs", [TP, BT])
            post_tmp = sb("post_tmp", [TP, BT])
        gu = ctx.enter_context(nc.psum_tensor(f"{tag}_gu", [P, 2, 2, 512], F32))
        dn = ctx.enter_context(nc.psum_tensor(f"{tag}_dn", [P, BT, 512], F32))
        tp = ctx.enter_context(nc.psum_tensor(f"{tag}_tp", [P, 512], F32))
        rt = tp[0:NR, 0:BN]
        lt = tp[0:TP, BN:BN + BT * NR]

        const_in = sem("const_in")
        x_in = [sem("x_in0"), sem("x_in1")]
        acc_in = [sem("acc_in0"), sem("acc_in1")]
        w_in = [sem(f"w_in{i}") for i in range(RING)]
        stored = [sem("stored0"), sem("stored1")]
        xn_out = [sem("xn_out0"), sem("xn_out1")]
        pads = sem("pads")
        iota_done = sem("iota_done")
        bn_done = sem("bn_done")
        aggr_done = sem("aggr_done")
        var_done = sem("var_done")
        sqrt_done = sem("sqrt_done")
        xn_done = sem("xn_done")
        tr_full = sem("tr_full")
        xf_done = sem("xf_done")
        xhi_done = sem("xhi_done")
        xlo_done = sem("xlo_done")
        rhi_done = sem("rhi_done")
        rlo_done = sem("rlo_done")
        rt_full = sem("rt_full")
        rt_done = sem("rt_done")
        lg_full = sem("lg_full")
        lg_done = sem("lg_done")
        mx_done = sem("mx_done")
        ex_done = sem("ex_done")
        gate_done = sem("gate_done")
        whi_done = sem("whi_done")
        wlo_done = sem("wlo_done")
        gu_full = sem("gu_full")
        sil_done = sem("sil_done")
        h_done = sem("h_done")
        hhi_done = sem("hhi_done")
        hlo_done = sem("hlo_done")
        dn_full = sem("dn_full")
        acc_done = sem("acc_done")
        post_bn = sem("post_bn")
        post_aggr = sem("post_aggr")
        post_var = sem("post_var")
        post_sqrt = sem("post_sqrt")
        post_done = sem("post_done")
        norm_chain = sem("norm_chain")
        top_chain = sem("top_chain")
        post_chain = sem("post_chain")
        setup_chain = sem("setup_chain")

        def at_time(b, par, c, time, ahead):
            out = []
            for late in range(2):
                u = b + (ahead - late)
                if time == c + late * NC and not (isinstance(u, int) and not ahead <= u < B):
                    out.append((u, (par + ahead - late) % 2))
            return out

        def sequences(eng, body):
            body(0, 0)
            body(1, 1)
            with eng.Fori(2, B - 3, 2) as i:
                for par in range(2):
                    body(i + par, par)
            body(B - 2, 0)
            body(B - 1, 1)

        def parity(par, c):
            return (par * NC + c) % 2

        def pieces(c):
            h, out = HS[c], []
            for p in range(3 * c, 3 * c + 3):
                buf, half = raw[:, p % RING, :], p % 3
                if half < 2:
                    out.append((p, buf.rearrange("p (k n) -> p k n", n=P)[:, :, 0:h], w1_hi[:, c, :, half, 0:h],
                                w1_lo[:, c, :, half, 0:h]))
                else:
                    out.append((p, buf[0:h, 0:D], w2_hi[0:h, c, :], w2_lo[0:h, c, :]))
            return out

        def rows(d, b):
            r = d[b * N:(b + 1) * N, :] if isinstance(b, int) else d[bass.ds(b * N, N), :]
            return r.rearrange("(t p) d -> p t d", p=TP)

        block = ctx.enter_context(nc.Block())

        @block.sync
        def _(sp):
            sp.dma_start(xn[:, 0], rows(x_src, 0)).then_inc(x_in[0], 16)

            def weights(c):
                for p, to, _, _ in pieces(c):
                    if p >= RING:
                        sp.wait_ge(wlo_done, p - RING + 1)
                    src = w1_cols(c, p % 3).rearrange("(k p) n -> p k n", p=P) if p % 3 < 2 else w2_rows(c)
                    sp.dma_start(to, src).then_inc(w_in[p % RING], 16)

            def keep(u, par):
                if not tok:
                    sp.wait_ge(xn_done, (u + 1) * BT)
                    sp.dma_start(rows(xn_d, u), xn[:, par]).then_inc(xn_out[par], 16)

            weights(0)
            sp.dma_start(xn[:, 1], rows(x_src, 1)).then_inc(x_in[1], 16)
            weights(1)
            keep(0, 0)
            keep(1, 1)
            for u in range(2, B):
                sp.wait_ge(tr_full, (u - 1) * KT)
                if not tok:
                    sp.wait_ge(xn_out[u % 2], 16 * (u // 2))
                sp.dma_start(xn[:, u % 2], rows(x_src, u)).then_inc(x_in[u % 2], 16)
                if u == 2:
                    for c in range(2, NC):
                        weights(c)
                keep(u, u % 2)
            if not tok:
                for par in range(2):
                    sp.wait_ge(xn_out[par], 16 * (B // 2))

        @block.gpsimd
        def _(pool):
            pool.dma_start(ident[:], ident_dram).then_inc(const_in, 16)
            pool.dma_start(r_raw[:], router.rearrange("(k p) n -> p k n", p=P)).then_inc(const_in, 16)
            if tok:
                pool.dma_start(gb[:, 0, :], ln_g).then_inc(const_in, 16)
                pool.dma_start(gb[:, 1, :], ln_b).then_inc(const_in, 16)
                pool.dma_start(rb[:], router_b.partition_broadcast(TP)).then_inc(const_in, 16)
                pool.dma_start(post[:, 0, :], post_g.partition_broadcast(TP)).then_inc(const_in, 16)
                pool.dma_start(post[:, 1, :], post_b.partition_broadcast(TP)).then_inc(const_in, 16)
            else:
                for par in range(2):
                    pool.dma_start(acc[:, par], rows(x_src, par)).then_inc(acc_in[par], 16)
            nc.gpsimd.memset(x_hi[:, :, :, N:BN].bitcast(F32), 0.0).then_inc(pads, 1)
            nc.gpsimd.memset(x_lo[:, :, :, N:BN].bitcast(F32), 0.0).then_inc(pads, 1)
            nc.gpsimd.iota(iota[:], pattern=[[1, E]], base=0, channel_multiplier=0,
                           allow_small_or_imprecise_dtypes=True).then_inc(iota_done, 1)

            def store(b, par, refill):
                if tok:
                    pool.wait_ge(post_done, (b + 1) * BT)
                else:
                    pool.wait_ge(acc_done, (b + 1) * (NC * BT))
                pool.dma_start(rows(dst, b), acc[:, par]).then_inc(stored[par], 16)
                if refill and not tok:
                    pool.wait_ge(stored[par], (b - par) * 8 + 16)
                    pool.dma_start(acc[:, par], rows(x_src, b + 2)).then_inc(acc_in[par], 16)
            with pool.Fori(0, B - 3, 2) as i:
                for par in range(2):
                    store(i + par, par, True)
            store(B - 2, 0, False)
            store(B - 1, 1, False)
            for par in range(2):
                pool.wait_ge(stored[par], 16 * (B // 2))

        NCONST = 16 * (7 if tok else 2)

        @block.tensor
        def _(pe):
            pe.wait_ge(const_in, NCONST)
            pe.wait_ge(pads, 2)

            def transposes(u, par, k):
                if k == 0:
                    pe.wait_ge(xn_done, (u + 1) * BT)
                    if not (isinstance(u, int) and u == 0):
                        pe.wait_ge(lg_done, u)
                if not (isinstance(u, int) and u == 0 and k == 0):
                    pe.wait_ge(xf_done if tok else xlo_done, u * KT + k)
                for t in range(BT):
                    mm = pe.transpose(tp[:, t * TP:(t + 1) * TP], xn[:, par, t, k * P:(k + 1) * P],
                                      ident[0:TP, 0:TP])
                mm.then_inc(tr_full, 1)

            def router_logits(u, par):
                pe.wait_ge(xlo_done, (u + 1) * KT)
                for k in range(KT):
                    mm = three(pe, rt[:], r_hi[:, k, :], r_lo[:, k, :], x_hi[:, par, k, :], x_lo[:, par, k, :],
                               k == 0, k == KT - 1)
                mm.then_inc(rt_full, 1)

            def token_logits():
                for t in range(BT):
                    mm = pe.transpose(lt[:, t * NR:(t + 1) * NR], rT[:, t * TP:(t + 1) * TP], ident[0:NR, 0:NR])
                mm.then_inc(lg_full, 1)

            def down(n, npar, c, first):
                if first:
                    pe.wait_ge(wlo_done, 3 * (c + 1))
                pe.wait_ge(hlo_done, n + 1)
                for t in range(BT):
                    if not (isinstance(n, int) and n == 0):
                        pe.wait_ge(acc_done, n * BT + (t + 1 - BT))
                    tk, h = slice(t * TP, (t + 1) * TP), HS[c]
                    three(pe, dn[0:TP, t, :], h_hi[0:h, npar, tk], h_lo[0:h, npar, tk],
                          w2_hi[0:h, c, :], w2_lo[0:h, c, :], True, True).then_inc(dn_full, 1)

            def body(b, par):
                first = isinstance(b, int) and b == 0
                for c in range(NC):
                    n, npar, h = b * NC + c, parity(par, c), HS[c]
                    if first:
                        pe.wait_ge(wlo_done, 3 * c + 2)
                    if c == 0:
                        pe.wait_ge(xlo_done, (b + 1) * KT)
                    if not (first and c < 2):
                        pe.wait_ge(h_done, n - 1)
                    for half in range(2):
                        for k in range(KT):
                            mm = three(pe, gu[0:h, npar, half, 0:BN], w1_hi[:, c, k, half, 0:h],
                                       w1_lo[:, c, k, half, 0:h], x_hi[:, par, k, :], x_lo[:, par, k, :],
                                       k == 0, k == KT - 1)
                    mm.then_inc(gu_full, 1)
                    logits = at_time(b, par, c, LOGITS, 1)
                    for u, _ in logits:
                        pe.wait_ge(rt_done, u + 1)
                    if not (first and c == 0):
                        down(n - 1, 1 - npar, (c - 1) % NC, first or (isinstance(b, int) and b == 1 and c == 0))
                    for k in range(KT):
                        for u, upar in at_time(b, par, c, k, 1):
                            transposes(u, upar, k)
                    for u, upar in at_time(b, par, c, ROUTER, 1):
                        router_logits(u, upar)
                    for _ in logits:
                        token_logits()

            for k in range(KT):
                transposes(0, 0, k)
            pe.wait_ge(rlo_done, 1)
            router_logits(0, 0)
            pe.wait_ge(rt_done, 1)
            token_logits()
            sequences(pe, body)
            down(B * NC - 1, parity(1, NC - 1), NC - 1, False)

        @block.scalar
        def _(act):
            a = nc.scalar

            def root(u):
                act.wait_ge(var_done, u + 1)
                a.activation(rs[:], ve[:], ACT.Sqrt).then_inc(sqrt_done, 1)

            def split_x(u, par, k):
                if k == 0 and not (isinstance(u, int) and u < 2):
                    act.wait_ge(gu_full, (u - 1) * NC)
                act.wait_ge(tr_full, u * KT + (k + 1))
                if tok:
                    if not (isinstance(u, int) and u == 0 and k == 0):
                        act.wait_ge(xlo_done, u * KT + k)
                        if k == 0:
                            act.wait_ge(lg_full, u)
                    a.activation(xf[:], tp[:, 0:N], ACT.Identity, bias=gb[:, 1, k:k + 1],
                                 scale=gb[:, 0, k:k + 1]).then_inc(xf_done, 1)
                    act.wait_ge(xf_done, u * KT + (k + 1))
                a.activation(x_hi[:, par, k, 0:N], xf[:] if tok else tp[:, 0:N], ACT.Copy).then_inc(xhi_done, 1)

            def copy_logits(u):
                act.wait_ge(rt_full, u + 1)
                if not (isinstance(u, int) and u == 0):
                    act.wait_ge(lg_full, u)
                a.activation(rT[:], rt[:, 0:N], ACT.Copy).then_inc(rt_done, 1)

            def softmax(u, par):
                act.wait_ge(mx_done, u + 1)
                a.activation(pr[:], key[:], ACT.Exp).then_inc(ex_done, 1)
                if not tok:
                    if not (isinstance(u, int) and u < 2):
                        act.wait_ge(acc_done, (u - 1) * (NC * BT))
                    a.activation(comb[:, par], lg[:, :, E:E + 1], ACT.Sigmoid).then_inc(gate_done, 1)

            def split_w(c, which=range(3)):
                for p, src, hi, _ in pieces(c)[which.start:which.stop]:
                    act.wait_ge(w_in[p % RING], 16 * (p // RING + 1))
                    a.activation(hi, src, ACT.Copy).then_inc(whi_done, 1)

            def body(b, par):
                first = isinstance(b, int) and b == 0
                for c in range(NC):
                    n, npar, h = b * NC + c, parity(par, c), HS[c]
                    if first and c + 1 < NC:
                        split_w(c + 1)
                    for u, _ in at_time(b, par, c, LOGITS, 1):
                        copy_logits(u)
                    act.wait_ge(gu_full, n + 1)
                    if not (first and c < 2):
                        act.wait_ge(h_done, n - 1)
                    a.activation(sil[0:h, npar, 0:N], gu[0:h, npar, 0, 0:N], ACT.Silu).then_inc(sil_done, 1)
                    for k in range(KT):
                        for u, upar in at_time(b, par, c, k + 1, 1):
                            split_x(u, upar, k)
                    act.wait_ge(h_done, n + 1)
                    if not (first and c < 2):
                        act.wait_ge(dn_full, (n - 1) * BT)
                    a.activation(h_hi[0:h, npar, 0:N], hid[0:h, npar, 0:N], ACT.Copy).then_inc(hhi_done, 1)
                    for u, upar in at_time(b, par, c, EXP, 1):
                        softmax(u, upar)
                    for u, upar in at_time(b, par, c, ROOT, 2):
                        root(u)
                    if tok and c == POST_ROOT and not first:
                        act.wait_ge(post_var, b)
                        a.activation(post_rs[:], post_ve[:], ACT.Sqrt).then_inc(post_sqrt, 1)

            root(0)
            act.wait_ge(const_in, NCONST)
            split_w(0, range(2))
            for k in range(KT):
                split_x(0, 0, k)
            a.activation(r_hi[:], r_raw[:], ACT.Copy).then_inc(rhi_done, 1)
            copy_logits(0)
            split_w(0, range(2, 3))
            root(1)
            softmax(0, 0)
            sequences(act, body)
            if tok:
                act.wait_ge(post_var, B)
                a.activation(post_rs[:], post_ve[:], ACT.Sqrt).then_inc(post_sqrt, 1)

        @block.vector
        def _(dve):
            v = nc.vector
            norm, top, postl, setup = (Link(dve, s) for s in (norm_chain, top_chain, post_chain, setup_chain))
            if tok:
                setup(v.memset(comb[:, :, :, E:NC], 1.0))
            def bc(ap):
                return ap.unsqueeze(2).broadcast_to((TP, BT, E))

            def statistics(u, par, t):
                if t == 0:
                    dve.wait_ge(x_in[par], (u - par) * 8 + 16)
                for i in range(NB):
                    w = K // NB
                    v.bn_stats(st[:, t, i, :], xn[:, par, t, i * w:(i + 1) * w]).then_inc(bn_done, 1)
                if t == BT - 1:
                    dve.wait_ge(bn_done, (u + 1) * (BT * NB))
                    v.memset(fence[:, par:par + 1], 0.0)
                    for i in range(BT):
                        v.bn_aggr(mv[:, i, :], st[:, i, :, :]).then_inc(aggr_done, 1)
                    dve.wait_ge(aggr_done, (u + 1) * BT)
                    v.tensor_scalar(ve[:], mv[:, :, 1], EPS_IN, None, ALU.add).then_inc(var_done, 1)

            def normalise(u, par):
                norm.start(u * NEWTON)
                dve.wait_ge(sqrt_done, u + 1)
                rstd_newton(norm, v, ve[:], rs[:], tmp[:])
                assert norm.n == NEWTON
                for t in range(BT):
                    v.tensor_scalar(xn[:, par, t, :], xn[:, par, t, :], mv[:, t, 0:1], rs[:, t:t + 1],
                                    ALU.subtract, ALU.mult).then_inc(xn_done, 1)

            def split_x(u, par, k):
                dve.wait_ge(xhi_done, u * KT + (k + 1))
                v.tensor_tensor(x_lo[:, par, k, 0:N], xf[:] if tok else tp[:, 0:N],
                                x_hi[:, par, k, 0:N].bitcast(F32), ALU.subtract).then_inc(xlo_done, 1)

            TOP_LINKS = (1, 13, 25) if tok else (1, 12, 22)

            def softmax(u, par):
                top.start(u * TOP_LINKS[2])
                dve.wait_ge(lg_full, u + 1)
                lp = lt.rearrange("p (t e) -> p t e", e=NR)
                if tok:
                    v.tensor_tensor(lg[:], lp, rb[:].unsqueeze(1).broadcast_to((TP, BT, E)), ALU.add).then_inc(lg_done, 1)
                else:
                    v.tensor_copy(lg[:], lp).then_inc(lg_done, 1)
                dve.wait_ge(lg_done, u + 1)
                top(v.tensor_reduce(red[:], lg[:, :, 0:E], AX.X, ALU.max))
                v.tensor_tensor(key[:], lg[:, :, 0:E], bc(red[:]), ALU.subtract).then_inc(mx_done, 1)

            def choose(u, par, r):
                ib = iota[:].unsqueeze(1).broadcast_to((TP, BT, E))
                top.start(u * TOP_LINKS[2])
                top.n = TOP_LINKS[r]
                if r == 0:
                    dve.wait_ge(ex_done, u + 1)
                    dve.wait_ge(iota_done, 1)
                    top(v.tensor_reduce(red[:], pr[:], AX.X, ALU.add))
                    top(v.reciprocal(red[:], red[:]))
                    top(v.tensor_tensor(pr[:], pr[:], bc(red[:]), ALU.mult))
                best = tops[r]
                top(v.tensor_reduce(best[:], pr[:], AX.X, ALU.max))
                top(v.tensor_tensor(key[:], pr[:], bc(best[:]), ALU.is_lt))
                top(v.tensor_scalar(key[:], key[:], float(E), None, ALU.mult))
                top(v.tensor_tensor(key[:], key[:], ib, ALU.add))
                top(v.tensor_reduce(red[:], key[:], AX.X, ALU.min))
                top(v.tensor_tensor(one[:], ib, bc(red[:]), ALU.is_equal))
                if tok:
                    if r == 0:
                        top(v.tensor_tensor(comb[:, par, :, 0:E], one[:], bc(best[:]), ALU.mult))
                    else:
                        top(v.tensor_tensor(key[:], one[:], bc(best[:]), ALU.mult))
                        top(v.tensor_tensor(comb[:, par, :, 0:E], comb[:, par, :, 0:E], key[:], ALU.add))
                else:
                    hot = routes["hot"][:, r, u * BT:(u + 1) * BT, :] if isinstance(u, int) \
                        else routes["hot"][:, r, bass.ds(u * BT, BT), :]
                    v.tensor_copy(hot, one[:])
                if r == 0:
                    top(v.tensor_scalar(key[:], one[:], -2.0, None, ALU.mult))
                    top(v.tensor_tensor(pr[:], pr[:], key[:], ALU.add))
                    assert top.n == TOP_LINKS[1], top.n
                    return
                top(v.tensor_tensor(red[:], tops[0][:], tops[1][:], ALU.add))
                if tok:
                    top(v.tensor_scalar(red[:], red[:], 1e-20, None, ALU.add))
                top(v.reciprocal(red[:], red[:]))
                if tok:
                    top(v.tensor_tensor(comb[:, par, :, 0:E], comb[:, par, :, 0:E], bc(red[:]), ALU.mult))
                else:
                    for i, best in enumerate(tops):
                        weight = routes["weight"][:, i, u * BT:(u + 1) * BT] if isinstance(u, int) \
                            else routes["weight"][:, i, bass.ds(u * BT, BT)]
                        top(v.tensor_tensor(weight, best[:], red[:], ALU.mult))
                assert top.n == TOP_LINKS[2], top.n

            def split_w(c, which=range(3)):
                for p, src, hi, lo in pieces(c)[which.start:which.stop]:
                    dve.wait_ge(whi_done, p + 1)
                    v.tensor_tensor(lo, src, hi.bitcast(F32), ALU.subtract).then_inc(wlo_done, 1)

            def add(n, npar, par, c):
                for t in range(BT):
                    dve.wait_ge(dn_full, n * BT + (t + 1))
                    w = comb[:, par, t, c:c + 1] if tok else comb[:, par, t, 0:1]
                    src, to = dn[0:TP, t, :], acc[:, par, t, :]
                    if tok and c == 0:
                        v.tensor_scalar(to, src, w, None, ALU.mult).then_inc(acc_done, 1)
                    else:
                        if c:
                            dve.wait_ge(acc_done, n * BT + (t + 1 - BT))
                        v.scalar_tensor_tensor(out=to, in0=src, scalar=w, in1=to, op0=ALU.mult,
                                               op1=ALU.add).then_inc(acc_done, 1)

            def add_first(n, npar, b, par, first_two):
                if tok:
                    if not first_two:
                        dve.wait_ge(stored[par], (b - par) * 8)
                else:
                    dve.wait_ge(acc_in[par], (b - par) * 8 + 16)
                    dve.wait_ge(gate_done, b + 1)
                add(n, npar, par, 0)

            def post_stats(b, par):
                dve.wait_ge(acc_done, (b + 1) * (NC * BT))
                for t in range(BT):
                    v.bn_stats(post_st[:, t, :], acc[:, par, t, :]).then_inc(post_bn, 1)
                dve.wait_ge(post_bn, (b + 1) * BT)
                v.memset(fence[:, par + 2:par + 3], 0.0)
                for t in range(BT):
                    v.bn_aggr(post_mv[:, t, :], post_st[:, t, :]).then_inc(post_aggr, 1)
                dve.wait_ge(post_aggr, (b + 1) * BT)
                v.tensor_scalar(post_ve[:], post_mv[:, :, 1], 1e-6, None, ALU.add).then_inc(post_var, 1)

            def post_tile(b, par, t):
                PER = NEWTON + 2 * BT
                postl.start(b * PER)
                if t == 0:
                    dve.wait_ge(post_sqrt, b + 1)
                    rstd_newton(postl, v, post_ve[:], post_rs[:], post_tmp[:])
                else:
                    postl.n = NEWTON + 2 * t
                to = acc[:, par, t, :]
                postl(v.tensor_scalar(to, to, post_mv[:, t, 0:1], post_rs[:, t:t + 1], ALU.subtract, ALU.mult))
                postl(v.tensor_tensor(to, to, post[:, 0, :], ALU.mult))
                v.tensor_tensor(to, to, post[:, 1, :], ALU.add).then_inc(post_done, 1)

            def body(b, par):
                first = isinstance(b, int) and b == 0
                first_two = isinstance(b, int) and b < 2
                for c in range(NC):
                    n, npar, h = b * NC + c, parity(par, c), HS[c]
                    if first and c + 1 < NC:
                        split_w(c + 1)
                    dve.wait_ge(sil_done, n + 1)
                    if not (first and c < 2):
                        dve.wait_ge(hlo_done, n - 1)
                    v.tensor_tensor(hid[0:h, npar, 0:N], sil[0:h, npar, 0:N], gu[0:h, npar, 1, 0:N],
                                    ALU.mult).then_inc(h_done, 1)
                    for k in range(KT):
                        for u, upar in at_time(b, par, c, k + 1, 1):
                            split_x(u, upar, k)
                    dve.wait_ge(hhi_done, n + 1)
                    v.tensor_tensor(h_lo[0:h, npar, 0:N], hid[0:h, npar, 0:N],
                                    h_hi[0:h, npar, 0:N].bitcast(F32), ALU.subtract).then_inc(hlo_done, 1)
                    if c == 1:
                        add_first(n - 1, 1 - npar, b, par, first_two)
                    elif c:
                        add(n - 1, 1 - npar, par, c - 1)
                    elif not first:
                        add(n - 1, 1 - npar, 1 - par, NC - 1)
                    for u, upar in at_time(b, par, c, NORM, 2):
                        normalise(u, upar)
                    for t in range(BT):
                        for u, upar in at_time(b, par, c, STATS[t], 2):
                            statistics(u, upar, t)
                    for u, upar in at_time(b, par, c, SOFTMAX, 1):
                        softmax(u, upar)
                    for r, time in enumerate((TOP_A, TOP_B)):
                        for u, upar in at_time(b, par, c, time, 1):
                            choose(u, upar, r)
                    if tok and not first:
                        if c == POST_STATS:
                            post_stats(b - 1, 1 - par)
                        elif c in POST:
                            post_tile(b - 1, 1 - par, c - POST[0])

            for t in range(BT):
                statistics(0, 0, t)
            normalise(0, 0)
            split_w(0, range(2))
            for k in range(KT):
                split_x(0, 0, k)
            dve.wait_ge(rhi_done, 1)
            v.tensor_tensor(r_lo[:], r_raw[:], r_hi[:].bitcast(F32), ALU.subtract).then_inc(rlo_done, 1)
            split_w(0, range(2, 3))
            for t in range(BT):
                statistics(1, 1, t)
            normalise(1, 1)
            softmax(0, 0)
            for r in range(2):
                choose(0, 0, r)
            sequences(dve, body)
            add(B * NC - 1, parity(1, NC - 1), 1, NC - 1)
            if tok:
                post_stats(B - 1, 1)
                for t in range(BT):
                    post_tile(B - 1, 1, t)


def kv_phase(nc, h_src, wk, wv, bk, bv, ident_dram, xT_hi_d, xT_lo_d, kv_hi_d, kv_lo_d):
    KT = D // P
    VW = HD + 2
    with Semaphores(nc) as sems, ExitStack() as ctx:
        def sb(name, shape, dt=F32):
            return ctx.enter_context(nc.sbuf_tensor(f"kv_{name}", shape, dt))

        def sem(name):
            return sems.new(f"kv_{name}")

        ident = sb("ident", [P, P])
        w_raw = sb("w_raw", [P, 2, KT, D])
        w_hi = sb("w_hi", [P, 2, KT, D], F32R)
        w_lo = sb("w_lo", [P, 2, KT, D], F32R)
        bias = sb("bias", [TP, 2, D])
        h_in = sb("h_in", [TP, 2, BT, D])
        xn = sb("xn", [TP, 2, BT, D])
        x_hi = sb("x_hi", [P, 2, KT, BN], F32R)
        x_lo = sb("x_lo", [P, 2, KT, BN], F32R)
        kf = sb("kf", [TP, 2, D])
        ex = sb("ex", [TP, 2, D])
        vf = sb("vf", [TP, 2, D])
        k_hi = sb("k_hi", [TP, 2, BT, D], F32R)
        k_lo = sb("k_lo", [TP, 2, BT, D], F32R)
        v_hi = sb("v_hi", [TP, 2, BT, NKV, VW], F32R)
        v_lo = sb("v_lo", [TP, 2, BT, NKV, VW], F32R)
        kv_hi = sb("kv_hi", [P, 2, NKV, VW], F32R)
        kv_lo = sb("kv_lo", [P, 2, NKV, VW], F32R)
        st = sb("st", [TP, BT, 6])
        fence = sb("fence", [1, 2])
        mv = sb("mv", [TP, BT, 2])
        ve = sb("ve", [TP, BT])
        rs = sb("rs", [TP, BT])
        tmp = sb("tmp", [TP, BT])
        tp = ctx.enter_context(nc.psum_tensor("kv_tp", [P, 2, 512], F32))
        kp = ctx.enter_context(nc.psum_tensor("kv_kp", [P, 2, 2, 512], F32))
        kvp = ctx.enter_context(nc.psum_tensor("kv_kvp", [P, 2, 512], F32))

        const_in = sem("const_in")
        h_loaded = [sem("h_in0"), sem("h_in1")]
        x_out = [sem("x_out0"), sem("x_out1")]
        kv_out = [sem("kv_out0"), sem("kv_out1")]
        pads = sem("pads")
        whi_done = sem("whi_done")
        wlo_done = sem("wlo_done")
        var_done = sem("var_done")
        sqrt_done = sem("sqrt_done")
        xn_done = sem("xn_done")
        tr_full = sem("tr_full")
        xhi_done = sem("xhi_done")
        xlo_done = sem("xlo_done")
        k_full = sem("k_full")
        v_full = sem("v_full")
        kb_done = sem("kb_done")
        mn_done = sem("mn_done")
        ex_done = sem("ex_done")
        sk_done = sem("sk_done")
        vb_done = sem("vb_done")
        khi_done = sem("khi_done")
        vhi_done = sem("vhi_done")
        klo_done = sem("klo_done")
        vlo_done = sem("vlo_done")
        kv_full = sem("kv_full")
        kvhi_done = sem("kvhi_done")
        kvlo_done = sem("kvlo_done")
        bn_done = sem("bn_done")
        aggr_done = sem("aggr_done")
        chain = sem("chain")

        def sequences(eng, body):
            for b in range(2):
                body(b, b, True)
            with eng.Fori(2, B - 1, 2) as i:
                for par in range(2):
                    body(i + par, par, False)

        def sequence_steps(eng, step):
            step(0, 0)
            step(1, 1)
            with eng.Fori(2, B - 3, 2) as i:
                for par in range(2):
                    step(i + par, par)
            step(B - 2, 0)
            step(B - 1, 1, True)

        def at(d, b):
            return d[b] if isinstance(b, int) else d[bass.ds(b, 1)].squeeze(0)

        block = ctx.enter_context(nc.Block())

        def rows(b):
            r = h_src[b * (BT * TP):(b + 1) * (BT * TP), :] if isinstance(b, int) \
                else h_src[bass.ds(b * (BT * TP), BT * TP), :]
            return r.rearrange("(t p) d -> p t d", p=TP)

        @block.sync
        def _(sp):
            sp.dma_start(h_in[:, 0], rows(0)).then_inc(h_loaded[0], 16)
            sp.dma_start(ident[:], ident_dram).then_inc(const_in, 16)
            sp.dma_start(w_raw[:, 0], wk.rearrange("(k p) n -> p k n", p=P)).then_inc(const_in, 16)
            sp.dma_start(w_raw[:, 1], wv.rearrange("(k p) n -> p k n", p=P)).then_inc(const_in, 16)
            sp.dma_start(bias[:, 0, :], bk.partition_broadcast(TP)).then_inc(const_in, 16)
            sp.dma_start(bias[:, 1, :], bv.partition_broadcast(TP)).then_inc(const_in, 16)
            sp.dma_start(h_in[:, 1], rows(1)).then_inc(h_loaded[1], 16)
            with sp.Fori(2, B - 1, 2) as i:
                for par in range(2):
                    sp.wait_ge(xn_done, (i + (par - 1)) * BT)
                    sp.dma_start(h_in[:, par], rows(i + par)).then_inc(h_loaded[par], 16)

        @block.gpsimd
        def _(pool):
            nc.gpsimd.memset(x_hi[:, :, :, BT * TP:BN].bitcast(F32), 0.0).then_inc(pads, 1)
            nc.gpsimd.memset(x_lo[:, :, :, BT * TP:BN].bitcast(F32), 0.0).then_inc(pads, 1)
            nc.gpsimd.memset(v_hi[:, :, :, :, HD:VW].bitcast(F32), 1.0).then_inc(pads, 1)
            nc.gpsimd.memset(v_lo[:, :, :, :, HD:VW].bitcast(F32), 0.0).then_inc(pads, 1)
            pool.wait_ge(pads, 4)

            def body(b, par, first):
                pool.wait_ge(xlo_done, (b + 1) * KT)
                pool.dma_start(at(xT_hi_d, b), x_hi[:, par].bitcast(F32)).then_inc(x_out[par], 16)
                pool.dma_start(at(xT_lo_d, b), x_lo[:, par].bitcast(F32)).then_inc(x_out[par], 16)
                pool.wait_ge(kvlo_done, (b + 1) * 2)
                pool.dma_start(at(kv_hi_d, b), kv_hi[:, par].bitcast(F32)).then_inc(kv_out[par], 16)
                pool.dma_start(at(kv_lo_d, b), kv_lo[:, par].bitcast(F32)).then_inc(kv_out[par], 16)
            sequences(pool, body)
            for par in range(2):
                pool.wait_ge(x_out[par], 16 * B)
                pool.wait_ge(kv_out[par], 16 * B)

        @block.tensor
        def _(pe):
            pe.wait_ge(const_in, 80)
            pe.wait_ge(pads, 4)

            def transposes(u, par, ks):
                for k in ks:
                    if k == 0:
                        pe.wait_ge(xn_done, (u + 1) * BT)
                    if not (isinstance(u, int) and u == 0 and k < 2):
                        pe.wait_ge(xlo_done, u * KT + (k - 1))
                    for i in range(BT):
                        mm = pe.transpose(tp[:, k % 2, i * TP:(i + 1) * TP], xn[:, par, i, k * P:(k + 1) * P],
                                          ident[0:TP, 0:TP])
                    mm.then_inc(tr_full, 1)

            def project(b, par, i):
                if i == 0:
                    pe.wait_ge(xlo_done, (b + 1) * KT)
                n = b * BT + i
                bank = (par + i) % 2
                for j, free, full in ((0, kb_done, k_full), (1, vb_done, v_full)):
                    if not (isinstance(n, int) and n < 2):
                        pe.wait_ge(free, n - 1)
                    for k in range(KT):
                        tk = slice(i * TP, (i + 1) * TP)
                        mm = three(pe, kp[0:TP, bank, j, :], x_hi[:, par, k, tk], x_lo[:, par, k, tk],
                                   w_hi[:, j, k, :], w_lo[:, j, k, :], k == 0, k == KT - 1)
                    mm.then_inc(full, 1)

            def sums(b, par, first):
                pe.wait_ge(klo_done, (b + 1) * BT)
                pe.wait_ge(vlo_done, (b + 1) * BT)
                for g in range(NKV):
                    if g % 2 == 0 and not first:
                        pe.wait_ge(kvlo_done, b * 2 + (g // 2 - 1))
                    for i in range(BT):
                        hd = slice(g * HD, (g + 1) * HD)
                        mm = three(pe, kvp[:, g // 2, (g % 2) * VW:(g % 2 + 1) * VW], k_hi[:, par, i, hd],
                                   k_lo[:, par, i, hd], v_hi[:, par, i, g, :], v_lo[:, par, i, g, :],
                                   i == 0, i == BT - 1)
                    if g % 2:
                        mm.then_inc(kv_full, 1)

            transposes(0, 0, range(KT))
            pe.wait_ge(wlo_done, 2)

            def step(b, par, last=False):
                project(b, par, 0)
                project(b, par, 1)
                if not last:
                    transposes(b + 1, 1 - par, (0, 1))
                project(b, par, 2)
                if not last:
                    transposes(b + 1, 1 - par, (2, 3))
                if not (isinstance(b, int) and b == 0):
                    sums(b - 1, 1 - par, isinstance(b, int) and b == 1)
            sequence_steps(pe, step)
            sums(B - 1, (B - 1) % 2, False)

        @block.scalar
        def _(act):
            act.wait_ge(pads, 4)

            def root(u):
                act.wait_ge(var_done, u + 1)
                nc.scalar.activation(rs[:], ve[:], ACT.Sqrt).then_inc(sqrt_done, 1)

            def split_x(u, par, ks):
                if 0 in ks and not (isinstance(u, int) and u < 2):
                    act.wait_ge(x_out[par], (u - par) * 16)
                    act.wait_ge(v_full, (u - 1) * BT)
                for k in ks:
                    act.wait_ge(tr_full, u * KT + (k + 1))
                    nc.scalar.activation(x_hi[:, par, k, 0:BT * TP], tp[:, k % 2, 0:BT * TP],
                                         ACT.Copy).then_inc(xhi_done, 1)

            def project(b, par, i):
                if i == 0 and not (isinstance(b, int) and b < 2):
                    act.wait_ge(kv_full, (b - 1) * 2)
                n, z = b * BT + i, (par + i) % 2
                act.wait_ge(mn_done, n + 1)
                nc.scalar.activation(ex[:, z, :], ex[:, z, :], ACT.Exp).then_inc(ex_done, 1)
                act.wait_ge(sk_done, n + 1)
                nc.scalar.activation(k_hi[:, par, i, :], kf[:, z, :], ACT.Copy).then_inc(khi_done, 1)
                act.wait_ge(vb_done, n + 1)
                nc.scalar.activation(v_hi[:, par, i, :, 0:HD], vf[:, z, :].rearrange("p (g d) -> p g d", d=HD),
                                     ACT.Copy).then_inc(vhi_done, 1)

            def sums(b, par, first):
                if not first:
                    act.wait_ge(kv_out[par], (b - par) * 16)
                for c in range(2):
                    act.wait_ge(kv_full, b * 2 + (c + 1))
                    nc.scalar.activation(kv_hi[:, par, 2 * c:2 * c + 2, :],
                                         kvp[:, c, 0:2 * VW].rearrange("p (g d) -> p g d", d=VW),
                                         ACT.Copy).then_inc(kvhi_done, 1)

            root(0)
            split_x(0, 0, range(KT))
            act.wait_ge(const_in, 80)
            for j in range(2):
                nc.scalar.activation(w_hi[:, j], w_raw[:, j], ACT.Copy).then_inc(whi_done, 1)

            def step(b, par, last=False):
                if not last:
                    root(b + 1)
                project(b, par, 0)
                project(b, par, 1)
                if not last:
                    split_x(b + 1, 1 - par, (0, 1))
                project(b, par, 2)
                if not last:
                    split_x(b + 1, 1 - par, (2, 3))
                if not (isinstance(b, int) and b == 0):
                    sums(b - 1, 1 - par, isinstance(b, int) and b < 3)
            sequence_steps(act, step)
            sums(B - 1, (B - 1) % 2, False)

        @block.vector
        def _(dve):
            link = Link(dve, chain)

            def statistics(b, par):
                dve.wait_ge(h_loaded[par], (b - par) * 8 + 16)
                for i in range(BT):
                    nc.vector.bn_stats(st[:, i, :], h_in[:, par, i, :]).then_inc(bn_done, 1)
                for i in range(BT):
                    if i == 0:
                        dve.wait_ge(bn_done, (b + 1) * BT)
                        nc.vector.memset(fence[:, par:par + 1], 0.0)
                    nc.vector.bn_aggr(mv[:, i, :], st[:, i, :]).then_inc(aggr_done, 1)
                dve.wait_ge(aggr_done, (b + 1) * BT)
                nc.vector.tensor_scalar(ve[:], mv[:, :, 1], 1e-5, None, ALU.add).then_inc(var_done, 1)

            def normalise(b, par):
                link.start(b * NEWTON)
                dve.wait_ge(sqrt_done, b + 1)
                rstd_newton(link, nc.vector, ve[:], rs[:], tmp[:])
                if not (isinstance(b, int) and b < 2):
                    dve.wait_ge(tr_full, (b - 1) * KT)
                for i in range(BT):
                    nc.vector.tensor_scalar(xn[:, par, i, :], h_in[:, par, i, :], mv[:, i, 0:1], rs[:, i:i + 1],
                                            ALU.subtract, ALU.mult).then_inc(xn_done, 1)

            def split_x(b, par, ks):
                for k in ks:
                    dve.wait_ge(xhi_done, b * KT + (k + 1))
                    nc.vector.tensor_tensor(x_lo[:, par, k, 0:BT * TP], tp[:, k % 2, 0:BT * TP],
                                            x_hi[:, par, k, 0:BT * TP].bitcast(F32),
                                            ALU.subtract).then_inc(xlo_done, 1)

            def project(b, par, i):
                n, z = b * BT + i, (par + i) % 2
                early = isinstance(n, int) and n < 2
                dve.wait_ge(k_full, n + 1)
                if not early:
                    dve.wait_ge(klo_done, n - 1)
                nc.vector.tensor_tensor(kf[:, z, :], kp[0:TP, z, 0, :], bias[:, 0, :], ALU.add).then_inc(kb_done, 1)
                dve.wait_ge(kb_done, n + 1)
                nc.vector.tensor_scalar(ex[:, z, :], kf[:, z, :], 0.0, None, ALU.min).then_inc(mn_done, 1)
                dve.wait_ge(v_full, n + 1)
                if not early:
                    dve.wait_ge(vlo_done, n - 1)
                nc.vector.tensor_tensor(vf[:, z, :], kp[0:TP, z, 1, :], bias[:, 1, :], ALU.add).then_inc(vb_done, 1)
                dve.wait_ge(ex_done, n + 1)
                nc.vector.scalar_tensor_tensor(out=kf[:, z, :], in0=kf[:, z, :], scalar=0.0, in1=ex[:, z, :],
                                               op0=ALU.max, op1=ALU.add).then_inc(sk_done, 1)
                dve.wait_ge(khi_done, n + 1)
                nc.vector.tensor_tensor(k_lo[:, par, i, :], kf[:, z, :], k_hi[:, par, i, :].bitcast(F32),
                                        ALU.subtract).then_inc(klo_done, 1)
                dve.wait_ge(vhi_done, n + 1)
                nc.vector.tensor_tensor(v_lo[:, par, i, :, 0:HD], vf[:, z, :].rearrange("p (g d) -> p g d", d=HD),
                                        v_hi[:, par, i, :, 0:HD].bitcast(F32),
                                        ALU.subtract).then_inc(vlo_done, 1)

            def sums(b, par, first):
                for c in range(2):
                    dve.wait_ge(kvhi_done, b * 2 + (c + 1))
                    nc.vector.tensor_tensor(kv_lo[:, par, 2 * c:2 * c + 2, :],
                                            kvp[:, c, 0:2 * VW].rearrange("p (g d) -> p g d", d=VW),
                                            kv_hi[:, par, 2 * c:2 * c + 2, :].bitcast(F32),
                                            ALU.subtract).then_inc(kvlo_done, 1)

            statistics(0, 0)
            normalise(0, 0)
            split_x(0, 0, range(KT))
            for j in range(2):
                dve.wait_ge(whi_done, j + 1)
                nc.vector.tensor_tensor(w_lo[:, j], w_raw[:, j], w_hi[:, j].bitcast(F32),
                                        ALU.subtract).then_inc(wlo_done, 1)

            def step(b, par, last=False):
                if not last:
                    statistics(b + 1, 1 - par)
                project(b, par, 0)
                if not last:
                    normalise(b + 1, 1 - par)
                project(b, par, 1)
                if not last:
                    split_x(b + 1, 1 - par, (0, 1))
                project(b, par, 2)
                if not last:
                    split_x(b + 1, 1 - par, (2, 3))
                if not (isinstance(b, int) and b == 0):
                    sums(b - 1, 1 - par, False)
            sequence_steps(dve, step)
            sums(B - 1, (B - 1) % 2, False)


def query_phase(nc, h_src, wq, wo, bq, ident_dram, xT_hi_d, xT_lo_d, kv_hi_d, kv_lo_d, dst):
    KT = D // P
    VW = HD + 2
    PIECE = 1024
    QH, OH = PIECE // HD, PIECE // D
    START = [("q", 0, k) for k in range(KT)]
    LATER = [("o", 0), ("o", 1), ("q", 1, 0), ("q", 1, 1), ("o", 2), ("q", 1, 2), ("q", 1, 3)] + \
        [("o", i) for i in range(3, NH // OH)]
    PIECES = START + LATER
    with Semaphores(nc) as sems, ExitStack() as ctx:
        def sb(name, shape, dt=F32):
            return ctx.enter_context(nc.sbuf_tensor(f"q_{name}", shape, dt))

        def sem(name):
            return sems.new(f"q_{name}")

        ident = sb("ident", [P, P])
        raw = sb("raw", [P, 2, PIECE])
        wq_hi = sb("wq_hi", [P, KT, NH * HD], F32R)
        wq_lo = sb("wq_lo", [P, KT, NH * HD], F32R)
        wo_hi = sb("wo_hi", [P, NH, D], F32R)
        wo_lo = sb("wo_lo", [P, NH, D], F32R)
        bias = sb("bias", [P, NH])
        x_hi = sb("x_hi", [P, 2, KT, BN], F32R)
        x_lo = sb("x_lo", [P, 2, KT, BN], F32R)
        kv_hi = sb("kv_hi", [P, 2, NKV, VW], F32R)
        kv_lo = sb("kv_lo", [P, 2, NKV, VW], F32R)
        res = sb("res", [TP, 2, BT, D])
        rel = sb("rel", [P, 2, BN])
        ex = sb("ex", [P, 2, BN])
        q_hi = sb("q_hi", [P, 2, BN], F32R)
        q_lo = sb("q_lo", [P, 2, BN], F32R)
        rn = sb("rn", [TP, BT, 1])
        at = sb("at", [TP, 2, BT, HD])
        a_hi = sb("a_hi", [P, 2, BN], F32R)
        a_lo = sb("a_lo", [P, 2, BN], F32R)
        qp = ctx.enter_context(nc.psum_tensor("q_qp", [P, 2, 512], F32))
        op = ctx.enter_context(nc.psum_tensor("q_op", [P, 512], F32))
        tp = ctx.enter_context(nc.psum_tensor("q_tp", [P, 512], F32))
        wp = ctx.enter_context(nc.psum_tensor("q_wp", [P, BT, 512], F32))

        const_in = sem("const_in")
        w_in = [sem("w_in0"), sem("w_in1")]
        b_in = [sem("b_in0"), sem("b_in1")]
        stored = [sem("stored0"), sem("stored1")]
        whi_done = sem("whi_done")
        wlo_done = sem("wlo_done")
        q_full = sem("q_full")
        rel_done = sem("rel_done")
        mn_done = sem("mn_done")
        ex_done = sem("ex_done")
        sq_done = sem("sq_done")
        qhi_done = sem("qhi_done")
        qlo_done = sem("qlo_done")
        o_full = sem("o_full")
        at_done = sem("at_done")
        tr_full = sem("tr_full")
        ahi_done = sem("ahi_done")
        alo_done = sem("alo_done")
        wo_full = sem("wo_full")
        res_done = sem("res_done")
        chain = sem("chain")

        STEPS = 2 * NH
        SKEW = 3

        def steps(eng, body):
            for l in range(STEPS):
                body(0, l, True)
            with eng.Fori(STEPS, B * NH, STEPS) as n0:
                for l in range(STEPS):
                    body(n0, l, False)
            for l in range(SKEW):
                body(B * NH, l, None)

        def head(l):
            l = l % STEPS
            return l // NH, l % NH, l % 2

        def at_seq(d, b):
            return d[b] if isinstance(b, int) else d[bass.ds(b, 1)].squeeze(0)

        def rows(d, b):
            r = d[b * (BT * TP):(b + 1) * (BT * TP), :] if isinstance(b, int) \
                else d[bass.ds(b * (BT * TP), BT * TP), :]
            return r.rearrange("(t p) d -> p t d", p=TP)

        block = ctx.enter_context(nc.Block())

        wo_v = wo.rearrange("(h p) n -> p h n", p=P)

        def piece(i):
            kind, c, *k = PIECES[i]
            if kind == "q":
                cols = slice(c * PIECE, (c + 1) * PIECE)
                return wq[k[0] * P:(k[0] + 1) * P, cols], raw[:, i % 2, :], wq_hi[:, k[0], cols], wq_lo[:, k[0], cols]
            hs = slice(c * OH, (c + 1) * OH)
            return wo_v[:, hs, :], raw[:, i % 2, :].rearrange("p (h n) -> p h n", n=D), wo_hi[:, hs, :], wo_lo[:, hs, :]

        @block.sync
        def _(sp):
            def load(b, par):
                for d, s in ((xT_hi_d, x_hi), (xT_lo_d, x_lo), (kv_hi_d, kv_hi), (kv_lo_d, kv_lo)):
                    sp.dma_start(s[:, par].bitcast(F32), at_seq(d, b)).then_inc(b_in[par], 16)
                sp.dma_start(res[:, par], rows(h_src, b)).then_inc(b_in[par], 16)

            sp.dma_start(ident[:], ident_dram).then_inc(const_in, 16)
            sp.dma_start(bias[:], bq).then_inc(const_in, 16)
            for i in range(len(PIECES)):
                if i == 2:
                    load(0, 0)
                if i >= 2:
                    sp.wait_ge(wlo_done, i - 1)
                sp.dma_start(piece(i)[1], piece(i)[0]).then_inc(w_in[i % 2], 16)
            load(1, 1)
            with sp.Fori(2, B - 1, 2) as b:
                for par in range(2):
                    sp.wait_ge(stored[par], b * 8)
                    load(b + par, par)

        @block.gpsimd
        def _(pool):
            with pool.Fori(0, B - 1, 2) as b:
                for par in range(2):
                    pool.wait_ge(res_done, (b + (par + 1)) * BT)
                    pool.dma_start(rows(dst, b + par), res[:, par]).then_inc(stored[par], 16)
            for par in range(2):
                pool.wait_ge(stored[par], 8 * B)

        @block.tensor
        def _(pe):
            pe.wait_ge(const_in, 32)
            def body(n0, l, new):
                if new is not None:
                    s, h, z = head(l)
                    if h == 0:
                        pe.wait_ge(b_in[s], n0 * (5 * 16) // (2 * NH) + 80 if isinstance(n0, int) else
                                   (n0 // (2 * NH)) * 80 + 80)
                    if not (new and l < 2):
                        pe.wait_ge(mn_done, n0 + (l - 1))
                        pe.wait_ge(rel_done, n0 + (l - 1))
                    if new and l < NH and h % QH == 0:
                        pe.wait_ge(wlo_done, PIECES.index(("q", h // QH, KT - 1)) + 1)
                    for k in range(KT):
                        hd = slice(h * HD, (h + 1) * HD)
                        mm = three(pe, qp[:, z, 0:BN], wq_hi[:, k, hd], wq_lo[:, k, hd], x_hi[:, s, k, :],
                                   x_lo[:, s, k, :], k == 0, k == KT - 1)
                    mm.then_inc(q_full, 1)
                if not (new and l < 1) and not (new is None and l >= 1):
                    s, h, z = head(l - 1)
                    pe.wait_ge(qlo_done, n0 + l)
                    if not (new and l < 2):
                        pe.wait_ge(at_done, n0 + (l - 1))
                    for i in range(BT):
                        tk = slice(i * TP, (i + 1) * TP)
                        mm = three(pe, op[0:TP, i * VW:(i + 1) * VW], q_hi[:, z, tk], q_lo[:, z, tk],
                                   kv_hi[:, s, h // (NH // NKV), :], kv_lo[:, s, h // (NH // NKV), :], True, True)
                    mm.then_inc(o_full, 1)
                if not (new and l < 2) and not (new is None and l >= 2):
                    s, h, z = head(l - 2)
                    pe.wait_ge(at_done, n0 + (l - 1))
                    if not (new and l < 3):
                        pe.wait_ge(alo_done, n0 + (l - 2))
                    for i in range(BT):
                        mm = pe.transpose(tp[:, i * TP:(i + 1) * TP], at[:, z, i, :], ident[0:TP, 0:TP])
                    mm.then_inc(tr_full, 1)
                if not (new and l < 3):
                    s, h, z = head(l - 3)
                    pe.wait_ge(alo_done, n0 + (l - 2))
                    if new and l - 3 < NH and h % OH == 0:
                        pe.wait_ge(wlo_done, PIECES.index(("o", h // OH)) + 1)
                    if h == 0 and not (new and l < NH):
                        pe.wait_ge(res_done, 3 * ((l - 3) // NH) if isinstance(n0, int) and n0 == 0 else
                                   (n0 // NH) * BT + BT * ((l - 3) // NH))
                    for i in range(BT):
                        tk = slice(i * TP, (i + 1) * TP)
                        mm = three(pe, wp[0:TP, i, :], a_hi[:, z, tk], a_lo[:, z, tk], wo_hi[:, h, :],
                                   wo_lo[:, h, :], h == 0, h == NH - 1)
                    mm.then_inc(wo_full, 1)
            steps(pe, body)

        @block.scalar
        def _(act):
            act.wait_ge(const_in, 32)

            def split(i):
                act.wait_ge(w_in[i % 2], 16 * (i // 2 + 1))
                nc.scalar.activation(piece(i)[2], piece(i)[1], ACT.Copy).then_inc(whi_done, 1)
            for i in range(len(START)):
                split(i)

            def body(n0, l, new):
                if new is not None:
                    s, h, z = head(l)
                    act.wait_ge(q_full, n0 + (l + 1))
                    if not (new and l < 2):
                        act.wait_ge(qlo_done, n0 + (l - 1))
                    nc.scalar.activation(rel[:, z, :], qp[:, z, 0:BN], ACT.Relu, bias=bias[:, h:h + 1]).then_inc(rel_done, 1)
                    act.wait_ge(mn_done, n0 + (l + 1))
                    nc.scalar.activation(ex[:, z, :], ex[:, z, :], ACT.Exp).then_inc(ex_done, 1)
                    act.wait_ge(sq_done, n0 + (l + 1))
                    if not (new and l < 2):
                        act.wait_ge(o_full, n0 + (l - 1))
                    nc.scalar.activation(q_hi[:, z, :], rel[:, z, :], ACT.Copy).then_inc(qhi_done, 1)
                if not (new and l < 2) and not (new is None and l >= 2):
                    s, h, z = head(l - 2)
                    act.wait_ge(tr_full, n0 + (l - 1))
                    if not (new and l < 4):
                        act.wait_ge(wo_full, n0 + (l - 3))
                    nc.scalar.activation(a_hi[:, z, 0:BT * TP], tp[:, 0:BT * TP], ACT.Copy).then_inc(ahi_done, 1)
                if new and l < len(LATER):
                    split(len(START) + l)
            steps(act, body)

        @block.vector
        def _(dve):
            def split(i):
                dve.wait_ge(whi_done, i + 1)
                _, src, hi, lo = piece(i)
                nc.vector.tensor_tensor(lo, src, hi.bitcast(F32), ALU.subtract).then_inc(wlo_done, 1)
            for i in range(len(START)):
                split(i)
            dve.wait_ge(const_in, 32)
            link = Link(dve, chain)

            def body(n0, l, new):
                if new is not None:
                    s, h, z = head(l)
                    dve.wait_ge(rel_done, n0 + (l + 1))
                    if not (new and l < 2):
                        dve.wait_ge(sq_done, n0 + (l - 1))
                    nc.vector.tensor_scalar(ex[:, z, :], qp[:, z, 0:BN], bias[:, h:h + 1], 0.0, ALU.add,
                                            ALU.min).then_inc(mn_done, 1)
                    dve.wait_ge(ex_done, n0 + (l + 1))
                    nc.vector.tensor_tensor(rel[:, z, :], rel[:, z, :], ex[:, z, :], ALU.add).then_inc(sq_done, 1)
                    dve.wait_ge(qhi_done, n0 + (l + 1))
                    nc.vector.tensor_tensor(q_lo[:, z, :], rel[:, z, :], q_hi[:, z, :].bitcast(F32),
                                            ALU.subtract).then_inc(qlo_done, 1)
                if not (new and l < 1) and not (new is None and l >= 1):
                    s, h, z = head(l - 1)
                    dve.wait_ge(o_full, n0 + l)
                    if not (new and l < 3):
                        dve.wait_ge(tr_full, n0 + (l - 2))
                    link.start((n0 + (l - 1)) * 2)
                    o3 = op[0:TP, 0:BT * VW].rearrange("p (t v) -> p t v", v=VW)
                    link(nc.vector.tensor_scalar(rn[:], o3[:, :, HD:HD + 1], 1e-6, None, ALU.add))
                    link(nc.vector.reciprocal(rn[:], rn[:]))
                    nc.vector.tensor_tensor(at[:, z], o3[:, :, 0:HD], rn[:].broadcast_to((TP, BT, HD)),
                                            ALU.mult).then_inc(at_done, 1)
                if not (new and l < 2) and not (new is None and l >= 2):
                    s, h, z = head(l - 2)
                    dve.wait_ge(ahi_done, n0 + (l - 1))
                    nc.vector.tensor_tensor(a_lo[:, z, 0:BT * TP], tp[:, 0:BT * TP],
                                            a_hi[:, z, 0:BT * TP].bitcast(F32), ALU.subtract).then_inc(alo_done, 1)
                if not (new and l < 3):
                    s, h, z = head(l - 3)
                    if h == NH - 1:
                        dve.wait_ge(wo_full, n0 + (l - 2))
                        for i in range(BT):
                            nc.vector.tensor_tensor(res[:, s, i, :], wp[0:TP, i, :], res[:, s, i, :],
                                                    ALU.add).then_inc(res_done, 1)
                if new and l < len(LATER):
                    split(len(START) + l)
            steps(dve, body)


def expert_phase(nc, xn_d, w1, w2, routes, ident_dram, upper_dram, ids_d, y_d):
    KT = D // P
    H = w2.shape[1]
    HS = [min(P, H - j) for j in range(0, H, P)]
    HT = len(HS)
    UH = UNIT // P
    MAXC = -(-T // UNIT)
    with Semaphores(nc) as sems, ExitStack() as ctx:
        def sb(name, shape, dt=F32):
            return ctx.enter_context(nc.sbuf_tensor(f"ex_{name}", shape, dt))

        def sem(name):
            return sems.new(f"ex_{name}")

        ident = sb("ident", [P, P])
        upper = sb("upper", [TP, TP])
        ones = sb("ones", [TP, TP])
        both = sb("both", [TP, NT, E])
        tot = sb("tot", [TP, NT, E])
        cum = sb("cum", [TP, 2, NT, E])
        slotmap = sb("slotmap", [TP, NT, E])
        thr = sb("thr", [TP, MAXC])
        over = sb("over", [TP, E, MAXC])
        units = sb("units", [TP, E])
        uinc = sb("uinc", [TP, 2, E])
        uiota = sb("uiota", [TP, NU])
        uge = sb("uge", [TP, NU, E])
        uexp = sb("uexp", [TP, NU])
        uexp_i = sb("uexp_i", [TP, NU], I32)
        slot_f = sb("slot_f", [TP, NT])
        tok_id = sb("tok_id", [TP, NT], I32)
        zero_i = sb("zero_i", [P, NU * UH], I32)
        fence = sb("fence", [1, 2])
        ids = sb("ids", [P, 2, UH], I32)
        xg = sb("xg", [P, 2, UH, D])
        x_hi = sb("x_hi", [P, 2, KT, UNIT], F32R)
        x_lo = sb("x_lo", [P, 2, KT, UNIT], F32R)
        w1_raw = sb("w1_raw", [P, 2, KT, 2 * H])
        w2_raw = sb("w2_raw", [P, 2, HT, D])
        w1_hi = sb("w1_hi", [P, 2, KT, 2 * H], F32R)
        w1_lo = sb("w1_lo", [P, 2, KT, 2 * H], F32R)
        w2_hi = sb("w2_hi", [P, 2, HT, D], F32R)
        w2_lo = sb("w2_lo", [P, 2, HT, D], F32R)
        sil = sb("sil", [P, 2, UNIT])
        hid = sb("hid", [P, 2, UNIT])
        h_hi = sb("h_hi", [P, 2, HT, UNIT], F32R)
        h_lo = sb("h_lo", [P, 2, HT, UNIT], F32R)
        y = sb("y", [P, 2, UH, D])
        gu = ctx.enter_context(nc.psum_tensor("ex_gu", [P, 2, 2, UNIT], F32))
        tp = ctx.enter_context(nc.psum_tensor("ex_tp", [P, 2, 2, UNIT], F32))
        dn = ctx.enter_context(nc.psum_tensor("ex_dn", [P, 2, UH, D], F32))

        const_in = sem("const_in")
        tables = sem("tables")
        sums_full = sem("sums_full")
        table_done = sem("table_done")
        slots_done = sem("slots_done")
        ids_zero = sem("ids_zero")
        ids_out = sem("ids_out")
        fenced = sem("fenced")
        ids_in = [sem("ids_in0"), sem("ids_in1")]
        x_in = [sem("x_in0"), sem("x_in1")]
        w_in = [sem("w_in0"), sem("w_in1")]
        y_out = [sem("y_out0"), sem("y_out1")]
        tr_full = sem("tr_full")
        xhi_done = sem("xhi_done")
        xlo_done = sem("xlo_done")
        w1hi_done = sem("w1hi_done")
        w1lo_done = sem("w1lo_done")
        w2hi_done = sem("w2hi_done")
        w2lo_done = sem("w2lo_done")
        gu_full = sem("gu_full")
        sil_done = sem("sil_done")
        h_done = sem("h_done")
        hhi_done = sem("hhi_done")
        hlo_done = sem("hlo_done")
        dn_full = sem("dn_full")
        y_done = sem("y_done")
        chain = sem("chain")

        def loop(eng, body):
            body(0, 0, True)
            body(1, 1, True)
            with eng.Fori(2, NU - 1 if NU % 2 else NU, 2) as i:
                for par in range(2):
                    body(i + par, par, False)
            if NU % 2:
                body(NU - 1, 0, False)

        block = ctx.enter_context(nc.Block())

        def half_rows(d, u):
            r = d[u * UNIT:(u + 1) * UNIT, :] if isinstance(u, int) else d[bass.ds(u * UNIT, UNIT), :]
            return r.rearrange("(p h) d -> p h d", p=P)

        @block.sync
        def _(sp):
            sp.dma_start(ident[:], ident_dram).then_inc(const_in, 16)
            sp.dma_start(upper[:], upper_dram[0:TP, 0:TP]).then_inc(const_in, 16)
            sp.wait_ge(tables, 5)
            sp.dma_start(ids_d.rearrange("(p a) o -> p (a o)", p=P), zero_i[:]).then_inc(ids_zero, 16)
            sp.wait_ge(table_done, 1)

            def load(u, par):
                at = uexp_i[0:1, u:u + 1] if isinstance(u, int) else uexp_i[0:1, bass.ds(u, 1)]
                e = sp.value_load(at, min_val=0, max_val=E - 1)
                sp.dma_start(w1_raw[:, par], w1[bass.ds(e, 1)].rearrange("o (k p) n -> p (o k) n", p=P))\
                  .then_inc(w_in[par], 16)
                w2e = w2[bass.ds(e, 1)].rearrange("o h n -> (o h) n")
                full = H // P
                sp.dma_start(w2_raw[:, par, 0:full, :], w2e[0:full * P, :].rearrange("(j p) n -> p j n", p=P))\
                  .then_inc(w_in[par], 16)
                sp.dma_start(w2_raw[0:H % P, par, full, :], w2e[full * P:H, :]).then_inc(w_in[par], 16)

            load(0, 0)
            load(1, 1)

            def body(u, par, first):
                sp.wait_ge(w2lo_done, (u + 1) * HT)
                load(u + 2, par)
            body(0, 0, True)
            with sp.Fori(1, NU - 3, 2) as i:
                for j in range(2):
                    body(i + j, (1 + j) % 2, False)
            for u in range(NU - 2 - (NU - 3) % 2, NU - 2):
                body(u, u % 2, False)

        @block.gpsimd
        def _(pool):
            nc.gpsimd.memset(ones[:], 1.0).then_inc(tables, 1)
            nc.gpsimd.iota(thr[:], pattern=[[UNIT, MAXC]], base=0, channel_multiplier=0,
                           allow_small_or_imprecise_dtypes=True).then_inc(tables, 1)
            nc.gpsimd.iota(uiota[:], pattern=[[1, NU]], base=0, channel_multiplier=0,
                           allow_small_or_imprecise_dtypes=True).then_inc(tables, 1)
            nc.gpsimd.iota(tok_id[:], pattern=[[TP, NT]], base=0, channel_multiplier=1).then_inc(tables, 1)
            nc.gpsimd.memset(zero_i[:], 0).then_inc(tables, 1)
            nc.gpsimd.memset(fence[:], 0.0).then_inc(tables, 1)
            pool.wait_ge(tables, 6)
            pool.wait_ge(slots_done, 2)
            pool.wait_ge(ids_zero, 16)
            for r in range(2):
                for i in range(NT):
                    pool.indirect_dma_start(ids_d, bass.IndirectOffsetOnAxis(ap=routes["slot"][:, r, i:i + 1], axis=0),
                                            tok_id[:, i:i + 1], None).then_inc(ids_out, 16)
            pool.wait_ge(ids_out, 16 * 2 * NT)

            def body(u, par, first):
                if not first:
                    pool.wait_ge(x_in[par], (u - par) * (16 * UH // 2))
                pool.dma_start(ids[:, par, :], half_rows(ids_d, u).rearrange("p h o -> p (h o)")).then_inc(ids_in[par], 16)
                if not first:
                    pool.wait_ge(tr_full, (u - 1) * 2)
                pool.wait_ge(ids_in[par], (u - par) * 8 + 16)
                if not (first and u == 0):
                    pool.wait_ge(fenced, u)
                nc.gpsimd.tensor_tensor(fence[:, 0:1], fence[:, 1:2], fence[:, 1:2], ALU.add).then_inc(fenced, 1)
                for h in range(UH):
                    pool.indirect_dma_start(xg[:, par, h, :], None, xn_d,
                                            bass.IndirectOffsetOnAxis(ap=ids[:, par, h:h + 1], axis=0))\
                        .then_inc(x_in[par], 16)
            loop(pool, body)

        @block.tensor
        def _(pe):
            pe.wait_ge(const_in, 32)
            pe.wait_ge(tables, 6)
            pe.wait_ge(chain, 1)
            flat = both[:].rearrange("p t e -> p (t e)")
            pe.matmul(dn[0:TP, 0, 0, 0:NT * E], upper[:], flat, start=True, stop=True)
            pe.matmul(dn[0:TP, 0, 1, 0:NT * E], ones[:], flat, start=True, stop=True).then_inc(sums_full, 1)
            pe.wait_ge(slots_done, 2)

            def transposes(u, par, first):
                pe.wait_ge(x_in[par], (u - par) * (16 * UH // 2) + 16 * UH)
                for kk in range(KT // 2):
                    if not (first and u == 0):
                        pe.wait_ge(xlo_done, (u - 1) * (KT // 2) + (kk + 1))
                    for k in range(2):
                        for h in range(UH):
                            kc = (2 * kk + k) * P
                            mm = pe.transpose(tp[:, kk, k, h * P:(h + 1) * P], xg[:, par, h, kc:kc + P], ident[:])
                    mm.then_inc(tr_full, 1)

            def gate_up(u, par, first):
                pe.wait_ge(w1lo_done, (u + 1) * KT)
                pe.wait_ge(xlo_done, (u + 1) * (KT // 2))
                for j, hs in enumerate(HS):
                    m, mpar = u * HT + j, (par + j) % 2
                    pe.wait_ge(h_done, m + 1)
                    for half in range(2):
                        for k in range(KT):
                            wc = slice(half * H + j * P, half * H + j * P + hs)
                            mm = three(pe, gu[0:hs, mpar, half, :], w1_hi[:, par, k, wc], w1_lo[:, par, k, wc],
                                       x_hi[:, par, k, :], x_lo[:, par, k, :], k == 0, k == KT - 1)
                    mm.then_inc(gu_full, 1)

            def down(u, par, first):
                pe.wait_ge(w2lo_done, (u + 1) * HT)
                pe.wait_ge(hlo_done, (u + 1) * HT + 2)
                if not first:
                    pe.wait_ge(y_done, (u - 1) * UH)
                for t in range(UH):
                    for j, hs in enumerate(HS):
                        tk = slice(t * P, (t + 1) * P)
                        mm = three(pe, dn[:, par, t, :], h_hi[0:hs, par, j, tk], h_lo[0:hs, par, j, tk],
                                   w2_hi[0:hs, par, j, :], w2_lo[0:hs, par, j, :], j == 0, j == HT - 1)
                    mm.then_inc(dn_full, 1)

            transposes(0, 0, True)
            gate_up(0, 0, True)
            transposes(1, 1, True)
            gate_up(1, 1, True)
            transposes(2, 0, False)
            down(0, 0, True)
            gate_up(2, 0, False)
            transposes(3, 1, False)
            down(1, 1, True)
            with pe.Fori(3, NU - 2, 2) as i:
                for j in range(2):
                    par = (1 + j) % 2
                    gate_up(i + j, par, False)
                    transposes(i + (j + 1), 1 - par, False)
                    down(i + (j - 1), 1 - par, False)
            for u in range(NU - 1 - (NU - 4) % 2, NU):
                gate_up(u, u % 2, False)
                if u + 1 < NU:
                    transposes(u + 1, (u + 1) % 2, False)
                down(u - 1, (u - 1) % 2, False)
            down(NU - 1, (NU - 1) % 2, False)

        def split_x(eng, u, par, first, act):
            if act and not first:
                eng.wait_ge(gu_full, (u - 1) * HT)
            for kk in range(KT // 2):
                src, hi, lo = tp[:, kk], x_hi[:, par, 2 * kk:2 * kk + 2, :], x_lo[:, par, 2 * kk:2 * kk + 2, :]
                if act:
                    eng.wait_ge(tr_full, u * (KT // 2) + (kk + 1))
                    nc.scalar.activation(hi, src, ACT.Copy).then_inc(xhi_done, 1)
                else:
                    eng.wait_ge(xhi_done, u * (KT // 2) + (kk + 1))
                    nc.vector.tensor_tensor(lo, src, hi.bitcast(F32), ALU.subtract).then_inc(xlo_done, 1)

        def split_w1(eng, u, par, first, act, pieces):
            if act and 0 in pieces:
                eng.wait_ge(w_in[par], (u - par) * 24 + 48)
                if not first:
                    eng.wait_ge(gu_full, (u - 1) * HT)
            for k in pieces:
                raw, hi, lo = w1_raw[:, par, k, :], w1_hi[:, par, k, :], w1_lo[:, par, k, :]
                if act:
                    nc.scalar.activation(hi, raw, ACT.Copy).then_inc(w1hi_done, 1)
                else:
                    eng.wait_ge(w1hi_done, u * KT + (k + 1))
                    nc.vector.tensor_tensor(lo, raw, hi.bitcast(F32), ALU.subtract).then_inc(w1lo_done, 1)

        def split_w2(eng, u, par, first, act):
            if act:
                eng.wait_ge(w_in[par], (u - par) * 24 + 48)
                if not first:
                    eng.wait_ge(dn_full, (u - 1) * UH)
            for j, hs in enumerate(HS):
                raw, hi, lo = w2_raw[0:hs, par, j, :], w2_hi[0:hs, par, j, :], w2_lo[0:hs, par, j, :]
                if act:
                    nc.scalar.activation(hi, raw, ACT.Copy).then_inc(w2hi_done, 1)
                else:
                    eng.wait_ge(w2hi_done, u * HT + (j + 1))
                    nc.vector.tensor_tensor(lo, raw, hi.bitcast(F32), ALU.subtract).then_inc(w2lo_done, 1)

        def hidden(eng, u, par, first, act, between):
            for j, hs in enumerate(HS):
                m, mpar = u * HT + j, (par + j) % 2
                if act:
                    eng.wait_ge(gu_full, m + 1)
                    eng.wait_ge(h_done, m + 1)
                    nc.scalar.activation(sil[0:hs, mpar, :], gu[0:hs, mpar, 0, :], ACT.Silu).then_inc(sil_done, 1)
                    between(2 * j)
                    eng.wait_ge(h_done, m + 3)
                    if j == 0 and not first:
                        eng.wait_ge(dn_full, (u - 1) * UH)
                    nc.scalar.activation(h_hi[0:hs, par, j, :], hid[0:hs, mpar, :], ACT.Copy).then_inc(hhi_done, 1)
                    between(2 * j + 1)
                else:
                    eng.wait_ge(sil_done, m + 1)
                    eng.wait_ge(hlo_done, m + 1)
                    nc.vector.tensor_tensor(hid[0:hs, mpar, :], sil[0:hs, mpar, :], gu[0:hs, mpar, 1, :],
                                            ALU.mult).then_inc(h_done, 1)
                    between(2 * j)
                    eng.wait_ge(hhi_done, m + 1)
                    nc.vector.tensor_tensor(h_lo[0:hs, par, j, :], hid[0:hs, mpar, :],
                                            h_hi[0:hs, par, j, :].bitcast(F32), ALU.subtract).then_inc(hlo_done, 1)
                    between(2 * j + 1)

        def store(eng, u, par, first, act):
            if act:
                for t in range(UH):
                    eng.wait_ge(dn_full, u * UH + (t + 1))
                    if t == 0 and not first:
                        eng.wait_ge(y_out[par], (u - par) * 8)
                    nc.scalar.activation(y[:, par, t, :], dn[:, par, t, :], ACT.Copy).then_inc(y_done, 1)
                eng.wait_ge(y_done, (u + 1) * UH)
                eng.dma_start(half_rows(y_d, u), y[:, par]).then_inc(y_out[par], 16)

        def schedule(eng, act):
            split_w1(eng, 0, 0, True, act, range(KT))
            split_w2(eng, 0, 0, True, act)
            split_x(eng, 0, 0, True, act)

            def body(u, par, first, firsts, last=False):
                def between(i):
                    if not last and i < KT:
                        split_w1(eng, u + 1, 1 - par, first, act, [i])
                hidden(eng, u, par, firsts, act, between)
                if not last:
                    split_x(eng, u + 1, 1 - par, first, act)
                    split_w2(eng, u + 1, 1 - par, first, act)

            body(0, 0, True, True)
            body(1, 1, False, True)
            store(eng, 0, 0, True, act)
            body(2, 0, False, False)
            store(eng, 1, 1, True, act)
            with eng.Fori(3, NU - 2, 2) as i:
                for j in range(2):
                    par = (1 + j) % 2
                    body(i + j, par, False, False)
                    store(eng, i + (j - 1), 1 - par, False, act)
            for u in range(NU - 1 - (NU - 4) % 2, NU):
                body(u, u % 2, False, False, u == NU - 1)
                store(eng, u - 1, (u - 1) % 2, False, act)
            store(eng, NU - 1, (NU - 1) % 2, False, act)

        @block.scalar
        def _(act):
            schedule(act, True)
            for par in range(2):
                act.wait_ge(y_out[par], 16 * ((NU + 1 - par) // 2))

        @block.vector
        def _(dve):
            v = nc.vector
            link = Link(dve, chain)
            hot = routes["hot"]
            link(v.tensor_tensor(both[:], hot[:, 0], hot[:, 1], ALU.add))
            dve.wait_ge(tables, 6)
            dve.wait_ge(sums_full, 1)
            rank = dn[0:TP, 0, 0, 0:NT * E].rearrange("p (t e) -> p t e", e=E)
            link(v.tensor_copy(tot[:], dn[0:TP, 0, 1, 0:NT * E].rearrange("p (t e) -> p t e", e=E)))
            src, step, z = tot[:], 1, 0
            while step < NT:
                link(v.tensor_copy(cum[:, z, 0:step, :], src[:, 0:step, :]))
                link(v.tensor_tensor(cum[:, z, step:NT, :], src[:, step:NT, :], src[:, 0:NT - step, :], ALU.add))
                src, step, z = cum[:, z], step * 2, 1 - z
            link(v.tensor_tensor(over[:], src[:, NT - 1, :].unsqueeze(2).broadcast_to((TP, E, MAXC)),
                                 thr[:].unsqueeze(1).broadcast_to((TP, E, MAXC)), ALU.is_gt))
            link(v.tensor_reduce(units[:], over[:], AX.X, ALU.add))
            usrc, step, uz = units[:], 1, 0
            while step < E:
                link(v.tensor_copy(uinc[:, uz, 0:step], usrc[:, 0:step]))
                link(v.tensor_tensor(uinc[:, uz, step:E], usrc[:, step:E], usrc[:, 0:E - step], ALU.add))
                usrc, step, uz = uinc[:, uz], step * 2, 1 - uz
            link(v.tensor_tensor(uge[:], usrc.unsqueeze(1).broadcast_to((TP, NU, E)),
                                 uiota[:].unsqueeze(2).broadcast_to((TP, NU, E)), ALU.is_le))
            link(v.tensor_reduce(uexp[:], uge[:], AX.X, ALU.add))
            link(v.tensor_scalar(uexp[:], uexp[:], float(E - 1), None, ALU.min))
            v.tensor_copy(uexp_i[:], uexp[:]).then_inc(table_done, 1)
            link(v.tensor_tensor(units[:], usrc, units[:], ALU.subtract))
            link(v.tensor_scalar(units[:], units[:], float(UNIT), None, ALU.mult))
            link(v.tensor_tensor(slotmap[:], src, tot[:], ALU.subtract))
            link(v.tensor_tensor(slotmap[:], slotmap[:], rank, ALU.add))
            link(v.tensor_tensor(slotmap[:], slotmap[:], units[:].unsqueeze(1).broadcast_to((TP, NT, E)), ALU.add))
            for r in range(2):
                link(v.tensor_tensor(both[:], hot[:, r], slotmap[:], ALU.mult))
                link(v.tensor_reduce(slot_f[:], both[:], AX.X, ALU.add))
                v.tensor_copy(routes["slot"][:, r, :], slot_f[:]).then_inc(slots_done, 1)
                dve.wait_ge(slots_done, r + 1)
            dve.sem_inc(h_done, 2)
            dve.sem_inc(hlo_done, 2)
            schedule(dve, False)


def combine_phase(nc, base_d, y_d, routes, dst):
    R = 4
    with Semaphores(nc) as sems, ExitStack() as ctx:
        base = ctx.enter_context(nc.sbuf_tensor("cb_base", [TP, R, D], F32))
        ys = ctx.enter_context(nc.sbuf_tensor("cb_y", [TP, R, 2, D], F32))
        base_in = [sems.new(f"cb_base_in{i}") for i in range(R)]
        y_in = [sems.new(f"cb_y_in{i}") for i in range(R)]
        stored = [sems.new(f"cb_stored{i}") for i in range(R)]
        added = sems.new("cb_added")
        block = ctx.enter_context(nc.Block())

        @block.sync
        def _(sp):
            for i in range(NT):
                if i >= R:
                    sp.wait_ge(stored[i % R], 16 * (i // R))
                sp.dma_start(base[:, i % R, :], base_d[i * TP:(i + 1) * TP, :]).then_inc(base_in[i % R], 16)

        @block.gpsimd
        def _(pool):
            for i in range(NT):
                if i >= R:
                    pool.wait_ge(added, 2 * (i - R + 1))
                for r in range(2):
                    pool.indirect_dma_start(ys[:, i % R, r, :], None, y_d,
                                            bass.IndirectOffsetOnAxis(ap=routes["slot"][:, r, i:i + 1], axis=0))\
                        .then_inc(y_in[i % R], 16)

        @block.vector
        def _(dve):
            for i in range(NT):
                dve.wait_ge(base_in[i % R], 16 * (i // R + 1))
                dve.wait_ge(y_in[i % R], 32 * (i // R + 1))
                for r in range(2):
                    nc.vector.scalar_tensor_tensor(out=base[:, i % R, :], in0=ys[:, i % R, r, :],
                                                   scalar=routes["weight"][:, r, i:i + 1], in1=base[:, i % R, :],
                                                   op0=ALU.mult, op1=ALU.add).then_inc(added, 1)
                    if r == 0:
                        dve.wait_ge(added, 2 * i + 1)

        @block.scalar
        def _(act):
            for i in range(NT):
                act.wait_ge(added, 2 * (i + 1))
                act.dma_start(dst[i * TP:(i + 1) * TP, :], base[:, i % R, :]).then_inc(stored[i % R], 16)
            for r in range(R):
                act.wait_ge(stored[r], 16 * (NT // R))


def build(nc, x, ln_pre_g, ln_pre_b, tok_router, tok_router_b, tok_w1, tok_w2, ln_post_g, ln_post_b, wq, bq, wk,
          bk, wv, bv, wo, ffn_router, ffn_w1, ffn_w2,
          ffn_sh1, ffn_sh2, ident, upper, out):
    def scratch(name, shape, dt):
        return nc.dram_tensor(name, shape, dt, kind="Internal").ap()

    h1 = scratch("h1", (T, D), F32)
    h2 = scratch("h2", (T, D), F32)
    xT_hi = scratch("xT_hi", (B, P, D // P, BN), F32)
    xT_lo = scratch("xT_lo", (B, P, D // P, BN), F32)
    kv_hi = scratch("kv_hi", (B, P, NKV, HD + 2), F32)
    kv_lo = scratch("kv_lo", (B, P, NKV, HD + 2), F32)
    moe_phase(nc, x, lambda c, half: tok_w1[c][:, half * P:(half + 1) * P], lambda c: tok_w2[c],
              [P] * tok_w1.shape[0], tok_router, tok_router_b, ln_pre_g, ln_pre_b, ln_post_g, ln_post_b, ident, h1,
              "tok")
    kv_phase(nc, h1, wk, wv, bk, bv, ident, xT_hi, xT_lo, kv_hi, kv_lo)
    query_phase(nc, h1, wq, wo, bq, ident, xT_hi, xT_lo, kv_hi, kv_lo, h2)
    base = scratch("base", (T, D), F32)
    xn = scratch("xn", (T, D), F32)
    ids = scratch("ids", (NU * UNIT, 1), I32)
    y = scratch("y", (NU * UNIT, D), F32)
    with ExitStack() as ctx:
        routes = {
            "hot": ctx.enter_context(nc.sbuf_tensor("rt_hot", [TP, 2, NT, E], F32)),
            "weight": ctx.enter_context(nc.sbuf_tensor("rt_weight", [TP, 2, NT], F32)),
            "slot": ctx.enter_context(nc.sbuf_tensor("rt_slot", [TP, 2, NT], I32)),
        }
        HS = ffn_sh2.shape[0]
        moe_phase(nc, h2, lambda c, half: ffn_sh1[half][:, c * P:min(HS, (c + 1) * P)],
                  lambda c: ffn_sh2[c * P:min(HS, (c + 1) * P), :], [min(P, HS - c) for c in range(0, HS, P)],
                  ffn_router, None, None, None, None, None, ident, base, "ffn", routes, xn)
        expert_phase(nc, xn, ffn_w1, ffn_w2, routes, ident, upper, ids, y)
        combine_phase(nc, base, y, routes, out)


def kernel(**inputs):
    import numpy as np
    from concourse import bacc
    from concourse.bass_utils import run_bass_kernel_spmd

    a = {k: np.asarray(v) for k, v in inputs.items()}
    L = "L0_"
    arrays = {
        "x": a["x"].reshape(T, -1),
        "ln_pre_g": a[L + "tok_ln_pre_g"].reshape(-1, P).T,
        "ln_pre_b": a[L + "tok_ln_pre_b"].reshape(-1, P).T,
        "tok_router": a[L + "tok_router_w"].T,
        "tok_router_b": a[L + "tok_router_b"],
        "tok_w1": np.concatenate([a[L + "tok_experts_w12"], a[L + "tok_shared_w12"][None]]).transpose(0, 2, 1),
        "tok_w2": np.concatenate([a[L + "tok_experts_w3"], a[L + "tok_shared_w3"][None]]).transpose(0, 2, 1),
        "ln_post_g": a[L + "tok_ln_post_g"],
        "ln_post_b": a[L + "tok_ln_post_b"],
        "wq": a[L + "attn_Wq"].T,
        "bq": a[L + "attn_bq"].reshape(NH, HD).T,
        "wk": a[L + "attn_Wk"].T,
        "bk": a[L + "attn_bk"],
        "wv": a[L + "attn_Wv"].T,
        "bv": a[L + "attn_bv"],
        "wo": a[L + "attn_Wo"].T,
        "ffn_router": np.concatenate([a[L + "ffn_gate_w"], a[L + "ffn_shgate_w"][None]]).T,
        "ffn_w1": np.concatenate([a[L + "ffn_w_gate"], a[L + "ffn_w_up"]], axis=2),
        "ffn_w2": a[L + "ffn_w_down"],
        "ffn_sh1": np.stack([a[L + "ffn_shw_gate"], a[L + "ffn_shw_up"]]),
        "ffn_sh2": a[L + "ffn_shw_down"],
        "ident": np.eye(P, dtype=np.float32),
        "upper": np.triu(np.ones((P, P), np.float32), 1),
    }
    arrays = {k: np.ascontiguousarray(v) for k, v in arrays.items()}
    nc = bacc.Bacc("TRN2", target_bir_lowering=False, num_devices=1)
    args = [nc.dram_tensor(k, v.shape, mybir.dt.from_np(v.dtype), kind="ExternalInput").ap() for k, v in arrays.items()]
    out = nc.dram_tensor("out", (T, D), F32, kind="ExternalOutput").ap()
    build(nc, *args, out)
    r = run_bass_kernel_spmd(nc, [arrays], core_ids=[0])
    return r.results[0]["out"].reshape(B, T // B, D)
```
